# Optimizing a Trainium2 kernel written in Bass

```python
import numpy as np
import jax
import jax.numpy as jnp

def _softmax(x, axis=-1):
    return jax.nn.softmax(x, axis=axis)

def _gelu(x):
    return jax.nn.gelu(x, approximate=True)

def _silu(x):
    return jax.nn.silu(x)

def _sigmoid(x):
    return jax.nn.sigmoid(x)

def _layernorm(x, axis=-1, eps=1e-05):
    m = jnp.mean(x, axis=axis, keepdims=True)
    v = jnp.var(x, axis=axis, keepdims=True)
    return (x - m) / jnp.sqrt(v + eps)

def _scatter_add(tgt, idx, src, axis=0):
    return tgt.at[idx].add(src)

def _segment_sum(src, seg, n):
    return jax.ops.segment_sum(src, seg, n)
kernel_name = 'mk_gnn_preln_d2_gnn_r32_d071cf'

def setup_inputs(seed: int=0):
    np.random.seed(seed)
    _w = jnp.asarray

    def _rec_inputs():
        import jax
        import jax.numpy as jnp
        _gk = jax.random.key(seed)
        x = -0.000202 + 1 * jax.random.normal(jax.random.fold_in(_gk, 1), (3125, 128), jnp.float32)
        _s = jax.random.randint(jax.random.fold_in(_gk, 2), (25000,), 0, 3125, jnp.int32)
        _d = jax.random.randint(jax.random.fold_in(_gk, 3), (25000,), 0, 3125, jnp.int32)
        _loop = jnp.arange(3125, dtype=jnp.int32)
        src = jnp.concatenate([_s, _d, _loop])
        dst = jnp.concatenate([_d, _s, _loop])
        _o = jnp.argsort(dst, stable=True)
        src = src[_o]
        dst = dst[_o]
        edge_weight = jax.random.uniform(jax.random.fold_in(_gk, 12), (53125,), jnp.float32, 0.0, 0.999998)
        return (x, src, dst, edge_weight)
    x, src, dst, edge_weight = _rec_inputs()

    def _L0_gnn_setup():
        import jax, jax.numpy as jnp
        import numpy as np
        N_NODES = 50000
        N_EDGES = 25000
        IN_DIM = 128
        OUT_DIM = 128
        NEG_INIT = -1000000000.0
        LEAKY_SLOPE = 0.01
        key = jax.random.key(seed)
        ks = jax.random.split(key, 8)
        x = jax.random.normal(ks[0], (N_NODES, IN_DIM), dtype=jnp.float32)
        edge_index = jax.random.randint(ks[1], (2, N_EDGES), 0, N_NODES, dtype=jnp.int64)
        edge_weight = jax.random.uniform(ks[2], (N_EDGES,), dtype=jnp.float32)
        s1 = 1.0 / np.sqrt(IN_DIM)
        s2 = 1.0 / np.sqrt(OUT_DIM)
        w1 = jax.random.uniform(ks[3], (OUT_DIM, IN_DIM), minval=-s1, maxval=s1, dtype=jnp.float32)
        b1 = jax.random.uniform(ks[4], (OUT_DIM,), minval=-s1, maxval=s1, dtype=jnp.float32)
        w2 = jax.random.uniform(ks[5], (OUT_DIM, OUT_DIM), minval=-s2, maxval=s2, dtype=jnp.float32)
        b2 = jax.random.uniform(ks[6], (OUT_DIM,), minval=-s2, maxval=s2, dtype=jnp.float32)
        eps = jnp.zeros((1,), dtype=jnp.float32)
        return {'x': x, 'edge_index': edge_index, 'edge_weight': edge_weight, 'w1': w1, 'b1': b1, 'w2': w2, 'b2': b2, 'eps': eps}
    _L0_gnn_all = _L0_gnn_setup()
    _L0_gnn_in = {k: v for k, v in _L0_gnn_all.items() if k in ('w1', 'b1', 'w2', 'b2', 'eps')}
    del _L0_gnn_all

    def _L1_gnn_setup():
        import jax, jax.numpy as jnp
        import numpy as np
        NUM_LAYERS = 4
        HIDDEN = 128
        N_NODES = 50000
        N_EDGES = 25000

        def _gru_cell(inp, h, w_ih, w_hh, b_ih, b_hh):
            gi = inp @ w_ih.T + b_ih
            gh = h @ w_hh.T + b_hh
            i_r, i_z, i_n = jnp.split(gi, 3, axis=-1)
            h_r, h_z, h_n = jnp.split(gh, 3, axis=-1)
            r = jax.nn.sigmoid(i_r + h_r)
            z = jax.nn.sigmoid(i_z + h_z)
            n = jnp.tanh(i_n + r * h_n)
            return (1.0 - z) * n + z * h
        key = jax.random.key(seed)
        ks = jax.random.split(key, 8)
        s = 1.0 / np.sqrt(HIDDEN)
        node_embed = jax.random.normal(ks[0], (N_NODES, HIDDEN), dtype=jnp.float32)
        edge_index = jax.random.randint(ks[1], (2, N_EDGES), 0, N_NODES, dtype=jnp.int64)
        weight = jax.random.normal(ks[2], (NUM_LAYERS, HIDDEN, HIDDEN), dtype=jnp.float32) * s
        w_ih = jax.random.normal(ks[3], (3 * HIDDEN, HIDDEN), dtype=jnp.float32) * s
        w_hh = jax.random.normal(ks[4], (3 * HIDDEN, HIDDEN), dtype=jnp.float32) * s
        b_ih = jax.random.normal(ks[5], (3 * HIDDEN,), dtype=jnp.float32) * s
        b_hh = jax.random.normal(ks[6], (3 * HIDDEN,), dtype=jnp.float32) * s
        return {'node_embed': node_embed, 'edge_index': edge_index, 'weight': weight, 'w_ih': w_ih, 'w_hh': w_hh, 'b_ih': b_ih, 'b_hh': b_hh}
    _L1_gnn_all = _L1_gnn_setup()
    _L1_gnn_in = {k: v for k, v in _L1_gnn_all.items() if k in ('weight', 'w_ih', 'w_hh', 'b_ih', 'b_hh')}
    del _L1_gnn_all
    return {'x': x, 'src': src, 'dst': dst, 'edge_weight': edge_weight, 'L0_gnn_w1': _L0_gnn_in['w1'], 'L0_gnn_b1': _L0_gnn_in['b1'], 'L0_gnn_w2': _L0_gnn_in['w2'], 'L0_gnn_b2': _L0_gnn_in['b2'], 'L0_gnn_eps': _L0_gnn_in['eps'], 'L1_gnn_weight': _L1_gnn_in['weight'], 'L1_gnn_w_ih': _L1_gnn_in['w_ih'], 'L1_gnn_w_hh': _L1_gnn_in['w_hh'], 'L1_gnn_b_ih': _L1_gnn_in['b_ih'], 'L1_gnn_b_hh': _L1_gnn_in['b_hh']}

def reference(x, src, dst, edge_weight, L0_gnn_w1, L0_gnn_b1, L0_gnn_w2, L0_gnn_b2, L0_gnn_eps, L1_gnn_weight, L1_gnn_w_ih, L1_gnn_w_hh, L1_gnn_b_ih, L1_gnn_b_hh):
    import jax
    import jax.numpy as jnp

    def _L0_gnn_ref(x, edge_index, edge_weight, w1, b1, w2, b2, eps):
        import jax, jax.numpy as jnp
        import numpy as np
        N_NODES = 50000
        N_EDGES = 25000
        IN_DIM = 128
        OUT_DIM = 128
        NEG_INIT = -1000000000.0
        LEAKY_SLOPE = 0.01
        src = edge_index[0]
        dst = edge_index[1]
        messages = x[src] * edge_weight[:, None]
        agg = jnp.full(x.shape, NEG_INIT, dtype=x.dtype).at[dst].max(messages)
        agg = jnp.where(agg == NEG_INIT, jnp.zeros_like(agg), agg)
        h = (1.0 + eps) * x + agg
        h = h @ w1.T + b1
        h = jnp.where(h >= 0, h, LEAKY_SLOPE * h)
        out = h @ w2.T + b2
        return out

    def _L1_gnn_ref(node_embed, edge_index, weight, w_ih, w_hh, b_ih, b_hh):
        import jax, jax.numpy as jnp
        import numpy as np
        NUM_LAYERS = 4
        HIDDEN = 128
        N_NODES = 50000
        N_EDGES = 25000

        def _gru_cell(inp, h, w_ih, w_hh, b_ih, b_hh):
            gi = inp @ w_ih.T + b_ih
            gh = h @ w_hh.T + b_hh
            i_r, i_z, i_n = jnp.split(gi, 3, axis=-1)
            h_r, h_z, h_n = jnp.split(gh, 3, axis=-1)
            r = jax.nn.sigmoid(i_r + h_r)
            z = jax.nn.sigmoid(i_z + h_z)
            n = jnp.tanh(i_n + r * h_n)
            return (1.0 - z) * n + z * h
        src = edge_index[0]
        dst = edge_index[1]
        n_nodes = node_embed.shape[0]
        x = node_embed
        for l in range(NUM_LAYERS):
            m = x @ weight[l]
            agg = jax.ops.segment_sum(m[src], dst, num_segments=n_nodes)
            x = _gru_cell(agg, x, w_ih, w_hh, b_ih, b_hh)
        return x + node_embed
    edge_index = jnp.stack([src, dst])
    h = jnp.maximum(_layernorm(x, axis=-1), 0.0)
    x = x + _L0_gnn_ref(h, edge_index, edge_weight, L0_gnn_w1, L0_gnn_b1, L0_gnn_w2, L0_gnn_b2, L0_gnn_eps)
    h = jnp.maximum(_layernorm(x, axis=-1), 0.0)
    x = x + _L1_gnn_ref(h, edge_index, L1_gnn_weight, L1_gnn_w_ih, L1_gnn_w_hh, L1_gnn_b_ih, L1_gnn_b_hh)
    return x

_drawn_inputs = setup_inputs


def setup_inputs(seed=0):
    import zlib

    import numpy as np

    out = dict(_drawn_inputs(seed))
    spreads = {}
    factors = {}
    for name, (base, spread) in spreads.items():
        noise = np.random.default_rng([zlib.crc32(name.encode()), seed]).standard_normal(out[name].shape)
        drawn = base * np.exp(spread * noise) if base else spread * noise
        out[name] = jnp.asarray(drawn.astype(out[name].dtype))
    for name, factor in factors.items():
        out[name] = (out[name] * factor).astype(out[name].dtype)
    return out
```

```python
from contextlib import ExitStack

import concourse.bass as bass
from concourse import mybir

P = 128
ALU = mybir.AluOpType
ACT = mybir.ActivationFunctionType
F32 = mybir.dt.float32
BF16 = mybir.dt.bfloat16
FP16 = mybir.dt.float16
I32 = mybir.dt.int32

NEG_INIT = -1.0e9
LEAKY = 0.01
LN_EPS = 1.0e-5
FAR = 8192.0
PAD_DST = 4095
RESET = -(2.0 ** 120)
WIN = 20
DEPTH = 4


class Plan:

    def __init__(self, nodes, feat, edges, layers):
        self.N, self.E, self.L = nodes, edges, layers
        assert feat == P
        self.tiles = -(-nodes // P)
        self.last = nodes - P * (self.tiles - 1)
        self.chunks = -(-edges // 512)
        self.chunks += -self.chunks % DEPTH
        assert self.chunks <= P and nodes <= PAD_DST
        self.run = 4 * self.chunks
        self.slots = P * self.run
        self.cols = P * self.tiles
        self.acols = nodes + WIN - 1
        self.groups = -(-self.tiles // 4)
        self.steps = 7
        self.width = self.cols // self.steps // 64 * 64
        while self.width * self.steps < nodes:
            self.width += 64
        assert self.width <= 512 and self.width * self.steps <= self.acols


def gnn_kernel(nc, x, src, dst, edge_weight, w1, b1, w2, b2, eps, weight, w_ih, w_hh, b_ih, b_hh, out):
    N, F = x.shape
    pl = Plan(N, F, src.shape[0], weight.shape[0])
    h1_dram = nc.dram_tensor("h1_rows", (N, P), F32, kind="Internal").ap()
    x1_dram = nc.dram_tensor("x1_rows", (N, P), F32, kind="Internal").ap()
    h2_dram = nc.dram_tensor("h2_rows", (N, P), F32, kind="Internal").ap()
    run_dram = nc.dram_tensor("run_rows", (pl.slots + 1, P), F32, kind="Internal").ap()

    with ExitStack() as ctx:
        def sb(name, shape, dt, stack=ctx):
            return stack.enter_context(nc.sbuf_tensor(name, shape, dt))

        counts = sb("counts", [P, pl.tiles, pl.acols], BF16)
        w = dict(
            ident=sb("ident", [P, P], F32),
            w1T=sb("w1T", [P, P], F32),
            w2T=sb("w2T", [P, P], F32),
            wihT=sb("wihT", [P, 3, P], F32),
            whhT=sb("whhT", [P, 3, P], F32),
            b1c=sb("b1c", [P, 1], F32),
            bihc=sb("bihc", [P, 3], F32),
            bhhc=sb("bhhc", [P, 3], F32),
            bsum=sb("bsum", [P, 2], F32),
            b2row=sb("b2row", [1, P], F32),
            ones_row=sb("ones_row", [1, P], F32),
            eps1=sb("eps1", [P, 1], F32),
            row_of=sb("row_of", [P, pl.tiles], I32),
            odd=sb("odd", [1, 1], I32),
        )
        edges(nc, pl, w, counts, x, src, dst, edge_weight, w1, b1, w2, b2, eps, weight, w_ih, w_hh, b_ih, b_hh,
              h1_dram, run_dram)
        xT = sb("xT", [P, pl.cols], F32)
        mlp(nc, pl, w, xT, x, h1_dram, run_dram, x1_dram, h2_dram)
        layers(nc, pl, w, counts, xT, weight, x1_dram, h2_dram, out)
        odd = nc.values_load(w["odd"][0:1, 0:1], min_val=0, max_val=1,
                             skip_runtime_bounds_check_because="it is clamped to one when it is made")
        with nc.If(odd > 0):
            one_by_one = (src, dst, edge_weight)
            general_maxima(nc, pl, w, counts, one_by_one, h1_dram, run_dram)
            mlp(nc, pl, w, xT, x, h1_dram, run_dram, x1_dram, h2_dram, "general_")
            layers(nc, pl, w, counts, xT, weight, x1_dram, h2_dram, out, "general_", one_by_one)


def edges(nc, pl, w, counts, x, src, dst, edge_weight, w1, b1, w2, b2, eps, weight, w_ih, w_hh, b_ih, b_hh,
          h1_dram, run_dram):
    R, T, last, RUN = pl.chunks, pl.tiles, pl.last, pl.run
    TW = T * WIN
    turns = R // DEPTH
    assert turns - 1 >= T
    whole_p = pl.E // RUN
    rest_p = pl.E - whole_p * RUN
    whole_r = pl.E // 512
    rest_r = pl.E - whole_r * 512
    GX = pl.groups

    with ExitStack() as ctx:
        def sb(name, shape, dt):
            return ctx.enter_context(nc.sbuf_tensor(name, shape, dt))

        def sem(name):
            return ctx.enter_context(nc.semaphore(name))

        def ps(name):
            return ctx.enter_context(nc.psum_tensor(name, [P, 512], F32))

        src_walk = sb("src_walk", [P, RUN], I32)
        w_walk = sb("w_walk", [P, RUN], F32)
        dstI_walk = sb("dstI_walk", [P, RUN], I32)
        dst_walk = sb("dst_walk", [P, RUN + 1], F32)
        before = sb("before", [P, 1], I32)
        beforeF = sb("beforeF", [P, 1], F32)
        hot_cnt_m = sb("hot_cnt", [P, 4 * 512], BF16)
        hot_cnt = hot_cnt_m[:, 0:4 * TW].rearrange("p (j n) -> p j n", j=4)
        dst_rows = hot_cnt_m[:, 0:1024].bitcast(I32)
        src_rows = hot_cnt_m[:, 1024:2048].bitcast(I32)
        hot_src_m = sb("hot_src", [P, 4 * P], BF16)
        hot_src = hot_src_m[:, 0:4 * P].rearrange("p (j n) -> p j n", j=4)
        dloc = sb("dloc", [P, 512], F32)
        far = sb("far", [P, 512], F32)
        chain, carry, seam_mask = [far[:, i * P:(i + 1) * P] for i in range(3)]
        baseF = sb("baseF", [P, 2], F32)
        base = sb("base", [1, R, 2], I32)
        terms = sb("terms", [P, turns, 3, 4 * DEPTH], F32)
        now = sb("now", [P, 3, 4 * DEPTH], F32)
        iota_count = sb("iota_count", [P, TW], FP16)
        iota_src = sb("iota_src", [P, P], BF16)
        iota_node = sb("iota_node", [P, P], F32)
        node = sb("node", [P, T], F32)
        tile0 = sb("tile0", [P, T], F32)
        walk0 = sb("walk0", [P, 1], F32)
        shiftm = sb("shiftm", [P, 2 * P], F32)
        lastn = sb("lastn", [P, T], F32)
        prevn = sb("prevn", [P, T], F32)
        ge = sb("ge", [P, P], F32)
        at_part = sb("at_part", [P, P], F32)
        scrap = dstI_walk[:, 0:RUN // 2].bitcast(BF16)
        w_tmp = hot_cnt_m[:, 0:2 * RUN].bitcast(F32)
        cnt1 = sb("cnt1", [P, 1], F32)
        upto = sb("upto", [P, T + 1], F32)
        has = sb("has", [P, T], F32)
        first_n = sb("first_n", [P, 1], F32)
        seam_row = sb("seam_row", [P, 1], I32)
        seam = sb("seam", [P, 2], F32)
        tmp1 = sb("tmp1", [P, 1], F32)
        zero_row = sb("zero_row", [1, P], F32)
        mv = sb("mv", [P, T, 2], F32)
        stats = sb("stats", [P, 2, 6], F32)
        rstd = sb("rstd", [P, T], F32)
        shift = sb("shift", [P, T], F32)
        xs_run = sb("xs_run", [P, max(T, DEPTH * 4), P], F32)
        xs = xs_run
        runs_b = xs_run[:, 0:DEPTH * 4, :].rearrange("p (b j) f -> p b j f", b=DEPTH)
        rows = sb("rows", [P, DEPTH, 4, P], F32)
        idx = sb("idx", [P, DEPTH, 4], I32)
        mark = sb("mark", [P, DEPTH], F32)
        w_now = sb("w_now", [P, 4 * DEPTH], F32)
        scrap2 = terms.rearrange("p i s k -> p (i s k)")[:, 0:512]
        ones_col = sb("ones_col", [P, 1], F32)
        odd4 = sb("odd4", [P, 4], F32)

        wraw = counts[:, 0, 0:512].bitcast(F32)
        graw = counts[:, 1, 0:1536].bitcast(F32)

        cntP = [ps(f"cntP{i}") for i in range(2)]
        nodeP = ps("nodeP")
        qP = [ps(f"qP{i}") for i in range(2)]
        wP = [ps(f"wP{i}") for i in range(3)]

        x_in = [sem(f"x_in{i}") for i in range(GX)]
        e_set = sem("e_set")
        dstw_in = sem("dstw_in")
        rows_in = sem("rows_in")
        srcw_in = sem("srcw_in")
        w_in = sem("w_in")
        small_in = sem("small_in")
        zero_out = sem("zero_out")
        consts = sem("consts")
        st = sem("st")
        rooted = sem("rooted")
        normed = sem("normed")
        h1_out = sem("h1_out")
        prep = sem("prep")
        based = sem("based")
        q_turned = sem("q_turned")
        q_out = sem("q_out")
        w_turned = sem("w_turned")
        w_done = sem("w_done")
        zeroed = sem("zeroed")
        gathered = [sem(f"gathered{i}") for i in range(DEPTH)]
        idx_ready = sem("idx_ready")
        w_ready = sem("w_ready")
        marked = sem("marked")
        scaled = sem("scaled")
        maxed = sem("maxed")
        stored = [sem(f"stored{i}") for i in range(DEPTH)]
        hot_ready = sem("hot_ready")
        cnt_ready = sem("cnt_ready")
        cnt_added = sem("cnt_added")
        part_ready = sem("part_ready")
        node_ready = sem("node_ready")
        node_done = sem("node_done")
        tailsem = sem("tailsem")
        up_ready = sem("up_ready")
        found = sem("found")
        odd_summed = sem("odd_summed")
        ge_done = sem("ge_done")
        cnt1_done = sem("cnt1_done")
        now_ready = sem("now_ready")
        seam_sb = sem("seam_sb")
        shifted = sem("shifted")
        seam_spread = sem("seam_spread")
        last_turned = sem("last_turned")
        carry_ready = sem("carry_ready")
        carry_turned = sem("carry_turned")
        seam_in = sem("seam_in")
        seam_done = sem("seam_done")
        seam_out = sem("seam_out")

        block = ctx.enter_context(nc.Block())

        def x_spans(g):
            a, b = 4 * g, min(4 * g + 4, T)
            k = b - a - (1 if b == T and last < P else 0)
            return ([(P, a, k)] if k else []) + ([(last, T - 1, 1)] if b == T and last < P else [])

        @block.sync
        def _(sp):
            for g in range(GX):
                for n, a, k in x_spans(g):
                    sp.dma_start(xs[0:n, a:a + k, :],
                                 x[P * a:P * a + n * k, :].rearrange("(t p) f -> p t f", p=n)).then_inc(x_in[g], 16)
            sp.dma_start(wraw[:, 0:P], w1).then_inc(w_in, 16)
            sp.dma_start(wraw[:, P:2 * P], w2).then_inc(w_in, 16)
            sp.dma_start(graw[:, 0:3 * P].rearrange("p (g f) -> p g f", g=3),
                         w_ih.rearrange("(g p) f -> p g f", p=P)).then_inc(w_in, 16)
            sp.dma_start(graw[:, 3 * P:6 * P].rearrange("p (g f) -> p g f", g=3),
                         w_hh.rearrange("(g p) f -> p g f", p=P)).then_inc(w_in, 16)
            for g in range(GX):
                sp.wait_ge(normed, min(4 * g + 4, T))
                for n, a, k in x_spans(g):
                    sp.dma_start(h1_dram[P * a:P * a + n * k, :].rearrange("(t p) f -> p t f", p=n),
                                 xs[0:n, a:a + k, :]).then_inc(h1_out, 16)
            sp.dma_start(w["eps1"][:, :], eps.rearrange("(a b) -> a b", a=1).broadcast_to([P, 1])).then_inc(small_in, 16)
            sp.dma_start(w["b1c"][:, :], b1.rearrange("(p a) -> p a", a=1)).then_inc(small_in, 16)
            sp.dma_start(w["b2row"][:, :], b2.rearrange("(a p) -> a p", a=1)).then_inc(small_in, 16)
            for g in range(3):
                sp.dma_start(w["bihc"][:, g:g + 1], b_ih[g * P:(g + 1) * P].rearrange("(p a) -> p a", a=1)
                             ).then_inc(small_in, 16)
                sp.dma_start(w["bhhc"][:, g:g + 1], b_hh[g * P:(g + 1) * P].rearrange("(p a) -> p a", a=1)
                             ).then_inc(small_in, 16)
            sp.wait_ge(tailsem, 1)
            sp.dma_start(run_dram[pl.slots:pl.slots + 1, :], zero_row[:, :]).then_inc(zero_out, 16)

            by_walk = run_dram[0:pl.slots, :].rearrange("(p k) f -> p k f", p=P)

            def step(c, u):
                b = u % DEPTH
                sp.wait_ge(maxed, 4 * c + 4)
                to = by_walk[:, 4 * c:4 * c + 4, :] if isinstance(c, int) else by_walk[:, bass.ds(4 * c, 4), :]
                sp.dma_start(to, runs_b[:, b, :, :]).then_inc(stored[b], 16)
            for c in range(DEPTH):
                step(c, c)
            with sp.Fori(1, turns) as i:
                for u in range(DEPTH):
                    step(DEPTH * i + u, u)
            for b in range(DEPTH):
                sp.wait_ge(stored[b], 16 * turns)
            sp.wait_ge(zero_out, 16)
            sp.wait_ge(small_in, 16 * 9)

        @block.gpsimd
        def _(pool):
            def gpi(tile, step, base, cm, fp=True):
                return nc.gpsimd.iota(tile, pattern=[[step, tile.shape[-1]]], base=base, channel_multiplier=cm,
                                      allow_small_or_imprecise_dtypes=True)
            nc.gpsimd.memset(w["ident"][:, :], 0.0).then_inc(consts, 1)
            nc.gpsimd.memset(shiftm[:, :], 0.0).then_inc(consts, 1)
            pool.wait_ge(consts, 2)
            nc.gpsimd.affine_select(out=w["ident"][:, :], in_=w["ident"][:, :], compare_op=ALU.not_equal, fill=1.0,
                                    base=0, pattern=[[-1, P]], channel_multiplier=1).then_inc(consts, 1)
            nc.gpsimd.affine_select(out=shiftm[:, :], in_=shiftm[:, :], compare_op=ALU.not_equal, fill=1.0,
                                    base=1, pattern=[[-1, 2 * P]], channel_multiplier=1).then_inc(consts, 1)
            gpi(iota_count[:, :], 1, 0, 0).then_inc(consts, 1)
            gpi(iota_src[:, :], 1, 0, 0).then_inc(consts, 1)
            gpi(iota_node[:, :], 1, 0, 0).then_inc(consts, 1)
            gpi(node[:, :], P, 0, 1).then_inc(consts, 1)
            gpi(tile0[:, :], P, 0, 0).then_inc(consts, 1)
            gpi(walk0[:, :], 1, 0, RUN).then_inc(consts, 1)
            nc.gpsimd.memset(counts[:, 2:T // 3, :], 0.0).then_inc(zeroed, 1)

            n_out = sum(len(x_spans(g)) for g in range(GX))
            pool.wait_ge(h1_out, 16 * n_out)

            def step(c, u):
                b = u % DEPTH
                if u >= DEPTH:
                    pool.wait_ge(maxed, 4 * c + 4 - 4 * DEPTH)
                pool.wait_ge(idx_ready, c + 1)
                nc.gpsimd.tensor_tensor(mark[0:1, b:b + 1], w["ident"][0:1, 0:1], w["ident"][0:1, 0:1], ALU.mult
                                        ).then_inc(marked, 1)
                for j in range(4):
                    pool.indirect_dma_start(out=rows[:, b, j, :], out_offset=None, in_=h1_dram,
                                            in_offset=bass.IndirectOffsetOnAxis(ap=idx[:, b, j:j + 1], axis=0)
                                            ).then_inc(gathered[b], 16)
            pool.wait_ge(consts, 10)
            for c in range(DEPTH):
                step(c, c)
            with pool.Fori(1, turns) as i:
                for u in range(DEPTH):
                    step(DEPTH * i + u, u + DEPTH)

            for b in range(DEPTH):
                pool.wait_ge(stored[b], 16 * turns)
            pool.indirect_dma_start(out=rows[:, 0, 0, :], out_offset=None, in_=run_dram,
                                    in_offset=bass.IndirectOffsetOnAxis(ap=seam_row[:, 0:1], axis=0)
                                    ).then_inc(seam_in, 16)
            pool.wait_ge(seam_done, 1)
            pool.indirect_dma_start(out=run_dram, out_offset=bass.IndirectOffsetOnAxis(ap=seam_row[:, 0:1], axis=0),
                                    in_=rows[:, 0, 1, :], in_offset=None).then_inc(seam_out, 16)
            pool.wait_ge(seam_out, 16)

        @block.scalar
        def _(act):
            act.wait_ge(e_set, 2)
            act.dma_start(dstI_walk[0:whole_p, :], dst[0:whole_p * RUN].rearrange("(p k) -> p k", k=RUN)
                          ).then_inc(dstw_in, 16)
            act.dma_start(dstI_walk[whole_p:whole_p + 1, 0:rest_p],
                          dst[whole_p * RUN:pl.E].rearrange("(p k) -> p k", p=1)).then_inc(dstw_in, 16)
            act.dma_start(before[1:P, :], dst[0:(P - 1) * RUN].rearrange("(p k) -> p k", k=RUN)[:, RUN - 1:RUN],
                          allow_slow_non_contiguous=True).then_inc(dstw_in, 16)
            act.wait_ge(e_set, 3)
            act.dma_start(src_walk[0:whole_p, :], src[0:whole_p * RUN].rearrange("(p k) -> p k", k=RUN)
                          ).then_inc(srcw_in, 16)
            act.dma_start(src_walk[whole_p:whole_p + 1, 0:rest_p],
                          src[whole_p * RUN:pl.E].rearrange("(p k) -> p k", p=1)).then_inc(srcw_in, 16)
            act.wait_ge(e_set, 4)
            act.dma_start(w_walk[0:whole_p, :], edge_weight[0:whole_p * RUN].rearrange("(p k) -> p k", k=RUN)
                          ).then_inc(srcw_in, 16)
            act.dma_start(w_walk[whole_p:whole_p + 1, 0:rest_p],
                          edge_weight[whole_p * RUN:pl.E].rearrange("(p k) -> p k", p=1)).then_inc(srcw_in, 16)
            act.wait_ge(e_set, 6)
            for tile, dram in ((dst_rows, dst), (src_rows, src)):
                act.dma_start(tile[0:whole_r, :], dram[0:512 * whole_r].rearrange("(r i) -> r i", i=512)
                              ).then_inc(rows_in, 16)
                act.dma_start(tile[whole_r:whole_r + 1, 0:rest_r], dram[512 * whole_r:pl.E].rearrange("(r i) -> r i", r=1)
                              ).then_inc(rows_in, 16)

            act.wait_ge(st, 2 * T + 3)
            nc.scalar.activation(rstd[:, :], mv[:, :, 1], ACT.Sqrt).then_inc(rooted, 1)
            act.wait_ge(st, 2 * T + 5)
            for t in range(T):
                n = P if t < T - 1 else last
                nc.scalar.activation(xs[0:n, t, :], xs[0:n, t, :], ACT.Relu, bias=shift[0:n, t:t + 1],
                                     scale=rstd[0:n, t:t + 1]).then_inc(normed, 1)
            act.wait_ge(srcw_in, 64)
            for c in range(DEPTH):
                nc.scalar.copy(idx[:, c, :], src_walk[:, 4 * c:4 * c + 4]).then_inc(idx_ready, 1)
            act.wait_ge(w_turned, 3)
            nc.scalar.copy(w["w1T"][:, :], wP[0][:, 0:P]).then_inc(w_done, 1)
            nc.scalar.copy(w["w2T"][:, :], wP[0][:, P:2 * P]).then_inc(w_done, 1)
            nc.scalar.copy(w["wihT"][:, :, :], wP[1][:, 0:3 * P].rearrange("p (g f) -> p g f", g=3)).then_inc(w_done, 1)
            nc.scalar.copy(w["whhT"][:, :, :], wP[2][:, 0:3 * P].rearrange("p (g f) -> p g f", g=3)).then_inc(w_done, 1)

            def weights(i):
                act.wait_ge(scaled, DEPTH * i)
                nc.scalar.copy(w_now[:, :], w_walk[:, 4 * DEPTH * i:4 * DEPTH * (i + 1)] if isinstance(i, int) else
                               w_walk[:, bass.ds(4 * DEPTH * i, 4 * DEPTH)]).then_inc(w_ready, 1)
                act.wait_ge(w_ready, i + 1)

            def step(c, u, more):
                b = u % DEPTH
                act.wait_ge(gathered[b], 16 * (c - b) + 64)
                if more:
                    act.wait_ge(marked, c + 1)
                    k = 4 * (c + DEPTH)
                    nc.scalar.copy(idx[:, b, :], src_walk[:, k:k + 4] if isinstance(c, int) else
                                   src_walk[:, bass.ds(k, 4)]).then_inc(idx_ready, 1)
                for j in range(4):
                    ins = nc.scalar.activation(rows[:, b, j, :], rows[:, b, j, :], ACT.Copy,
                                               scale=w_now[:, 4 * b + j:4 * b + j + 1])
                ins.then_inc(scaled, 1)

            weights(0)
            for c in range(DEPTH):
                step(c, c, True)
            with act.Fori(1, turns - 1) as i:
                weights(i)
                for u in range(DEPTH):
                    step(DEPTH * i + u, u, True)
            weights(turns - 1)
            for u in range(DEPTH):
                step(R - DEPTH + u, u, False)

        @block.tensor
        def _(pe):
            pe.wait_ge(consts, 10)
            pe.wait_ge(prep, 1)
            for j in range(2):
                mm = nc.tensor.matmul(nodeP[0:1, j * R:(j + 1) * R], baseF[0:R, j:j + 1],
                                      w["ident"][0:R, 0:R], start=True, stop=True)
            mm.then_inc(based, 1)
            pe.wait_ge(prep, 9)
            for i, frm in enumerate((far, dloc)):
                for j in range(4):
                    mm = nc.tensor.transpose(qP[i][:, j * R:(j + 1) * R], frm[0:R, j * P:(j + 1) * P],
                                             w["ident"][0:R, 0:R])
                mm.then_inc(q_turned, 1)
            pe.wait_ge(w_in, 16 * 4)
            for i in range(2):
                mm = nc.tensor.transpose(wP[0][:, i * P:(i + 1) * P], wraw[:, i * P:(i + 1) * P], w["ident"][:, :])
            mm.then_inc(w_turned, 1)
            for b in range(2):
                for i in range(3):
                    mm = nc.tensor.transpose(wP[1 + b][:, i * P:(i + 1) * P],
                                             graw[:, (3 * b + i) * P:(3 * b + i + 1) * P], w["ident"][:, :])
                mm.then_inc(w_turned, 1)

            def step(c, u):
                for v in range(2):
                    pe.wait_ge(hot_ready, 2 * c + v + 1)
                    if u >= 1:
                        pe.wait_ge(cnt_added, 2 * c + v - 1)
                    for j in range(2):
                        mm = nc.tensor.matmul(cntP[v][:, 0:TW], hot_src[:, 2 * v + j, :],
                                              hot_cnt[:, 2 * v + j, :], start=(j == 0), stop=(j == 1))
                    mm.then_inc(cnt_ready, 1)

            def nodes_of_tile(t):
                pe.wait_ge(part_ready, t + 1)
                pe.wait_ge(node_done, t)
                nc.tensor.matmul(nodeP[:, 0:RUN + 1], at_part[:, :], dst_walk[:, :], start=True, stop=True
                                 ).then_inc(node_ready, 1)

            for c in range(DEPTH):
                step(c, c)
            with pe.Fori(1, turns) as i:
                for u in range(DEPTH):
                    step(DEPTH * i + u, u + DEPTH)
                    if u == 0:
                        nodes_of_tile(i - 1)

            pe.wait_ge(found, 4)
            nc.tensor.matmul(cntP[0][0:1, 0:4], ones_col[:, 0:1], odd4[:, :], start=True, stop=True).then_inc(odd_summed, 1)
            pe.wait_ge(up_ready, 1)
            nc.tensor.matmul(qP[0][:, 0:T], shiftm[:, 0:P], upto[:, 1:T + 1], start=True, stop=False)
            nc.tensor.matmul(qP[0][:, 0:T], shiftm[:, P:2 * P], upto[:, 0:T], start=False, stop=True
                             ).then_inc(shifted, 1)
            for i in range(2):
                mm = nc.tensor.matmul(qP[1][:, i * P:(i + 1) * P], seam[:, i:i + 1].broadcast_to([P, P]),
                                      w["ident"][:, :], start=True, stop=True)
            mm.then_inc(seam_spread, 1)
            pe.wait_ge(maxed, RUN)
            nc.tensor.transpose(wP[0][:, 0:P], runs_b[:, DEPTH - 1, 3, :], w["ident"][:, :]).then_inc(last_turned, 1)
            pe.wait_ge(carry_ready, 2)
            nc.tensor.transpose(wP[1][:, 0:P], carry[:, :], w["ident"][:, :]).then_inc(carry_turned, 1)

        @block.vector
        def _(dve):
            nc.vector.memset(dstI_walk[:, :], PAD_DST).then_inc(e_set, 1)
            nc.vector.memset(before[:, :], -1).then_inc(e_set, 1)
            nc.vector.memset(src_walk[:, :], 0).then_inc(e_set, 1)
            nc.vector.memset(w_walk[:, :], 0.0).then_inc(e_set, 1)
            nc.vector.memset(dst_rows[:, :], PAD_DST).then_inc(e_set, 1)
            nc.vector.memset(src_rows[:, :], 0).then_inc(e_set, 1)
            nc.vector.memset(zero_row[:, :], 0.0).then_inc(tailsem, 1)
            nc.vector.memset(w["ones_row"][:, :], 1.0).then_inc(tailsem, 1)
            nc.vector.memset(ones_col[:, :], 1.0).then_inc(tailsem, 1)
            nc.vector.memset(upto[:, 0:1], 0.0).then_inc(tailsem, 1)
            nc.vector.memset(mv[:, :, :], 1.0).then_inc(st, 1)
            dve.wait_ge(st, 1)
            done = 1
            for t in range(T):
                n = P if t < T - 1 else last
                if t % 4 == 0:
                    dve.wait_ge(x_in[t // 4], 16 * len(x_spans(t // 4)))
                if t >= 2:
                    dve.wait_ge(st, done - 2)
                nc.vector.bn_stats(stats[0:n, t % 2, :], xs[0:n, t, :]).then_inc(st, 1)
                dve.wait_ge(st, done + 1)
                nc.vector.bn_aggr(mv[0:n, t, :], stats[0:n, t % 2, :]).then_inc(st, 1)
                done += 2
            dve.wait_ge(st, done)
            nc.vector.tensor_scalar(shift[:, :], mv[:, :, 0], -1.0, None, ALU.mult).then_inc(st, 1)
            nc.vector.tensor_scalar(mv[:, :, 1], mv[:, :, 1], LN_EPS, None, ALU.add).then_inc(st, 1)
            dve.wait_ge(rooted, 1)
            nc.vector.reciprocal(rstd[:, :], rstd[:, :]).then_inc(st, 1)
            dve.wait_ge(st, done + 3)
            nc.vector.tensor_tensor(shift[:, :], shift[:, :], rstd[:, :], ALU.mult).then_inc(st, 1)

            k = [0]

            def step_of(s, ins):
                k[0] += 1
                ins.then_inc(s, 1)
                dve.wait_ge(s, k[0])

            dve.wait_ge(rows_in, 64)
            step_of(prep, nc.vector.tensor_copy(baseF[:, :], dst_rows[:, 0:512:256]))
            for j in range(2):
                step_of(prep, nc.vector.tensor_scalar(dloc[:, 256 * j:256 * j + 256], dst_rows[:, 256 * j:256 * j + 256],
                                                      baseF[:, j:j + 1], None, ALU.subtract))
            step_of(prep, nc.vector.tensor_scalar(far[:, :], dloc[:, :], float(WIN), FAR, ALU.is_ge, ALU.mult))
            nc.vector.scalar_tensor_tensor(out=scrap2[:, :], in0=dst_rows[:, :], scalar=float(PAD_DST), in1=far[:, :],
                                           op0=ALU.is_lt, op1=ALU.mult, accum_out=odd4[:, 0:1]).then_inc(found, 1)
            step_of(prep, nc.vector.tensor_tensor(dloc[:, :], dloc[:, :], far[:, :], ALU.add))
            dve.wait_ge(found, 1)
            step_of(prep, nc.vector.tensor_scalar(dst_rows[:, :], src_rows[:, :], P - 1, None, ALU.bitwise_and))
            step_of(prep, nc.vector.tensor_copy(far[:, :], dst_rows[:, :]))
            step_of(prep, nc.vector.tensor_scalar(src_rows[:, :], src_rows[:, :], 7, None, ALU.logical_shift_right))
            step_of(prep, nc.vector.scalar_tensor_tensor(out=dloc[:, :], in0=src_rows[:, :], scalar=float(WIN),
                                                         in1=dloc[:, :], op0=ALU.mult, op1=ALU.add))
            n_rows = k[0]
            dve.wait_ge(dstw_in, 48)
            dve.wait_ge(consts, 10)
            step_of(prep, nc.vector.tensor_copy(dst_walk[:, 0:RUN], dstI_walk[:, :]))
            nc.vector.tensor_copy(dst_walk[:, RUN:RUN + 1], walk0[:, :])
            nc.vector.memset(w_tmp[:, 0:1], 1.0)
            step_of(prep, nc.vector.tensor_tensor(w_tmp[:, 1:RUN], dst_walk[:, 1:RUN], dst_walk[:, 0:RUN - 1],
                                                  ALU.not_equal))
            step_of(prep, nc.vector.tensor_scalar(terms[:, :, 2, :], w_tmp.rearrange("p (i k) -> p i k", i=turns),
                                                  RESET, None, ALU.mult))
            step_of(prep, nc.vector.tensor_copy(beforeF[:, :], before[:, :]))
            nc.vector.tensor_scalar(lastn[:, :], tile0[:, :], -1.0, dst_walk[:, RUN - 1:RUN], ALU.mult, ALU.add)
            nc.vector.tensor_scalar(prevn[:, :], tile0[:, :], -1.0, beforeF[:, 0:1], ALU.mult, ALU.add)
            step_of(prep, nc.vector.tensor_scalar(scrap[:, :], dst_walk[:, 0:RUN], dst_walk[:, 0:1], 0.0, ALU.is_equal,
                                                  ALU.add, accum_out=first_n[:, 0:1]))
            step_of(prep, nc.vector.tensor_tensor(tmp1[:, :], first_n[:, :], walk0[:, :], ALU.add))
            step_of(prep, nc.vector.tensor_scalar(seam_row[:, :], tmp1[:, :], -1.0, None, ALU.add))
            step_of(prep, nc.vector.tensor_tensor(seam[:, 1:2], beforeF[:, :], dst_walk[:, 0:1], ALU.not_equal))
            step_of(prep, nc.vector.tensor_tensor(tmp1[:, :], dst_walk[:, RUN - 1:RUN], dst_walk[:, 0:1], ALU.not_equal))
            step_of(prep, nc.vector.tensor_tensor(tmp1[:, :], tmp1[:, :], seam[:, 1:2], ALU.max))
            step_of(prep, nc.vector.tensor_scalar(seam[:, 0:1], tmp1[:, :], RESET, None, ALU.mult))
            step_of(prep, nc.vector.tensor_scalar(seam[:, 1:2], seam[:, 1:2], RESET, None, ALU.mult))

            dve.wait_ge(based, 1)
            nc.vector.tensor_scalar(base[:, :, :], nodeP[0:1, 0:2 * R].rearrange("p (j c) -> p c j", j=2),
                                    0.0, float(pl.N - 1), ALU.max, ALU.min).then_inc(q_out, 1)
            for i in range(2):
                dve.wait_ge(q_turned, 1 + i)
                nc.vector.tensor_copy(terms[:, :, i, :].rearrange("p i (d j) -> p i d j", j=4),
                                      qP[i][:, 0:4 * R].rearrange("p (j i d) -> p i d j", j=4, d=DEPTH)).then_inc(q_out, 1)
            dve.wait_ge(w_turned, 3)
            nc.vector.memset(counts[:, 0:2, :], 0.0).then_inc(zeroed, 1)
            nc.vector.memset(counts[:, T // 3:T, :], 0.0).then_inc(zeroed, 1)
            dve.wait_ge(small_in, 16 * 9)
            nc.vector.tensor_tensor(w["bsum"][:, :], w["bihc"][:, 0:2], w["bhhc"][:, 0:2], ALU.add).then_inc(tailsem, 1)
            nc.vector.tensor_scalar(w["eps1"][:, :], w["eps1"][:, :], 1.0, None, ALU.add).then_inc(tailsem, 1)
            dve.wait_ge(q_out, 3)
            dve.wait_ge(zeroed, 3)

            def bases(i):
                row = base[0:1, DEPTH * i:DEPTH * i + DEPTH, :] if isinstance(i, int) else \
                    base[0:1, bass.ds(DEPTH * i, DEPTH), :]
                _, vals = nc.values_load_multi_w_load_instructions(
                    row.rearrange("p c v -> p (c v)"), engines=[mybir.EngineType.DVE], min_val=0, max_val=pl.N - 1,
                    skip_runtime_bounds_check_because="the bases are clamped to the nodes when they are made")
                return vals

            def part_of_tile(t):
                dve.wait_ge(node_ready, t)
                pc, lc = [q[:, bass.ds(t, 1)] for q in (prevn, lastn)]
                nc.vector.tensor_scalar(ge[:, :], iota_node[:, :], pc, None, ALU.is_ge).then_inc(ge_done, 1)
                dve.wait_ge(ge_done, t + 1)
                nc.vector.scalar_tensor_tensor(out=at_part[:, :], in0=iota_node[:, :], scalar=lc, in1=ge[:, :],
                                               op0=ALU.is_lt, op1=ALU.mult).then_inc(part_ready, 1)

            def count_of_tile(t):
                dve.wait_ge(node_ready, t + 1)
                nc.vector.tensor_scalar(scrap[:, :], nodeP[:, 0:RUN], node[:, bass.ds(t, 1)], 0.0, ALU.is_le, ALU.add,
                                        accum_out=cnt1[:, 0:1]).then_inc(cnt1_done, 1)
                dve.wait_ge(cnt1_done, t + 1)
                nc.vector.tensor_tensor(upto[:, bass.ds(t + 1, 1)], nodeP[:, RUN:RUN + 1], cnt1[:, 0:1], ALU.add
                                        ).then_inc(node_done, 1)

            def turn(i, first):
                src_i = terms[:, i, :, :] if isinstance(i, int) else \
                    terms[:, bass.ds(i, 1), :, :].rearrange("p a s k -> p (a s) k")
                dve.wait_ge(maxed, 4 * DEPTH * i)
                dve.wait_ge(hot_ready, 2 * DEPTH * i)
                nc.vector.tensor_copy(now[:, :, :], src_i).then_inc(now_ready, 1)
                at = bases(i)
                dve.wait_ge(now_ready, i + 1)
                for u in range(DEPTH):
                    c = DEPTH * i + u

                    def hot(j):
                        k = 4 * u + j
                        nc.vector.tensor_scalar(hot_src[:, j, :], iota_src[:, :], now[:, 0, k:k + 1], None,
                                                ALU.is_equal)
                        ins = nc.vector.tensor_scalar(hot_cnt[:, j, :], iota_count[:, :], now[:, 1, k:k + 1], None,
                                                      ALU.is_equal)
                        if j % 2:
                            ins.then_inc(hot_ready, 1)

                    def maximum(j):
                        if first and u == 0 and j == 0:
                            nc.vector.tensor_copy(runs_b[:, 0, 0, :], rows[:, 0, 0, :]).then_inc(maxed, 1)
                            return
                        pu, pj = (u, j - 1) if j else ((u - 1) % DEPTH, 3)
                        dve.wait_ge(maxed, 4 * c + j)
                        nc.vector.scalar_tensor_tensor(out=runs_b[:, u, j, :], in0=runs_b[:, pu, pj, :],
                                                       scalar=now[:, 2, 4 * u + j:4 * u + j + 1],
                                                       in1=rows[:, u, j, :], op0=ALU.add, op1=ALU.max
                                                       ).then_inc(maxed, 1)

                    def add_counts(v):
                        dve.wait_ge(cnt_ready, 2 * c + v + 1)
                        dve.wait_ge(cnt_added, 2 * c + v)
                        win = counts[:, :, bass.ds(at[2 * u + v], WIN)]
                        nc.vector.tensor_tensor(win, cntP[v][:, 0:TW].rearrange("p (t d) -> p t d", d=WIN), win,
                                                ALU.add).then_inc(cnt_added, 1)

                    hot(0)
                    hot(1)
                    dve.wait_ge(scaled, c + 1)
                    if first:
                        dve.wait_ge(h1_out, 16 * sum(len(x_spans(g)) for g in range(GX)))
                    else:
                        dve.wait_ge(stored[u], 16 * i)
                    maximum(0)
                    hot(2)
                    maximum(1)
                    hot(3)
                    maximum(2)
                    add_counts(0)
                    maximum(3)
                    add_counts(1)
                    if not first and u == 0:
                        part_of_tile(i - 1)
                    if not first and u == 1:
                        count_of_tile(i - 1)

            turn(0, True)
            with dve.Fori(1, turns) as i:
                turn(i, False)
            assert pl.slots - pl.E <= P
            nc.vector.scalar_tensor_tensor(out=scrap[:, 1:RUN], in0=dst_walk[:, 0:RUN - 1], scalar=0.0,
                                           in1=dst_walk[:, 1:RUN], op0=ALU.add, op1=ALU.is_gt,
                                           accum_out=odd4[:, 1:2]).then_inc(found, 1)
            dve.wait_ge(found, 2)
            nc.vector.scalar_tensor_tensor(out=scrap[:, P:RUN], in0=dst_walk[:, 0:RUN - P], scalar=0.0,
                                           in1=dst_walk[:, P:RUN], op0=ALU.add, op1=ALU.is_equal,
                                           accum_out=odd4[:, 2:3]).then_inc(found, 1)
            nc.vector.tensor_tensor(odd4[:, 3:4], beforeF[:, :], dst_walk[:, 0:1], ALU.is_gt).then_inc(found, 1)
            dve.wait_ge(node_done, turns - 1)
            nc.vector.tensor_scalar(upto[:, 0:1], upto[:, 0:1], 0.0, None, ALU.mult).then_inc(up_ready, 1)

            dve.wait_ge(seam_spread, 1)
            nc.vector.tensor_copy(seam_mask[:, :], qP[1][:, 0:P]).then_inc(seam_sb, 1)
            dve.wait_ge(last_turned, 1)
            dve.wait_ge(seam_sb, 1)
            nc.vector.tensor_tensor_scan(chain[:, :], seam_mask[:, :], wP[0][:, 0:P], 0.0, ALU.add, ALU.max
                                         ).then_inc(seam_sb, 1)
            dve.wait_ge(seam_sb, 2)
            nc.vector.memset(carry[:, 0:1], RESET).then_inc(carry_ready, 1)
            nc.vector.tensor_tensor(carry[:, 1:P], chain[:, 0:P - 1], qP[1][:, P + 1:2 * P], ALU.add
                                    ).then_inc(carry_ready, 1)
            dve.wait_ge(shifted, 1)
            nc.vector.tensor_tensor(has[:, :], upto[:, 1:T + 1], qP[0][:, 0:T], ALU.is_gt).then_inc(seam_sb, 1)
            dve.wait_ge(seam_sb, 3)
            nc.vector.scalar_tensor_tensor(out=has[:, :], in0=upto[:, 1:T + 1], scalar=float(-1 - pl.slots),
                                           in1=has[:, :], op0=ALU.add, op1=ALU.mult).then_inc(seam_sb, 1)
            dve.wait_ge(seam_sb, 4)
            nc.vector.tensor_scalar(w["row_of"][:, :], has[:, :], float(pl.slots), None, ALU.add).then_inc(seam_sb, 1)
            dve.wait_ge(odd_summed, 1)
            dve.wait_ge(now_ready, turns)
            nc.vector.tensor_reduce(odd4[0:1, 0:1], cntP[0][0:1, 0:4], mybir.AxisListType.X, ALU.add).then_inc(found, 1)
            dve.wait_ge(found, 5)
            nc.vector.tensor_scalar(w["odd"][:, :], odd4[0:1, 0:1], 1.0, None, ALU.min).then_inc(found, 1)
            dve.wait_ge(seam_in, 16)
            dve.wait_ge(carry_turned, 1)
            nc.vector.tensor_tensor(rows[:, 0, 1, :], wP[1][:, 0:P], rows[:, 0, 0, :], ALU.max).then_inc(seam_done, 1)


def mlp(nc, pl, w, xT, x, h1_dram, run_dram, x1_dram, h2_dram, tag=""):
    T, last = pl.tiles, pl.last
    G = pl.groups
    with ExitStack() as ctx:
        def sb(name, shape, dt):
            return ctx.enter_context(nc.sbuf_tensor(tag + name, shape, dt))

        def sem(name):
            return ctx.enter_context(nc.semaphore(tag + name))

        def ps(name):
            return ctx.enter_context(nc.psum_tensor(tag + name, [P, 512], F32))

        h1 = sb("h1", [P, 2, 4, P], F32)
        agg = sb("agg_rows", [P, 3, 4, P], F32)
        xr = sb("xr", [P, 3, 4, P], F32)
        u_in = sb("u_in", [P, 2, 512], F32)
        v_b = sb("v_b", [P, 512], F32)
        act1 = sb("act1", [P, 2, 512], F32)
        h2 = sb("h2", [P, 3, 4, P], F32)
        stats = sb("stats2", [P, 4, 6], F32)
        mv = sb("mv2", [P, 4, 2], F32)
        rstd = sb("rstd2", [P, 4], F32)
        shift = sb("shift2", [P, 4], F32)
        hP = [ps(f"hP{i}") for i in range(2)]
        vP = [ps(f"vP{i}") for i in range(2)]
        oP = [ps(f"oP{i}") for i in range(2)]
        tP = [ps(f"tP{i}") for i in range(2)]

        h_in = [sem(f"h_in{i}") for i in range(2)]
        xr_in = [sem(f"xr_in{i}") for i in range(3)]
        agg_in = [sem(f"agg_in{i}") for i in range(3)]
        u_rows = sem("u_rows")
        h_turned = sem("h_turned")
        aggfix = sem("aggfix")
        u_ready = sem("u_ready")
        v_ready = sem("v_ready")
        vb_ready = sem("vb_ready")
        leaky = sem("leaky")
        o_ready = sem("o_ready")
        x1_ready = sem("x1_ready")
        ln = sem("ln")
        root = sem("root")
        h2_ready = sem("h2_ready")
        rows_out = [sem(f"rows_out{i}") for i in range(3)]
        h2_turned = sem("h2_turned")
        xT_ready = sem("xT_ready")

        def tiles(g):
            return [(t, P if t < T - 1 else last) for t in range(4 * g, min(4 * g + 4, T))]

        def cols(g):
            a = 512 * g
            return a, min(512, pl.N - a)

        def move(eng, sb_tile, dram, g, to_dram, s):
            ts = tiles(g)
            fullt = [t for t, n in ts if n == P]
            n_dma = 0
            if fullt:
                a = fullt[0]
                k = len(fullt)
                d = dram[P * a:P * (a + k), :].rearrange("(t p) f -> p t f", p=P)
                s_ = sb_tile[:, 0:k, :]
                (eng.dma_start(d, s_) if to_dram else eng.dma_start(s_, d)).then_inc(s, 16)
                n_dma += 1
            if len(fullt) < len(ts):
                t, n = ts[-1]
                d = dram[P * t:P * t + n, :]
                s_ = sb_tile[0:n, t - 4 * g, :]
                (eng.dma_start(d, s_) if to_dram else eng.dma_start(s_, d)).then_inc(s, 16)
                n_dma += 1
            return n_dma

        def n_dmas(g):
            ns = [n for _, n in tiles(g)]
            return int(P in ns) + int(any(n < P for n in ns))

        def total(g, ring):
            return 16 * sum(n_dmas(k) for k in range(g % ring, g + 1, ring))

        block = ctx.enter_context(nc.Block())

        @block.sync
        def _(sp):
            def load(g):
                if g >= 2:
                    sp.wait_ge(u_rows, g - 1)
                move(sp, h1[:, g % 2, :, :], h1_dram, g, False, h_in[g % 2])
                if g >= 3:
                    sp.wait_ge(rows_out[g % 3], 2 * total(g - 3, 3))
                move(sp, xr[:, g % 3, :, :], x, g, False, xr_in[g % 3])
            load(0)
            load(1)
            for g in range(G):
                if g + 2 < G:
                    load(g + 2)
                sp.wait_ge(x1_ready, g + 1)
                move(sp, xr[:, g % 3, :, :], x1_dram, g, True, rows_out[g % 3])
                sp.wait_ge(h2_ready, g + 1)
                move(sp, h2[:, g % 3, :, :], h2_dram, g, True, rows_out[g % 3])
            for g in range(G - 3, G):
                sp.wait_ge(rows_out[g % 3], 2 * total(g, 3))

        @block.gpsimd
        def _(pool):
            for g in range(G):
                if g >= 3:
                    pool.wait_ge(h_turned, g - 2)
                for t, _ in tiles(g):
                    pool.indirect_dma_start(out=agg[:, g % 3, t - 4 * g, :], out_offset=None, in_=run_dram,
                                            in_offset=bass.IndirectOffsetOnAxis(ap=w["row_of"][:, t:t + 1], axis=0)
                                            ).then_inc(agg_in[g % 3], 16)

        def s1_pe(pe, g):
            pe.wait_ge(u_rows, g + 1)
            if g >= 2:
                pe.wait_ge(u_ready, g - 1)
            for t, n in tiles(g):
                j = t - 4 * g
                mm = nc.tensor.transpose(hP[g % 2][:, j * P:j * P + n], agg[0:n, g % 3, j, :], w["ident"][0:n, 0:n])
            mm.then_inc(h_turned, 1)

        def s2_pe(pe, g):
            a, n = cols(g)
            pe.wait_ge(u_ready, g + 1)
            if g >= 2:
                pe.wait_ge(vb_ready, g - 1)
            nc.tensor.matmul(vP[g % 2][:, 0:n], w["w1T"][:, :], u_in[:, g % 2, 0:n], start=True, stop=True
                             ).then_inc(v_ready, 1)

        def s3_pe(pe, g):
            pe.wait_ge(leaky, g + 1)
            if g >= 2:
                pe.wait_ge(x1_ready, g - 1)
            for t, n in tiles(g):
                j = t - 4 * g
                nc.tensor.matmul(oP[g % 2][0:n, j * P:(j + 1) * P], act1[:, g % 2, j * P:j * P + n], w["w2T"][:, :],
                                 start=True, stop=False)
                mm = nc.tensor.matmul(oP[g % 2][0:n, j * P:(j + 1) * P], w["ones_row"][0:1, 0:n], w["b2row"][0:1, :],
                                      start=False, stop=True)
            mm.then_inc(o_ready, 1)

        def s4_pe(pe, g):
            pe.wait_ge(h2_ready, g + 1)
            if g >= 2:
                pe.wait_ge(xT_ready, g - 1)
            for t, n in tiles(g):
                j = t - 4 * g
                mm = nc.tensor.transpose(tP[g % 2][:, j * P:j * P + n], h2[0:n, g % 3, j, :], w["ident"][0:n, 0:n])
            mm.then_inc(h2_turned, 1)

        def s1_dve(dve, g):
            ts = tiles(g)
            k = len(ts)
            dve.wait_ge(agg_in[g % 3], 16 * sum(len(tiles(i)) for i in range(g % 3, g + 1, 3)))
            nc.vector.scalar_tensor_tensor(out=agg[:, g % 3, 0:k, :], in0=agg[:, g % 3, 0:k, :], scalar=NEG_INIT,
                                           in1=agg[:, g % 3, 0:k, :], op0=ALU.is_gt, op1=ALU.mult).then_inc(aggfix, 1)
            dve.wait_ge(aggfix, g + 1)
            dve.wait_ge(h_in[g % 2], total(g, 2))
            m = min(n for _, n in ts)
            nc.vector.scalar_tensor_tensor(out=agg[0:m, g % 3, 0:k, :], in0=h1[0:m, g % 2, 0:k, :],
                                           scalar=w["eps1"][0:m, 0:1], in1=agg[0:m, g % 3, 0:k, :], op0=ALU.mult,
                                           op1=ALU.add).then_inc(u_rows, 1)

        def s1_act(act, g):
            a, n = cols(g)
            act.wait_ge(h_turned, g + 1)
            if g >= 2:
                act.wait_ge(v_ready, g - 1)
            nc.scalar.copy(u_in[:, g % 2, 0:n], hP[g % 2][:, 0:n]).then_inc(u_ready, 1)

        def s2_act(act, g):
            a, n = cols(g)
            act.wait_ge(v_ready, g + 1)
            if g >= 1:
                act.wait_ge(leaky, g)
            nc.scalar.activation(v_b[:, 0:n], vP[g % 2][:, 0:n], ACT.Identity, bias=w["b1c"][:, 0:1]
                                 ).then_inc(vb_ready, 1)

        def s2_dve(dve, g):
            a, n = cols(g)
            dve.wait_ge(vb_ready, g + 1)
            if g >= 2:
                dve.wait_ge(o_ready, g - 1)
            nc.vector.scalar_tensor_tensor(out=act1[:, g % 2, 0:n], in0=v_b[:, 0:n], scalar=LEAKY, in1=v_b[:, 0:n],
                                           op0=ALU.mult, op1=ALU.max).then_inc(leaky, 1)

        lncount = [0]

        def s3_dve(dve, g):
            dve.wait_ge(o_ready, g + 1)
            dve.wait_ge(xr_in[g % 3], total(g, 3))
            ts = tiles(g)
            k = len([1 for _, n in ts if n == P])
            if k:
                nc_last = nc.vector.tensor_tensor(xr[:, g % 3, 0:k, :], oP[g % 2][:, 0:k * P].rearrange("p (j f) -> p j f", f=P),
                                                  xr[:, g % 3, 0:k, :], ALU.add)
                rows_ = P
            if k < len(ts):
                n = ts[-1][1]
                nc_last = nc.vector.tensor_tensor(xr[0:n, g % 3, k, :], oP[g % 2][0:n, k * P:(k + 1) * P],
                                                  xr[0:n, g % 3, k, :], ALU.add)
            nc_last.then_inc(x1_ready, 1)
            dve.wait_ge(x1_ready, g + 1)
            if g >= 1:
                dve.wait_ge(h2_ready, g)
            for t, n in ts:
                j = t - 4 * g
                ins = nc.vector.bn_stats(stats[0:n, j, :], xr[0:n, g % 3, j, :])
            ins.then_inc(ln, 1)
            lncount[0] += 1
            dve.wait_ge(ln, lncount[0])
            for t, n in ts:
                j = t - 4 * g
                ins = nc.vector.bn_aggr(mv[0:n, j, :], stats[0:n, j, :])
            ins.then_inc(ln, 1)
            lncount[0] += 1
            dve.wait_ge(ln, lncount[0])
            m, k = min(n for _, n in ts), len(ts)
            nc.vector.tensor_scalar(mv[0:m, 0:k, 1], mv[0:m, 0:k, 1], LN_EPS, None, ALU.add).then_inc(ln, 1)
            lncount[0] += 1
            dve.wait_ge(root, g + 1)
            nc.vector.reciprocal(rstd[0:m, 0:k], rstd[0:m, 0:k]).then_inc(ln, 1)
            lncount[0] += 1
            dve.wait_ge(ln, lncount[0])
            nc.vector.scalar_tensor_tensor(out=shift[0:m, 0:k], in0=mv[0:m, 0:k, 0], scalar=-1.0, in1=rstd[0:m, 0:k],
                                           op0=ALU.mult, op1=ALU.mult).then_inc(ln, 1)
            lncount[0] += 1

        def s3_act(act, g):
            ts = tiles(g)
            m, k = min(n for _, n in ts), len(ts)
            act.wait_ge(ln, 5 * g + 3)
            nc.scalar.activation(rstd[0:m, 0:k], mv[0:m, 0:k, 1], ACT.Sqrt).then_inc(root, 1)
            act.wait_ge(ln, 5 * g + 5)
            if g >= 3:
                act.wait_ge(rows_out[g % 3], 2 * total(g - 3, 3))
                act.wait_ge(h2_turned, g - 2)
            for t, n in ts:
                j = t - 4 * g
                ins = nc.scalar.activation(h2[0:n, g % 3, j, :], xr[0:n, g % 3, j, :], ACT.Relu,
                                           bias=shift[0:n, j:j + 1], scale=rstd[0:n, j:j + 1])
            ins.then_inc(h2_ready, 1)

        def s4_act(act, g):
            a, n = cols(g)
            act.wait_ge(h2_turned, g + 1)
            nc.scalar.copy(xT[:, a:a + n], tP[g % 2][:, 0:n]).then_inc(xT_ready, 1)

        def skewed(stages):
            for turn in range(G + len(stages) - 1):
                for k, stage in enumerate(stages):
                    if stage and 0 <= turn - k < G:
                        stage(turn - k)

        @block.tensor
        def _(pe):
            skewed([lambda g: s1_pe(pe, g), lambda g: s2_pe(pe, g), lambda g: s3_pe(pe, g), lambda g: s4_pe(pe, g)])

        @block.vector
        def _(dve):
            nc.vector.memset(xT[:, pl.N:pl.cols], 0.0)
            skewed([lambda g: s1_dve(dve, g), lambda g: s2_dve(dve, g), lambda g: s3_dve(dve, g), None])

        @block.scalar
        def _(act):
            skewed([lambda g: s1_act(act, g), lambda g: s2_act(act, g), lambda g: s3_act(act, g), lambda g: s4_act(act, g)])


def as_columns(pl, counts, i):
    return counts.rearrange("p t c -> p (t c)")[:, 2 * pl.cols * i:2 * pl.cols * (i + 1)].bitcast(F32)


def edge_pages(pl):
    page = max(k for k in range(1, 1025) if pl.E % k == 0)
    return pl.E // page, page, max(k for k in range(1, 6) if page % k == 0)


def page_in(act, pl, tile, dram, at):
    n, page = tile.shape
    return act.dma_start(tile, dram[bass.ds(at, page)].rearrange("(a k) -> a k", a=1).broadcast_to([n, page]))


def general_maxima(nc, pl, w, counts, one_by_one, h1_dram, run_dram):
    src, dst, edge_weight = one_by_one
    T, last = pl.tiles, pl.last
    pages, page, U = edge_pages(pl)
    with ExitStack() as ctx:
        def sb(name, shape, dt):
            return ctx.enter_context(nc.sbuf_tensor(name, shape, dt))

        def sem(name):
            return ctx.enter_context(nc.semaphore(name))

        h1T, aggT = as_columns(pl, counts, 0), as_columns(pl, counts, 1)
        row = sb("row", [P, P], F32)
        tile_cols = sb("tile_cols", [P, P], F32)
        ends = sb("ends", [1, 2, page], I32)
        wpage = sb("wpage", [P, page], F32)
        colP = ctx.enter_context(nc.psum_tensor("colP", [P, 512], F32))
        row_in = sem("row_in")
        row_turned = sem("row_turned")
        row_used = sem("row_used")
        row_out = sem("row_out")
        page_here = sem("page_here")
        started = sem("started")
        cut = sem("cut")
        edge_done = sem("edge_done")
        named = sem("named")

        with nc.Block() as block:
            @block.sync
            def _(sp):
                def load(t, n, node):
                    sp.wait_ge(row_turned, t)
                    sp.dma_start(row[0:n, :], h1_dram[node, :]).then_inc(row_in, 16)

                def store(t, n, node):
                    sp.wait_ge(row_used, T + t + 1)
                    sp.dma_start(run_dram[node, :], row[0:n, :]).then_inc(row_out, 16)
                load(0, P, slice(0, P))
                with sp.Fori(1, T - 1) as t:
                    load(t, P, bass.ds(P * t, P))
                load(T - 1, last, slice(P * (T - 1), pl.N))
                with sp.Fori(0, T - 1) as t:
                    store(t, P, bass.ds(P * t, P))
                store(T - 1, last, slice(P * (T - 1), pl.N))
                sp.wait_ge(row_out, 16 * T)

            @block.scalar
            def _(act):
                with act.Fori(0, pages) as i:
                    act.wait_ge(edge_done, page * i)
                    page_in(act, pl, ends[:, 0, :], src, page * i).then_inc(page_here, 16)
                    page_in(act, pl, ends[:, 1, :], dst, page * i).then_inc(page_here, 16)
                    page_in(act, pl, wpage[:, :], edge_weight, page * i).then_inc(page_here, 16)

            @block.gpsimd
            def _(pool):
                nc.gpsimd.iota(w["row_of"][:, :], pattern=[[P, T]], base=0, channel_multiplier=1).then_inc(named, 1)

            @block.tensor
            def _(pe):
                def rows_to_columns(t, n):
                    pe.wait_ge(row_in, 16 * t + 16)
                    pe.wait_ge(row_used, t)
                    nc.tensor.transpose(colP[:, 0:n], row[0:n, :], w["ident"][0:n, 0:n]).then_inc(row_turned, 1)

                def columns_to_rows(t):
                    pe.wait_ge(cut, t + 1)
                    nc.tensor.transpose(colP[:, 0:P], tile_cols[:, :], w["ident"][:, :]).then_inc(row_turned, 1)
                with pe.Fori(0, T - 1) as t:
                    rows_to_columns(t, P)
                rows_to_columns(T - 1, last)
                with pe.Fori(0, T) as t:
                    columns_to_rows(t)

            @block.vector
            def _(dve):
                def out_of_psum(t, n):
                    dve.wait_ge(row_turned, t + 1)
                    nc.vector.tensor_copy(h1T[:, bass.ds(P * t, n)], colP[:, 0:n]).then_inc(row_used, 1)

                def rows_out(t):
                    dve.wait_ge(row_used, T + t)
                    nc.vector.tensor_copy(tile_cols[:, :], aggT[:, bass.ds(P * t, P)]).then_inc(cut, 1)
                    dve.wait_ge(row_turned, T + t + 1)
                    dve.wait_ge(row_out, 16 * t)
                    nc.vector.tensor_copy(row[:, :], colP[:, 0:P]).then_inc(row_used, 1)
                nc.vector.memset(aggT[:, :], NEG_INIT).then_inc(started, 1)
                with dve.Fori(0, T) as t:
                    out_of_psum(t, P)
                dve.wait_ge(started, 1)
                dve.wait_ge(row_used, T)
                with dve.Fori(0, pages) as i:
                    dve.wait_ge(page_here, 48 * i + 48)
                    nc.vector.tensor_copy(tile_cols[0:1, 0:1], w["ones_row"][0:1, 0:1])
                    with dve.Fori(0, page // U) as k:
                        s, d = ends_of(nc, pl, ends, U * k, U)
                        for u in range(U):
                            to = aggT[:, bass.ds(d[u], 1)]
                            dve.wait_ge(edge_done, page * i + U * k + u)
                            nc.vector.scalar_tensor_tensor(out=to, in0=h1T[:, bass.ds(s[u], 1)],
                                                           scalar=wpage[:, bass.ds(U * k + u, 1)], in1=to,
                                                           op0=ALU.mult, op1=ALU.max).then_inc(edge_done, 1)
                dve.wait_ge(edge_done, pl.E)
                with dve.Fori(0, T) as t:
                    rows_out(t)
                dve.wait_ge(named, 1)


def ends_of(nc, pl, ends, k, n):
    return [nc.values_load_multi_w_load_instructions(
        ends[0:1, e, bass.ds(k, n)], engines=[mybir.EngineType.DVE], min_val=0, max_val=pl.N - 1,
        skip_runtime_bounds_check_because="the reference takes nodes below N")[1] for e in range(2)]


def layers(nc, pl, w, counts, xT, weight, x1_dram, h2_dram, out, tag="", one_by_one=None):
    T, last, S, W, G = pl.tiles, pl.last, pl.steps, pl.width, pl.groups
    with ExitStack() as ctx:
        def sb(name, shape, dt):
            return ctx.enter_context(nc.sbuf_tensor(tag + name, shape, dt))

        def sem(name):
            return ctx.enter_context(nc.semaphore(tag + name))

        def ps(name):
            return ctx.enter_context(nc.psum_tensor(tag + name, [P, 512], F32))

        parts = sb("parts", [P, T, 3, P], BF16)
        rest = sb("rest", [P, 4, P], F32)
        lw = sb("lw", [P, pl.L, P], F32)
        agg = sb("agg", [P, 2, W], F32)
        rg = sb("rg", [P, W], F32)
        zg = sb("zg", [P, W], F32)
        ng = sb("ng", [P, W], F32)
        hn = sb("hn", [P, W], F32)

        mP = [ps(f"mP{i}") for i in range(2)]
        aP = [ps(f"aP{i}") for i in range(2)]
        rP, zP, iP, nP = ps("rP"), ps("zP"), ps("iP"), ps("nP")

        lw_in = sem("lw_in")
        m_ready = sem("m_ready")
        m_hi = sem("m_hi")
        m_rest = sem("m_rest")
        m_mid = sem("m_mid")
        m_lo = sem("m_lo")
        a_ready = sem("a_ready")
        a_out = sem("a_out")
        g_ready = sem("g_ready")
        r_done = sem("r_done")
        z_done = sem("z_done")
        hn_r = sem("hn_r")
        hn_i = sem("hn_i")
        n_done = sem("n_done")
        diff = sem("diff")
        prod = sem("prod")
        x_new = sem("x_new")

        if one_by_one:
            src, dst, _ = one_by_one
            mT, sumT = as_columns(pl, counts, 0), as_columns(pl, counts, 1)
            pages, page, U = edge_pages(pl)
            ends = as_columns(pl, counts, 2)[0:1, 0:2 * page].bitcast(I32).rearrange("p (e k) -> p e k", e=2)
            page_here = sem("page_here")
            m_out = sem("m_out")
            lw_cut = sem("lw_cut")
            lw_now = rest[:, 0, :]
            cleared = sem("cleared")
            edge_done = sem("edge_done")

        def tiles(g):
            return range(4 * g, min(4 * g + 4, T))

        def chunk_of(g):
            return min(S, -(-P * (tiles(g)[-1] + 1) // W))

        def m_group_pe(pe, l, g):
            if g == 0:
                pe.wait_ge(m_rest, G * l)
            elif g > 1:
                pe.wait_ge(m_rest, G * l + g - 1)
            pe.wait_ge(x_new, S * (l - 1) + chunk_of(g)) if not (l is 0) else None
            for t in tiles(g):
                rhs = lw[:, l, :] if isinstance(l, int) else \
                    lw[:, bass.ds(l, 1), :].rearrange("p a f -> p (a f)")
                mm = nc.tensor.matmul(mP[g % 2][:, (t - 4 * g) * P:(t - 4 * g + 1) * P],
                                      xT[:, t * P:(t + 1) * P], rhs, start=True, stop=True)
            mm.then_inc(m_ready, 1)

        def m_group_act(act, l, g):
            n = len(tiles(g))
            src_ = mP[g % 2][:, 0:n * P].rearrange("p (t f) -> p t f", f=P)
            act.wait_ge(m_ready, G * l + g + 1)
            nc.scalar.copy(parts[:, 4 * g:4 * g + n, 0, :], src_).then_inc(m_hi, 1)
            act.wait_ge(m_rest, G * l + g + 1)
            nc.scalar.copy(parts[:, 4 * g:4 * g + n, 1, :], rest[:, 0:n, :]).then_inc(m_mid, 1)

        def m_group_dve(dve, l, g):
            n = len(tiles(g))
            src_ = mP[g % 2][:, 0:n * P].rearrange("p (t f) -> p t f", f=P)
            dve.wait_ge(m_hi, G * l + g + 1)
            dve.wait_ge(m_lo, G * l + g)
            nc.vector.tensor_tensor(rest[:, 0:n, :], src_, parts[:, 4 * g:4 * g + n, 0, :], ALU.subtract
                                    ).then_inc(m_rest, 1)
            dve.wait_ge(m_mid, G * l + g + 1)
            nc.vector.tensor_tensor(parts[:, 4 * g:4 * g + n, 2, :], rest[:, 0:n, :], parts[:, 4 * g:4 * g + n, 1, :],
                                    ALU.subtract).then_inc(m_lo, 1)

        def agg_pe(pe, l, c):
            if c == 0:
                pe.wait_ge(a_out, S * l)
            elif c > 1:
                pe.wait_ge(a_out, S * l + c - 1)
            for t in range(T):
                if c == 0 and t % 4 == 0:
                    pe.wait_ge(m_lo, G * l + t // 4 + 1)
                for k in range(3):
                    mm = nc.tensor.matmul(aP[c % 2][:, 0:W], parts[:, t, k, :], counts[:, t, c * W:(c + 1) * W],
                                          start=(t == 0 and k == 0), stop=(t == T - 1 and k == 2))
            mm.then_inc(a_ready, 1)

        def gate_pe(pe, l, c):
            a = agg[:, c % 2, :]
            h = xT[:, c * W:(c + 1) * W]
            pe.wait_ge(a_out, S * l + c + 1)
            pe.wait_ge(z_done, S * l + c)
            pe.wait_ge(hn_i, S * l + c)
            nc.tensor.matmul(rP[:, 0:W], w["wihT"][:, 0, :], a, start=True, stop=False)
            nc.tensor.matmul(rP[:, 0:W], w["whhT"][:, 0, :], h, start=False, stop=True)
            nc.tensor.matmul(nP[:, 0:W], w["whhT"][:, 2, :], h, start=True, stop=True)
            nc.tensor.matmul(iP[:, 0:W], w["wihT"][:, 2, :], a, start=True, stop=True)
            nc.tensor.matmul(zP[:, 0:W], w["wihT"][:, 1, :], a, start=True, stop=False)
            nc.tensor.matmul(zP[:, 0:W], w["whhT"][:, 1, :], h, start=False, stop=True).then_inc(g_ready, 1)

        def agg_act(act, l, c):
            if one_by_one:
                act.wait_ge(edge_done, pl.E * (l + 1))
                if c >= 2:
                    act.wait_ge(g_ready, S * l + c - 1)
                nc.scalar.copy(agg[:, c % 2, :], sumT[:, c * W:(c + 1) * W]).then_inc(a_out, 1)
                return
            act.wait_ge(a_ready, S * l + c + 1)
            nc.scalar.copy(agg[:, c % 2, :], aP[c % 2][:, 0:W]).then_inc(a_out, 1)

        def gate_act(act, l, c):
            act.wait_ge(g_ready, S * l + c + 1)
            act.wait_ge(x_new, S * l + c)
            nc.scalar.activation(rg[:, :], rP[:, 0:W], ACT.Sigmoid, bias=w["bsum"][:, 0:1]).then_inc(r_done, 1)
            nc.scalar.activation(zg[:, :], zP[:, 0:W], ACT.Sigmoid, bias=w["bsum"][:, 1:2]).then_inc(z_done, 1)
            act.wait_ge(hn_i, S * l + c + 1)
            nc.scalar.activation(ng[:, :], hn[:, :], ACT.Tanh, bias=w["bihc"][:, 2:3]).then_inc(n_done, 1)

        def gate_dve(dve, l, c):
            h = xT[:, c * W:(c + 1) * W]
            dve.wait_ge(r_done, S * l + c + 1)
            dve.wait_ge(n_done, S * l + c)
            dve.wait_ge(g_ready, S * l + c + 1)
            nc.vector.scalar_tensor_tensor(out=hn[:, :], in0=nP[:, 0:W], scalar=w["bhhc"][:, 2:3], in1=rg[:, :],
                                           op0=ALU.add, op1=ALU.mult).then_inc(hn_r, 1)
            dve.wait_ge(hn_r, S * l + c + 1)
            nc.vector.tensor_tensor(hn[:, :], iP[:, 0:W], hn[:, :], ALU.add).then_inc(hn_i, 1)
            dve.wait_ge(n_done, S * l + c + 1)
            nc.vector.tensor_tensor(rg[:, :], h, ng[:, :], ALU.subtract).then_inc(diff, 1)
            dve.wait_ge(diff, S * l + c + 1)
            nc.vector.tensor_tensor(rg[:, :], rg[:, :], zg[:, :], ALU.mult).then_inc(prod, 1)
            dve.wait_ge(prod, S * l + c + 1)
            nc.vector.tensor_tensor(h, rg[:, :], ng[:, :], ALU.add).then_inc(x_new, 1)

        def messages_pe(pe, l):
            pe.wait_ge(x_new, S * l)
            pe.wait_ge(lw_cut, l + 1)
            for c in range(S):
                pe.wait_ge(m_out, S * l + c)
                nc.tensor.matmul(mP[0][:, 0:W], lw_now[:, :],
                                 xT[:, c * W:(c + 1) * W], start=True, stop=True).then_inc(m_ready, 1)

        def messages_act(act, l):
            nc.scalar.copy(lw_now[:, :], lw[:, bass.ds(l, 1), :].rearrange("p a f -> p (a f)")).then_inc(lw_cut, 1)
            for c in range(S):
                act.wait_ge(m_ready, S * l + c + 1)
                nc.scalar.copy(mT[:, c * W:(c + 1) * W], mP[0][:, 0:W]).then_inc(m_out, 1)

        def pages_act(act, l):
            with act.Fori(0, pages) as i:
                act.wait_ge(edge_done, pl.E * l + page * i)
                page_in(act, pl, ends[:, 0, :], src, page * i).then_inc(page_here, 16)
                page_in(act, pl, ends[:, 1, :], dst, page * i).then_inc(page_here, 16)

        def sums_dve(dve, l):
            dve.wait_ge(m_out, S * l + S)
            nc.vector.memset(sumT[:, :], 0.0).then_inc(cleared, 1)
            dve.wait_ge(cleared, l + 1)
            nc.vector.tensor_copy(rest[0:1, 1, 0:1], w["ones_row"][0:1, 0:1])
            with dve.Fori(0, pages) as i:
                dve.wait_ge(page_here, 32 * (pages * l + i) + 32)
                nc.vector.tensor_copy(rest[0:1, 1, 0:1], w["ones_row"][0:1, 0:1])
                with dve.Fori(0, page // U) as k:
                    s, d = ends_of(nc, pl, ends, U * k, U)
                    for u in range(U):
                        to = sumT[:, bass.ds(d[u], 1)]
                        dve.wait_ge(edge_done, pl.E * l + page * i + U * k + u)
                        nc.vector.tensor_tensor(to, to, mT[:, bass.ds(s[u], 1)], ALU.add).then_inc(edge_done, 1)

        def general_layers():
            with nc.Block() as block:
                @block.sync
                def _(sp):
                    sp.dma_start(lw[:, :, :], weight.rearrange("l p f -> p l f")).then_inc(lw_in, 16)

                @block.tensor
                def _(pe):
                    with pe.Fori(0, pl.L) as l:
                        messages_pe(pe, l)
                        for c in range(S):
                            gate_pe(pe, l, c)

                @block.scalar
                def _(act):
                    act.wait_ge(lw_in, 16)
                    with act.Fori(0, pl.L) as l:
                        messages_act(act, l)
                        pages_act(act, l)
                        agg_act(act, l, 0)
                        for c in range(1, S):
                            agg_act(act, l, c)
                            gate_act(act, l, c - 1)
                        gate_act(act, l, S - 1)

                @block.vector
                def _(dve):
                    with dve.Fori(0, pl.L) as l:
                        sums_dve(dve, l)
                        for c in range(S):
                            gate_dve(dve, l, c)

        def layer_pe(pe, l, more):
            agg_pe(pe, l, 0)
            for c in range(1, S):
                agg_pe(pe, l, c)
                gate_pe(pe, l, c - 1)
            gate_pe(pe, l, S - 1)
            if more:
                for g in range(G):
                    m_group_pe(pe, l + 1, g)

        def layer_act(act, l, more):
            agg_act(act, l, 0)
            for c in range(1, S):
                agg_act(act, l, c)
                gate_act(act, l, c - 1)
            gate_act(act, l, S - 1)
            if more:
                for g in range(G):
                    m_group_act(act, l + 1, g)

        def layer_dve(dve, l, more):
            for c in range(S):
                gate_dve(dve, l, c)
            if more:
                for g in range(G):
                    m_group_dve(dve, l + 1, g)

        def fast_layers():
            with nc.Block() as block:
                @block.sync
                def _(sp):
                    sp.dma_start(lw[:, :, :], weight.rearrange("l p f -> p l f")).then_inc(lw_in, 16)

                @block.tensor
                def _(pe):
                    pe.wait_ge(lw_in, 16)
                    for g in range(G):
                        m_group_pe(pe, 0, g)
                    with pe.Fori(0, pl.L - 1) as l:
                        layer_pe(pe, l, True)
                    layer_pe(pe, pl.L - 1, False)

                @block.scalar
                def _(act):
                    for g in range(G):
                        m_group_act(act, 0, g)
                    with act.Fori(0, pl.L - 1) as l:
                        layer_act(act, l, True)
                    layer_act(act, pl.L - 1, False)

                @block.vector
                def _(dve):
                    for g in range(G):
                        m_group_dve(dve, 0, g)
                    with dve.Fori(0, pl.L - 1) as l:
                        layer_dve(dve, l, True)
                    layer_dve(dve, pl.L - 1, False)

        general_layers() if one_by_one else fast_layers()

    with ExitStack() as ctx:
        rx = ctx.enter_context(nc.sbuf_tensor(tag + "rx", [P, T, P], F32))
        r1 = ctx.enter_context(nc.sbuf_tensor(tag + "r1", [P, 3, 4, P], F32))
        tP = [ctx.enter_context(nc.psum_tensor(tag + f"tP2{i}", [P, 512], F32)) for i in range(2)]
        h2_in = ctx.enter_context(nc.semaphore(tag + "h2_in"))
        x1_in = [ctx.enter_context(nc.semaphore(tag + f"x1_in{i}")) for i in range(3)]
        turned = ctx.enter_context(nc.semaphore(tag + "x_turned"))
        with_h2 = ctx.enter_context(nc.semaphore(tag + "with_h2"))
        summed = ctx.enter_context(nc.semaphore(tag + "summed"))
        stored = ctx.enter_context(nc.semaphore(tag + "stored"))
        full = pl.N // P

        def spans(g):
            a, b = 4 * g, min(4 * g + 4, T)
            k = min(b, full) - a
            found = [(P, 0, k, P * a)] if k > 0 else []
            if b > full:
                found.append((last, full - a, 1, P * full))
            return found

        def n_x1(g):
            return 16 * sum(len(spans(k)) for k in range(g % 3, g + 1, 3))

        with nc.Block() as block:
            @block.sync
            def _(sp):
                sp.dma_start(rx[:, 0:full, :], h2_dram[0:P * full, :].rearrange("(t p) f -> p t f", p=P)).then_inc(h2_in, 16)
                sp.dma_start(rx[0:last, full, :], h2_dram[P * full:pl.N, :]).then_inc(h2_in, 16)
                for g in range(G):
                    if g >= 3:
                        sp.wait_ge(summed, g - 2)
                    for n, s, k, node in spans(g):
                        d = x1_dram[node:node + n * k, :].rearrange("(t p) f -> p t f", p=n)
                        sp.dma_start(r1[0:n, g % 3, s:s + k, :], d).then_inc(x1_in[g % 3], 16)

            @block.gpsimd
            def _(pool):
                done = 0
                for g in range(G):
                    pool.wait_ge(summed, g + 1)
                    for n, s, k, node in spans(g):
                        d = out[node:node + n * k, :].rearrange("(t p) f -> p t f", p=n)
                        pool.dma_start(d, rx[0:n, 4 * g + s:4 * g + s + k, :]).then_inc(stored, 16)
                        done += 16
                pool.wait_ge(stored, done)

            @block.tensor
            def _(pe):
                for g in range(G):
                    if g >= 2:
                        pe.wait_ge(with_h2, g - 1)
                    for t in range(4 * g, min(4 * g + 4, T)):
                        mm = nc.tensor.transpose(tP[g % 2][:, (t - 4 * g) * P:(t - 4 * g + 1) * P],
                                                 xT[:, t * P:(t + 1) * P], w["ident"][:, :])
                    mm.then_inc(turned, 1)

            @block.vector
            def _(dve):
                dve.wait_ge(h2_in, 32)
                for g in range(G):
                    dve.wait_ge(turned, g + 1)
                    for n, s, k, node in spans(g):
                        r = rx[0:n, 4 * g + s:4 * g + s + k, :]
                        ins = nc.vector.tensor_tensor(r, tP[g % 2][0:n, s * P:(s + k) * P].rearrange("p (t f) -> p t f", f=P),
                                                      r, ALU.add)
                    ins.then_inc(with_h2, 1)
                    dve.wait_ge(with_h2, g + 1)
                    dve.wait_ge(x1_in[g % 3], n_x1(g))
                    for n, s, k, node in spans(g):
                        r = rx[0:n, 4 * g + s:4 * g + s + k, :]
                        ins = nc.vector.tensor_tensor(r, r, r1[0:n, g % 3, s:s + k, :], ALU.add)
                    ins.then_inc(summed, 1)


_INS = ['x', 'src', 'dst', 'edge_weight', 'L0_gnn_w1', 'L0_gnn_b1', 'L0_gnn_w2', 'L0_gnn_b2', 'L0_gnn_eps',
        'L1_gnn_weight', 'L1_gnn_w_ih', 'L1_gnn_w_hh', 'L1_gnn_b_ih', 'L1_gnn_b_hh']


def kernel(**inputs):
    import numpy as _np
    import concourse.bacc as _bacc
    from concourse import mybir as _mybir
    from concourse.bass_utils import run_bass_kernel_spmd as _run

    nc = _bacc.Bacc("TRN2", target_bir_lowering=False, num_devices=1)
    arrays, args = {}, []
    for name in _INS:
        a = _np.ascontiguousarray(inputs[name])
        arrays[f"in_{name}_dram"] = a
        args.append(nc.dram_tensor(f"in_{name}_dram", a.shape, _mybir.dt.from_np(a.dtype), kind="ExternalInput").ap())
    shape = tuple(inputs['x'].shape)
    args.append(nc.dram_tensor("out_0_dram", shape, _mybir.dt.float32, kind="ExternalOutput").ap())
    gnn_kernel(nc, *args)
    r = _run(nc, [arrays], core_ids=[0])
    return r.results[0]["out_0_dram"]
```

```python
from contextlib import ExitStack

import concourse.bass as bass
from concourse import mybir

P = 128
ALU = mybir.AluOpType
ACT = mybir.ActivationFunctionType
F32 = mybir.dt.float32
BF16 = mybir.dt.bfloat16
FP16 = mybir.dt.float16
I32 = mybir.dt.int32

NEG_INIT = -1.0e9
LEAKY = 0.01
LN_EPS = 1.0e-5
FAR = 8192.0
PAD_DST = 4095
RESET = -(2.0 ** 120)
WIN = 20
DEPTH = 4


class Plan:

    def __init__(self, nodes, feat, edges, layers):
        self.N, self.E, self.L = nodes, edges, layers
        assert feat == P
        self.tiles = -(-nodes // P)
        self.last = nodes - P * (self.tiles - 1)
        self.chunks = -(-edges // 512)
        self.chunks += -self.chunks % DEPTH
        assert self.chunks <= P and nodes <= PAD_DST
        self.run = 4 * self.chunks
        self.slots = P * self.run
        self.cols = P * self.tiles
        self.acols = nodes + WIN - 1
        self.groups = -(-self.tiles // 4)
        self.steps = 7
        self.width = self.cols // self.steps // 64 * 64
        while self.width * self.steps < nodes:
            self.width += 64
        assert self.width <= 512 and self.width * self.steps <= self.acols


def gnn_kernel(nc, x, src, dst, edge_weight, w1, b1, w2, b2, eps, weight, w_ih, w_hh, b_ih, b_hh, out):
    N, F = x.shape
    pl = Plan(N, F, src.shape[0], weight.shape[0])
    h1_dram = nc.dram_tensor("h1_rows", (N, P), F32, kind="Internal").ap()
    x1_dram = nc.dram_tensor("x1_rows", (N, P), F32, kind="Internal").ap()
    h2_dram = nc.dram_tensor("h2_rows", (N, P), F32, kind="Internal").ap()
    run_dram = nc.dram_tensor("run_rows", (pl.slots + 1, P), F32, kind="Internal").ap()

    with ExitStack() as ctx:
        def sb(name, shape, dt, stack=ctx):
            return stack.enter_context(nc.sbuf_tensor(name, shape, dt))

        counts = sb("counts", [P, pl.tiles, pl.acols], BF16)
        w = dict(
            ident=sb("ident", [P, P], F32),
            w1T=sb("w1T", [P, P], F32),
            w2T=sb("w2T", [P, P], F32),
            wihT=sb("wihT", [P, 3, P], F32),
            whhT=sb("whhT", [P, 3, P], F32),
            b1c=sb("b1c", [P, 1], F32),
            bihc=sb("bihc", [P, 3], F32),
            bhhc=sb("bhhc", [P, 3], F32),
            bsum=sb("bsum", [P, 2], F32),
            b2row=sb("b2row", [1, P], F32),
            ones_row=sb("ones_row", [1, P], F32),
            eps1=sb("eps1", [P, 1], F32),
            row_of=sb("row_of", [P, pl.tiles], I32),
            odd=sb("odd", [1, 1], I32),
        )
        sems = {}
        edges(nc, pl, w, counts, x, src, dst, edge_weight, w1, b1, w2, b2, eps, weight, w_ih, w_hh, b_ih, b_hh,
              h1_dram, run_dram)
        xT = sb("xT", [P, pl.cols], F32)
        mlp(nc, pl, w, sems, xT, x, h1_dram, run_dram, x1_dram, h2_dram)
        layers(nc, pl, w, sems, counts, xT, weight, x1_dram, h2_dram, out)
        odd = nc.values_load(w["odd"][0:1, 0:1], min_val=0, max_val=1,
                             skip_runtime_bounds_check_because="it is clamped to one when it is made")
        with nc.If(odd > 0):
            one_by_one = (src, dst, edge_weight)
            clear_semaphores(nc, sems)
            general_maxima(nc, pl, w, counts, one_by_one, h1_dram, run_dram)
            mlp(nc, pl, w, sems, xT, x, h1_dram, run_dram, x1_dram, h2_dram, "general_")
            layers(nc, pl, w, sems, counts, xT, weight, x1_dram, h2_dram, out, "general_", one_by_one)


def edges(nc, pl, w, counts, x, src, dst, edge_weight, w1, b1, w2, b2, eps, weight, w_ih, w_hh, b_ih, b_hh,
          h1_dram, run_dram):
    R, T, last, RUN = pl.chunks, pl.tiles, pl.last, pl.run
    TW = T * WIN
    turns = R // DEPTH
    assert turns - 1 >= T
    whole_p = pl.E // RUN
    rest_p = pl.E - whole_p * RUN
    whole_r = pl.E // 512
    rest_r = pl.E - whole_r * 512
    GX = pl.groups

    with ExitStack() as ctx:
        def sb(name, shape, dt):
            return ctx.enter_context(nc.sbuf_tensor(name, shape, dt))

        def sem(name):
            return ctx.enter_context(nc.semaphore(name))

        def ps(name):
            return ctx.enter_context(nc.psum_tensor(name, [P, 512], F32))

        src_walk = sb("src_walk", [P, RUN], I32)
        w_walk = sb("w_walk", [P, RUN], F32)
        dstI_walk = sb("dstI_walk", [P, RUN], I32)
        dst_walk = sb("dst_walk", [P, RUN + 1], F32)
        before = sb("before", [P, 1], I32)
        beforeF = sb("beforeF", [P, 1], F32)
        hot_cnt_m = sb("hot_cnt", [P, 4 * 512], BF16)
        hot_cnt = hot_cnt_m[:, 0:4 * TW].rearrange("p (j n) -> p j n", j=4)
        dst_rows = hot_cnt_m[:, 0:1024].bitcast(I32)
        src_rows = hot_cnt_m[:, 1024:2048].bitcast(I32)
        hot_src = sb("hot_src", [P, 2, 4, P], BF16)
        src_now = sb("src_now", [P, 4 * DEPTH], F32)
        dloc = sb("dloc", [P, 512], F32)
        far = sb("far", [P, 512], F32)
        chain, carry, seam_mask = [far[:, i * P:(i + 1) * P] for i in range(3)]
        baseF = sb("baseF", [P, 2], F32)
        base = sb("base", [1, R, 2], I32)
        terms = sb("terms", [P, turns, 3, 4 * DEPTH], F32)
        now = sb("now", [P, 3, 4 * DEPTH], F32)
        iota_count = sb("iota_count", [P, TW], FP16)
        iota_src = sb("iota_src", [P, P], BF16)
        node = sb("node", [P, T], F32)
        tile0 = sb("tile0", [P, T], F32)
        walk0 = sb("walk0", [P, 1], F32)
        shiftm = sb("shiftm", [P, 2 * P], F32)
        lastn = sb("lastn", [P, T], F32)
        prevn = sb("prevn", [P, T], F32)
        ge = sb("ge", [P, P], F32)
        at_part = sb("at_part", [P, P], F32)
        scrap = dstI_walk[:, 0:RUN // 2].bitcast(BF16)
        w_tmp = hot_cnt_m[:, 0:2 * RUN].bitcast(F32)
        cnt1 = sb("cnt1", [P, 1], F32)
        upto = sb("upto", [P, T + 1], F32)
        first_n = sb("first_n", [P, 1], F32)
        seam_row = sb("seam_row", [P, 1], I32)
        seam = sb("seam", [P, 2], F32)
        tmp1 = sb("tmp1", [P, 1], F32)
        zero_row = sb("zero_row", [1, P], F32)
        mv = sb("mv", [P, T, 2], F32)
        stats = sb("stats", [P, 2, 6], F32)
        rstd = sb("rstd", [P, T], F32)
        has = rstd
        shift = sb("shift", [P, T], F32)
        xs_run = sb("xs_run", [P, max(T, DEPTH * 4), P], F32)
        xs = xs_run
        runs_b = xs_run[:, 0:DEPTH * 4, :].rearrange("p (b j) f -> p b j f", b=DEPTH)
        rows = sb("rows", [P, DEPTH, 4, P], F32)
        idx = sb("idx", [P, DEPTH, 4], I32)
        mark = sb("mark", [P, DEPTH], F32)
        w_now = sb("w_now", [P, 4 * DEPTH], F32)
        scrap2 = terms.rearrange("p i s k -> p (i s k)")[:, 0:512]
        ones_col = sb("ones_col", [P, 1], F32)
        zero_col = sb("zero_col", [P, 1], BF16)
        odd4 = sb("odd4", [P, 4], F32)

        wraw = counts[:, 0, 0:512].bitcast(F32)
        graw = counts[:, 1, 0:1536].bitcast(F32)

        cntP = [ps(f"cntP{i}") for i in range(2)]
        nodeP = ps("nodeP")
        qP = [ps(f"qP{i}") for i in range(2)]
        wP = [ps(f"wP{i}") for i in range(3)]

        x_in = [sem(f"x_in{i}") for i in range(GX)]
        e_set = sem("e_set")
        dstw_in = sem("dstw_in")
        rows_in = sem("rows_in")
        srcw_in = sem("srcw_in")
        w_in = sem("w_in")
        small_in = sem("small_in")
        zero_out = sem("zero_out")
        consts = sem("consts")
        st = sem("st")
        rooted = sem("rooted")
        normed = sem("normed")
        h1_out = sem("h1_out")
        prep = sem("prep")
        based = sem("based")
        q_turned = sem("q_turned")
        q_out = sem("q_out")
        w_turned = sem("w_turned")
        w_done = sem("w_done")
        zeroed = sem("zeroed")
        gathered = [sem(f"gathered{i}") for i in range(DEPTH)]
        idx_ready = sem("idx_ready")
        w_ready = sem("w_ready")
        marked = sem("marked")
        scaled = sem("scaled")
        maxed = sem("maxed")
        stored = [sem(f"stored{i}") for i in range(DEPTH)]
        hot_ready = sem("hot_ready")
        cnt_ready = sem("cnt_ready")
        cnt_added = sem("cnt_added")
        part_ready = sem("part_ready")
        node_ready = sem("node_ready")
        node_done = sem("node_done")
        tailsem = sem("tailsem")
        up_ready = sem("up_ready")
        zero_set = sem("zero_set")
        s_ready = sem("s_ready")
        abs_done = sem("abs_done")
        src_ready = sem("src_ready")
        found = sem("found")
        odd_summed = sem("odd_summed")
        ge_done = sem("ge_done")
        cnt1_done = sem("cnt1_done")
        now_ready = sem("now_ready")
        seam_sb = sem("seam_sb")
        shifted = sem("shifted")
        seam_spread = sem("seam_spread")
        last_turned = sem("last_turned")
        carry_ready = sem("carry_ready")
        carry_turned = sem("carry_turned")
        seam_in = sem("seam_in")
        seam_done = sem("seam_done")
        seam_out = sem("seam_out")

        pool_tiles, dve_tiles = slice(2, 10), slice(10, 17)
        early_tiles, late_tiles = range(17, 21), range(21, T)

        block = ctx.enter_context(nc.Block())

        def x_spans(g):
            a, b = 4 * g, min(4 * g + 4, T)
            k = b - a - (1 if b == T and last < P else 0)
            return ([(P, a, k)] if k else []) + ([(last, T - 1, 1)] if b == T and last < P else [])

        @block.sync
        def _(sp):
            for g in range(GX):
                for n, a, k in x_spans(g):
                    sp.dma_start(xs[0:n, a:a + k, :],
                                 x[P * a:P * a + n * k, :].rearrange("(t p) f -> p t f", p=n)).then_inc(x_in[g], 16)
            sp.dma_start(wraw[:, 0:P], w1).then_inc(w_in, 16)
            sp.dma_start(wraw[:, P:2 * P], w2).then_inc(w_in, 16)
            sp.dma_start(graw[:, 0:3 * P].rearrange("p (g f) -> p g f", g=3),
                         w_ih.rearrange("(g p) f -> p g f", p=P)).then_inc(w_in, 16)
            sp.dma_start(graw[:, 3 * P:6 * P].rearrange("p (g f) -> p g f", g=3),
                         w_hh.rearrange("(g p) f -> p g f", p=P)).then_inc(w_in, 16)
            for g in range(GX):
                sp.wait_ge(normed, min(4 * g + 4, T))
                for n, a, k in x_spans(g):
                    sp.dma_start(h1_dram[P * a:P * a + n * k, :].rearrange("(t p) f -> p t f", p=n),
                                 xs[0:n, a:a + k, :]).then_inc(h1_out, 16)
            sp.dma_start(w["eps1"][:, :], eps.rearrange("(a b) -> a b", a=1).broadcast_to([P, 1])).then_inc(small_in, 16)
            sp.dma_start(w["b1c"][:, :], b1.rearrange("(p a) -> p a", a=1)).then_inc(small_in, 16)
            sp.dma_start(w["b2row"][:, :], b2.rearrange("(a p) -> a p", a=1)).then_inc(small_in, 16)
            for g in range(3):
                sp.dma_start(w["bihc"][:, g:g + 1], b_ih[g * P:(g + 1) * P].rearrange("(p a) -> p a", a=1)
                             ).then_inc(small_in, 16)
                sp.dma_start(w["bhhc"][:, g:g + 1], b_hh[g * P:(g + 1) * P].rearrange("(p a) -> p a", a=1)
                             ).then_inc(small_in, 16)
            sp.wait_ge(tailsem, 1)
            sp.dma_start(run_dram[pl.slots:pl.slots + 1, :], zero_row[:, :]).then_inc(zero_out, 16)

            by_walk = run_dram[0:pl.slots, :].rearrange("(p k) f -> p k f", p=P)

            def step(c, u):
                b = u % DEPTH
                sp.wait_ge(maxed, 4 * c + 4)
                to = by_walk[:, 4 * c:4 * c + 4, :] if isinstance(c, int) else by_walk[:, bass.ds(4 * c, 4), :]
                sp.dma_start(to, runs_b[:, b, :, :]).then_inc(stored[b], 16)
            for c in range(DEPTH):
                step(c, c)
            with sp.Fori(1, turns) as i:
                for u in range(DEPTH):
                    step(DEPTH * i + u, u)
            for b in range(DEPTH):
                sp.wait_ge(stored[b], 16 * turns)
            sp.wait_ge(zero_out, 16)
            sp.wait_ge(small_in, 16 * 9)

        @block.gpsimd
        def _(pool):
            def gpi(tile, step, base, cm, fp=True):
                return nc.gpsimd.iota(tile, pattern=[[step, tile.shape[-1]]], base=base, channel_multiplier=cm,
                                      allow_small_or_imprecise_dtypes=True)
            nc.gpsimd.memset(w["ident"][:, :], 0.0).then_inc(consts, 1)
            nc.gpsimd.memset(shiftm[:, :], 0.0).then_inc(consts, 1)
            pool.wait_ge(consts, 2)
            nc.gpsimd.affine_select(out=w["ident"][:, :], in_=w["ident"][:, :], compare_op=ALU.not_equal, fill=1.0,
                                    base=0, pattern=[[-1, P]], channel_multiplier=1).then_inc(consts, 1)
            nc.gpsimd.affine_select(out=shiftm[:, :], in_=shiftm[:, :], compare_op=ALU.not_equal, fill=1.0,
                                    base=1, pattern=[[-1, 2 * P]], channel_multiplier=1).then_inc(consts, 1)
            gpi(iota_count[:, :], 1, 0, 0).then_inc(consts, 1)
            gpi(iota_src[:, :], 1, 0, 0).then_inc(consts, 1)
            gpi(node[:, :], P, 0, 1).then_inc(consts, 1)
            gpi(tile0[:, :], P, 0, 0).then_inc(consts, 1)
            gpi(walk0[:, :], 1, 0, RUN).then_inc(consts, 1)
            nc.gpsimd.memset(counts[:, pool_tiles, :], 0.0).then_inc(zeroed, 1)

            n_out = sum(len(x_spans(g)) for g in range(GX))
            pool.wait_ge(h1_out, 16 * n_out)

            def step(c, u):
                b = u % DEPTH
                if u >= DEPTH:
                    pool.wait_ge(maxed, 4 * c + 4 - 4 * DEPTH)
                pool.wait_ge(idx_ready, c + 1)
                pool.sem_inc(marked, 1)
                for j in range(4):
                    pool.indirect_dma_start(out=rows[:, b, j, :], out_offset=None, in_=h1_dram,
                                            in_offset=bass.IndirectOffsetOnAxis(ap=idx[:, b, j:j + 1], axis=0)
                                            ).then_inc(gathered[b], 16)
            pool.wait_ge(consts, 9)
            for c in range(DEPTH):
                step(c, c)
            with pool.Fori(1, turns) as i:
                for u in range(DEPTH):
                    step(DEPTH * i + u, u + DEPTH)

            for b in range(DEPTH):
                pool.wait_ge(stored[b], 16 * turns)
            pool.indirect_dma_start(out=rows[:, 0, 0, :], out_offset=None, in_=run_dram,
                                    in_offset=bass.IndirectOffsetOnAxis(ap=seam_row[:, 0:1], axis=0)
                                    ).then_inc(seam_in, 16)
            pool.wait_ge(seam_done, 1)
            pool.indirect_dma_start(out=run_dram, out_offset=bass.IndirectOffsetOnAxis(ap=seam_row[:, 0:1], axis=0),
                                    in_=rows[:, 0, 1, :], in_offset=None).then_inc(seam_out, 16)
            pool.wait_ge(seam_out, 16)

        @block.scalar
        def _(act):
            act.wait_ge(e_set, 2)
            act.dma_start(dstI_walk[0:whole_p, :], dst[0:whole_p * RUN].rearrange("(p k) -> p k", k=RUN)
                          ).then_inc(dstw_in, 16)
            act.dma_start(dstI_walk[whole_p:whole_p + 1, 0:rest_p],
                          dst[whole_p * RUN:pl.E].rearrange("(p k) -> p k", p=1)).then_inc(dstw_in, 16)
            act.dma_start(before[1:P, :], dst[0:(P - 1) * RUN].rearrange("(p k) -> p k", k=RUN)[:, RUN - 1:RUN],
                          allow_slow_non_contiguous=True).then_inc(dstw_in, 16)
            act.wait_ge(e_set, 3)
            act.dma_start(src_walk[0:whole_p, :], src[0:whole_p * RUN].rearrange("(p k) -> p k", k=RUN)
                          ).then_inc(srcw_in, 16)
            act.dma_start(src_walk[whole_p:whole_p + 1, 0:rest_p],
                          src[whole_p * RUN:pl.E].rearrange("(p k) -> p k", p=1)).then_inc(srcw_in, 16)
            act.wait_ge(e_set, 4)
            act.dma_start(w_walk[0:whole_p, :], edge_weight[0:whole_p * RUN].rearrange("(p k) -> p k", k=RUN)
                          ).then_inc(srcw_in, 16)
            act.dma_start(w_walk[whole_p:whole_p + 1, 0:rest_p],
                          edge_weight[whole_p * RUN:pl.E].rearrange("(p k) -> p k", p=1)).then_inc(srcw_in, 16)
            act.wait_ge(e_set, 6)
            for tile, dram in ((dst_rows, dst), (src_rows, src)):
                act.dma_start(tile[0:whole_r, :], dram[0:512 * whole_r].rearrange("(r i) -> r i", i=512)
                              ).then_inc(rows_in, 16)
                act.dma_start(tile[whole_r:whole_r + 1, 0:rest_r], dram[512 * whole_r:pl.E].rearrange("(r i) -> r i", r=1)
                              ).then_inc(rows_in, 16)

            def clear(tiles_):
                act.wait_ge(zero_set, 1)
                for t in tiles_:
                    nc.scalar.copy(counts[:, t, :], zero_col[:, 0:1].broadcast_to([P, pl.acols])).then_inc(zeroed, 1)

            clear(early_tiles)
            act.wait_ge(st, 2 * T + 3)
            nc.scalar.activation(rstd[:, :], mv[:, :, 1], ACT.Sqrt).then_inc(rooted, 1)
            act.wait_ge(st, 2 * T + 5)
            for t in range(T):
                n = P if t < T - 1 else last
                nc.scalar.activation(xs[0:n, t, :], xs[0:n, t, :], ACT.Relu, bias=shift[0:n, t:t + 1],
                                     scale=rstd[0:n, t:t + 1]).then_inc(normed, 1)
            act.wait_ge(srcw_in, 64)
            for c in range(DEPTH):
                nc.scalar.copy(idx[:, c, :], src_walk[:, 4 * c:4 * c + 4]).then_inc(idx_ready, 1)
            act.wait_ge(w_turned, 3)
            nc.scalar.copy(w["w1T"][:, :], wP[0][:, 0:P]).then_inc(w_done, 1)
            nc.scalar.copy(w["w2T"][:, :], wP[0][:, P:2 * P]).then_inc(w_done, 1)
            nc.scalar.copy(w["wihT"][:, :, :], wP[1][:, 0:3 * P].rearrange("p (g f) -> p g f", g=3)).then_inc(w_done, 1)
            nc.scalar.copy(w["whhT"][:, :, :], wP[2][:, 0:3 * P].rearrange("p (g f) -> p g f", g=3)).then_inc(w_done, 1)

            def weights(i):
                act.wait_ge(scaled, DEPTH * i)
                nc.scalar.copy(w_now[:, :], w_walk[:, 4 * DEPTH * i:4 * DEPTH * (i + 1)] if isinstance(i, int) else
                               w_walk[:, bass.ds(4 * DEPTH * i, 4 * DEPTH)]).then_inc(w_ready, 1)
                act.wait_ge(w_ready, i + 1)

            def sources(i):
                act.wait_ge(src_ready, DEPTH * i)
                nc.scalar.copy(src_now[:, :], terms[:, i, 0, :] if isinstance(i, int) else
                               terms[:, bass.ds(i, 1), 0, :].rearrange("p a k -> p (a k)")).then_inc(s_ready, 1)
                act.wait_ge(s_ready, i + 1)

            def hot_sources(c, u):
                if u >= 2:
                    act.wait_ge(cnt_ready, 2 * c - 2)
                for j in range(4):
                    ins = nc.scalar.activation(hot_src[:, u % 2, j, :], iota_src[:, :], ACT.Abs,
                                               bias=src_now[:, 4 * (u % DEPTH) + j:4 * (u % DEPTH) + j + 1])
                ins.then_inc(abs_done, 1)
                act.wait_ge(abs_done, c + 1)
                nc.scalar.activation(hot_src[:, u % 2, :, :], hot_src[:, u % 2, :, :], ACT.Relu,
                                     bias=ones_col[:, 0:1], scale=-1.0).then_inc(src_ready, 1)

            def step(c, u, more):
                b = u % DEPTH
                hot_sources(c, u)
                act.wait_ge(gathered[b], 16 * (c - b) + 64)
                if more:
                    k = 4 * (c + DEPTH)
                    nc.scalar.copy(idx[:, b, :], src_walk[:, k:k + 4] if isinstance(c, int) else
                                   src_walk[:, bass.ds(k, 4)]).then_inc(idx_ready, 1)
                for j in range(4):
                    ins = nc.scalar.activation(rows[:, b, j, :], rows[:, b, j, :], ACT.Copy,
                                               scale=w_now[:, 4 * b + j:4 * b + j + 1])
                ins.then_inc(scaled, 1)

            clear(late_tiles)
            act.wait_ge(q_out, 3)
            act.wait_ge(consts, 9)
            act.wait_ge(tailsem, 3)
            weights(0)
            sources(0)
            for c in range(DEPTH):
                step(c, c, True)
            with act.Fori(1, turns - 1) as i:
                weights(i)
                sources(i)
                for u in range(DEPTH):
                    step(DEPTH * i + u, u + DEPTH, True)
            weights(turns - 1)
            sources(turns - 1)
            for u in range(DEPTH):
                step(R - DEPTH + u, u + DEPTH, False)

        @block.tensor
        def _(pe):
            pe.wait_ge(consts, 9)
            pe.wait_ge(prep, 1)
            for j in range(2):
                mm = nc.tensor.matmul(nodeP[0:1, j * R:(j + 1) * R], baseF[0:R, j:j + 1],
                                      w["ident"][0:R, 0:R], start=True, stop=True)
            mm.then_inc(based, 1)
            pe.wait_ge(prep, 9)
            for i, frm in enumerate((far, dloc)):
                for j in range(4):
                    mm = nc.tensor.transpose(qP[i][:, j * R:(j + 1) * R], frm[0:R, j * P:(j + 1) * P],
                                             w["ident"][0:R, 0:R])
                mm.then_inc(q_turned, 1)
            pe.wait_ge(w_in, 16 * 4)
            for i in range(2):
                mm = nc.tensor.transpose(wP[0][:, i * P:(i + 1) * P], wraw[:, i * P:(i + 1) * P], w["ident"][:, :])
            mm.then_inc(w_turned, 1)
            for b in range(2):
                for i in range(3):
                    mm = nc.tensor.transpose(wP[1 + b][:, i * P:(i + 1) * P],
                                             graw[:, (3 * b + i) * P:(3 * b + i + 1) * P], w["ident"][:, :])
                mm.then_inc(w_turned, 1)

            def step(c, u):
                for v in range(2):
                    pe.wait_ge(src_ready, c + 1)
                    pe.wait_ge(hot_ready, 2 * c + v + 1)
                    if u >= 1:
                        pe.wait_ge(cnt_added, 2 * c + v - 1)
                    for j in range(2):
                        mm = nc.tensor.matmul(cntP[v][:, 0:TW], hot_src[:, u % 2, 2 * v + j, :],
                                              hot_cnt[:, 2 * v + j, :], start=(j == 0), stop=(j == 1))
                    mm.then_inc(cnt_ready, 1)

            def nodes_of_tile(t):
                pe.wait_ge(part_ready, t + 1)
                pe.wait_ge(node_done, t)
                nc.tensor.matmul(nodeP[:, 0:RUN + 1], at_part[:, :], dst_walk[:, :], start=True, stop=True
                                 ).then_inc(node_ready, 1)

            for c in range(DEPTH):
                step(c, c)
            with pe.Fori(1, turns) as i:
                for u in range(DEPTH):
                    step(DEPTH * i + u, u + DEPTH)
                    if u == 0:
                        nodes_of_tile(i - 1)

            pe.wait_ge(found, 4)
            nc.tensor.matmul(cntP[0][0:1, 0:4], ones_col[:, 0:1], odd4[:, :], start=True, stop=True).then_inc(odd_summed, 1)
            pe.wait_ge(up_ready, 1)
            nc.tensor.matmul(qP[0][:, 0:T], shiftm[:, 0:P], upto[:, 1:T + 1], start=True, stop=False)
            nc.tensor.matmul(qP[0][:, 0:T], shiftm[:, P:2 * P], upto[:, 0:T], start=False, stop=True
                             ).then_inc(shifted, 1)
            for i in range(2):
                mm = nc.tensor.matmul(qP[1][:, i * P:(i + 1) * P], seam[:, i:i + 1].broadcast_to([P, P]),
                                      w["ident"][:, :], start=True, stop=True)
            mm.then_inc(seam_spread, 1)
            pe.wait_ge(maxed, RUN)
            nc.tensor.transpose(wP[0][:, 0:P], runs_b[:, DEPTH - 1, 3, :], w["ident"][:, :]).then_inc(last_turned, 1)
            pe.wait_ge(carry_ready, 2)
            nc.tensor.transpose(wP[1][:, 0:P], carry[:, :], w["ident"][:, :]).then_inc(carry_turned, 1)

        @block.vector
        def _(dve):
            nc.vector.memset(zero_col[:, :], 0.0).then_inc(zero_set, 1)
            nc.vector.memset(dstI_walk[:, :], PAD_DST).then_inc(e_set, 1)
            nc.vector.memset(before[:, :], -1).then_inc(e_set, 1)
            nc.vector.memset(src_walk[:, :], 0).then_inc(e_set, 1)
            nc.vector.memset(w_walk[:, :], 0.0).then_inc(e_set, 1)
            nc.vector.memset(dst_rows[:, :], PAD_DST).then_inc(e_set, 1)
            nc.vector.memset(src_rows[:, :], 0).then_inc(e_set, 1)
            nc.vector.memset(zero_row[:, :], 0.0).then_inc(tailsem, 1)
            nc.vector.memset(w["ones_row"][:, :], 1.0).then_inc(tailsem, 1)
            nc.vector.memset(ones_col[:, :], 1.0).then_inc(tailsem, 1)
            nc.vector.memset(upto[:, 0:1], 0.0).then_inc(tailsem, 1)
            nc.vector.memset(mv[:, :, :], 1.0).then_inc(st, 1)
            dve.wait_ge(st, 1)
            done = 1
            for t in range(T):
                n = P if t < T - 1 else last
                if t % 4 == 0:
                    dve.wait_ge(x_in[t // 4], 16 * len(x_spans(t // 4)))
                if t >= 2:
                    dve.wait_ge(st, done - 2)
                nc.vector.bn_stats(stats[0:n, t % 2, :], xs[0:n, t, :]).then_inc(st, 1)
                dve.wait_ge(st, done + 1)
                nc.vector.bn_aggr(mv[0:n, t, :], stats[0:n, t % 2, :]).then_inc(st, 1)
                done += 2
            dve.wait_ge(st, done)
            nc.vector.tensor_scalar(shift[:, :], mv[:, :, 0], -1.0, None, ALU.mult).then_inc(st, 1)
            nc.vector.tensor_scalar(mv[:, :, 1], mv[:, :, 1], LN_EPS, None, ALU.add).then_inc(st, 1)
            dve.wait_ge(rooted, 1)
            nc.vector.reciprocal(rstd[:, :], rstd[:, :]).then_inc(st, 1)
            dve.wait_ge(st, done + 3)
            nc.vector.tensor_tensor(shift[:, :], shift[:, :], rstd[:, :], ALU.mult).then_inc(st, 1)

            k = [0]

            def step_of(s, ins):
                k[0] += 1
                ins.then_inc(s, 1)
                dve.wait_ge(s, k[0])

            dve.wait_ge(rows_in, 64)
            step_of(prep, nc.vector.tensor_copy(baseF[:, :], dst_rows[:, 0:512:256]))
            for j in range(2):
                step_of(prep, nc.vector.tensor_scalar(dloc[:, 256 * j:256 * j + 256], dst_rows[:, 256 * j:256 * j + 256],
                                                      baseF[:, j:j + 1], None, ALU.subtract))
            step_of(prep, nc.vector.tensor_scalar(far[:, :], dloc[:, :], float(WIN), FAR, ALU.is_ge, ALU.mult))
            nc.vector.scalar_tensor_tensor(out=scrap2[:, :], in0=dst_rows[:, :], scalar=float(PAD_DST), in1=far[:, :],
                                           op0=ALU.is_lt, op1=ALU.mult, accum_out=odd4[:, 0:1]).then_inc(found, 1)
            step_of(prep, nc.vector.tensor_tensor(dloc[:, :], dloc[:, :], far[:, :], ALU.add))
            dve.wait_ge(found, 1)
            step_of(prep, nc.vector.tensor_scalar(dst_rows[:, :], src_rows[:, :], P - 1, None, ALU.bitwise_and))
            step_of(prep, nc.vector.tensor_copy(far[:, :], dst_rows[:, :]))
            step_of(prep, nc.vector.tensor_scalar(src_rows[:, :], src_rows[:, :], 7, None, ALU.logical_shift_right))
            step_of(prep, nc.vector.scalar_tensor_tensor(out=dloc[:, :], in0=src_rows[:, :], scalar=float(WIN),
                                                         in1=dloc[:, :], op0=ALU.mult, op1=ALU.add))
            n_rows = k[0]
            dve.wait_ge(dstw_in, 48)
            dve.wait_ge(consts, 9)
            step_of(prep, nc.vector.tensor_copy(dst_walk[:, 0:RUN], dstI_walk[:, :]))
            nc.vector.tensor_copy(dst_walk[:, RUN:RUN + 1], walk0[:, :])
            nc.vector.memset(w_tmp[:, 0:1], 1.0)
            step_of(prep, nc.vector.tensor_tensor(w_tmp[:, 1:RUN], dst_walk[:, 1:RUN], dst_walk[:, 0:RUN - 1],
                                                  ALU.not_equal))
            step_of(prep, nc.vector.tensor_scalar(terms[:, :, 2, :], w_tmp.rearrange("p (i k) -> p i k", i=turns),
                                                  RESET, None, ALU.mult))
            step_of(prep, nc.vector.tensor_copy(beforeF[:, :], before[:, :]))
            nc.vector.tensor_scalar(lastn[:, :], tile0[:, :], -1.0, dst_walk[:, RUN - 1:RUN], ALU.mult, ALU.add)
            nc.vector.tensor_scalar(prevn[:, :], tile0[:, :], -1.0, beforeF[:, 0:1], ALU.mult, ALU.add)
            step_of(prep, nc.vector.tensor_scalar(scrap[:, :], dst_walk[:, 0:RUN], dst_walk[:, 0:1], 0.0, ALU.is_equal,
                                                  ALU.add, accum_out=first_n[:, 0:1]))
            step_of(prep, nc.vector.tensor_tensor(tmp1[:, :], first_n[:, :], walk0[:, :], ALU.add))
            step_of(prep, nc.vector.tensor_scalar(seam_row[:, :], tmp1[:, :], -1.0, None, ALU.add))
            step_of(prep, nc.vector.tensor_tensor(seam[:, 1:2], beforeF[:, :], dst_walk[:, 0:1], ALU.not_equal))
            step_of(prep, nc.vector.tensor_tensor(tmp1[:, :], dst_walk[:, RUN - 1:RUN], dst_walk[:, 0:1], ALU.not_equal))
            step_of(prep, nc.vector.tensor_tensor(tmp1[:, :], tmp1[:, :], seam[:, 1:2], ALU.max))
            step_of(prep, nc.vector.tensor_scalar(seam[:, 0:1], tmp1[:, :], RESET, None, ALU.mult))
            step_of(prep, nc.vector.tensor_scalar(seam[:, 1:2], seam[:, 1:2], RESET, None, ALU.mult))

            dve.wait_ge(based, 1)
            nc.vector.tensor_scalar(base[:, :, :], nodeP[0:1, 0:2 * R].rearrange("p (j c) -> p c j", j=2),
                                    0.0, float(pl.N - 1), ALU.max, ALU.min).then_inc(q_out, 1)
            for i in range(2):
                dve.wait_ge(q_turned, 1 + i)
                nc.vector.tensor_scalar(terms[:, :, i, :].rearrange("p i (d j) -> p i d j", j=4),
                                        qP[i][:, 0:4 * R].rearrange("p (j i d) -> p i d j", j=4, d=DEPTH),
                                        (-1.0, 1.0)[i], None, ALU.mult).then_inc(q_out, 1)
            dve.wait_ge(w_turned, 3)
            nc.vector.memset(counts[:, 0:2, :], 0.0).then_inc(zeroed, 1)
            nc.vector.memset(counts[:, dve_tiles, :], 0.0).then_inc(zeroed, 1)
            dve.wait_ge(small_in, 16 * 9)
            nc.vector.tensor_tensor(w["bsum"][:, :], w["bihc"][:, 0:2], w["bhhc"][:, 0:2], ALU.add).then_inc(tailsem, 1)
            nc.vector.tensor_scalar(w["eps1"][:, :], w["eps1"][:, :], 1.0, None, ALU.add).then_inc(tailsem, 1)
            dve.wait_ge(q_out, 3)
            dve.wait_ge(zeroed, 3 + T - dve_tiles.stop)

            def bases(i):
                row = base[0:1, DEPTH * i:DEPTH * i + DEPTH, :] if isinstance(i, int) else \
                    base[0:1, bass.ds(DEPTH * i, DEPTH), :]
                _, vals = nc.values_load_multi_w_load_instructions(
                    row.rearrange("p c v -> p (c v)"), engines=[mybir.EngineType.DVE], min_val=0, max_val=pl.N - 1,
                    skip_runtime_bounds_check_because="the bases are clamped to the nodes when they are made")
                return vals

            def part_of_tile(t):
                dve.wait_ge(node_ready, t)
                pc, lc = [q[:, bass.ds(t, 1)] for q in (prevn, lastn)]
                nc.vector.tensor_scalar(ge[:, :], iota_src[:, :], pc, None, ALU.is_ge).then_inc(ge_done, 1)
                dve.wait_ge(ge_done, t + 1)
                nc.vector.scalar_tensor_tensor(out=at_part[:, :], in0=iota_src[:, :], scalar=lc, in1=ge[:, :],
                                               op0=ALU.is_lt, op1=ALU.mult).then_inc(part_ready, 1)

            def count_of_tile(t):
                dve.wait_ge(node_ready, t + 1)
                nc.vector.tensor_scalar(scrap[:, :], nodeP[:, 0:RUN], node[:, bass.ds(t, 1)], 0.0, ALU.is_le, ALU.add,
                                        accum_out=cnt1[:, 0:1]).then_inc(cnt1_done, 1)
                dve.wait_ge(cnt1_done, t + 1)
                nc.vector.tensor_tensor(upto[:, bass.ds(t + 1, 1)], nodeP[:, RUN:RUN + 1], cnt1[:, 0:1], ALU.add
                                        ).then_inc(node_done, 1)

            def turn(i, first):
                src_i = terms[:, i, :, :] if isinstance(i, int) else \
                    terms[:, bass.ds(i, 1), :, :].rearrange("p a s k -> p (a s) k")
                dve.wait_ge(maxed, 4 * DEPTH * i)
                dve.wait_ge(hot_ready, 2 * DEPTH * i)
                nc.vector.tensor_copy(now[:, :, :], src_i).then_inc(now_ready, 1)
                at = bases(i)
                dve.wait_ge(now_ready, i + 1)
                for u in range(DEPTH):
                    c = DEPTH * i + u

                    def hot(j):
                        k = 4 * u + j
                        ins = nc.vector.tensor_scalar(hot_cnt[:, j, :], iota_count[:, :], now[:, 1, k:k + 1], None,
                                                      ALU.is_equal)
                        if j % 2:
                            ins.then_inc(hot_ready, 1)

                    def maximum(j):
                        if first and u == 0 and j == 0:
                            nc.vector.tensor_copy(runs_b[:, 0, 0, :], rows[:, 0, 0, :]).then_inc(maxed, 1)
                            return
                        pu, pj = (u, j - 1) if j else ((u - 1) % DEPTH, 3)
                        dve.wait_ge(maxed, 4 * c + j)
                        nc.vector.scalar_tensor_tensor(out=runs_b[:, u, j, :], in0=runs_b[:, pu, pj, :],
                                                       scalar=now[:, 2, 4 * u + j:4 * u + j + 1],
                                                       in1=rows[:, u, j, :], op0=ALU.add, op1=ALU.max
                                                       ).then_inc(maxed, 1)

                    def add_counts(v):
                        dve.wait_ge(cnt_ready, 2 * c + v + 1)
                        dve.wait_ge(cnt_added, 2 * c + v)
                        win = counts[:, :, bass.ds(at[2 * u + v], WIN)]
                        nc.vector.tensor_tensor(win, cntP[v][:, 0:TW].rearrange("p (t d) -> p t d", d=WIN), win,
                                                ALU.add).then_inc(cnt_added, 1)

                    hot(0)
                    hot(1)
                    dve.wait_ge(scaled, c + 1)
                    if first:
                        dve.wait_ge(h1_out, 16 * sum(len(x_spans(g)) for g in range(GX)))
                    else:
                        dve.wait_ge(stored[u], 16 * i)
                    maximum(0)
                    hot(2)
                    maximum(1)
                    hot(3)
                    maximum(2)
                    add_counts(0)
                    maximum(3)
                    add_counts(1)
                    if not first and u == 0:
                        part_of_tile(i - 1)
                    if not first and u == 1:
                        count_of_tile(i - 1)

            turn(0, True)
            with dve.Fori(1, turns) as i:
                turn(i, False)
            assert pl.slots - pl.E <= P
            nc.vector.scalar_tensor_tensor(out=scrap[:, 1:RUN], in0=dst_walk[:, 0:RUN - 1], scalar=0.0,
                                           in1=dst_walk[:, 1:RUN], op0=ALU.add, op1=ALU.is_gt,
                                           accum_out=odd4[:, 1:2]).then_inc(found, 1)
            dve.wait_ge(found, 2)
            nc.vector.scalar_tensor_tensor(out=scrap[:, P:RUN], in0=dst_walk[:, 0:RUN - P], scalar=0.0,
                                           in1=dst_walk[:, P:RUN], op0=ALU.add, op1=ALU.is_equal,
                                           accum_out=odd4[:, 2:3]).then_inc(found, 1)
            nc.vector.tensor_tensor(odd4[:, 3:4], beforeF[:, :], dst_walk[:, 0:1], ALU.is_gt).then_inc(found, 1)
            dve.wait_ge(node_done, turns - 1)
            nc.vector.tensor_scalar(upto[:, 0:1], upto[:, 0:1], 0.0, None, ALU.mult).then_inc(up_ready, 1)

            dve.wait_ge(seam_spread, 1)
            nc.vector.tensor_copy(seam_mask[:, :], qP[1][:, 0:P]).then_inc(seam_sb, 1)
            dve.wait_ge(last_turned, 1)
            dve.wait_ge(seam_sb, 1)
            nc.vector.tensor_tensor_scan(chain[:, :], seam_mask[:, :], wP[0][:, 0:P], 0.0, ALU.add, ALU.max
                                         ).then_inc(seam_sb, 1)
            dve.wait_ge(seam_sb, 2)
            nc.vector.memset(carry[:, 0:1], RESET).then_inc(carry_ready, 1)
            nc.vector.tensor_tensor(carry[:, 1:P], chain[:, 0:P - 1], qP[1][:, P + 1:2 * P], ALU.add
                                    ).then_inc(carry_ready, 1)
            dve.wait_ge(shifted, 1)
            nc.vector.tensor_tensor(has[:, :], upto[:, 1:T + 1], qP[0][:, 0:T], ALU.is_gt).then_inc(seam_sb, 1)
            dve.wait_ge(seam_sb, 3)
            nc.vector.scalar_tensor_tensor(out=has[:, :], in0=upto[:, 1:T + 1], scalar=float(-1 - pl.slots),
                                           in1=has[:, :], op0=ALU.add, op1=ALU.mult).then_inc(seam_sb, 1)
            dve.wait_ge(seam_sb, 4)
            nc.vector.tensor_scalar(w["row_of"][:, :], has[:, :], float(pl.slots), float(pl.slots), ALU.add, ALU.min
                                    ).then_inc(seam_sb, 1)
            dve.wait_ge(odd_summed, 1)
            dve.wait_ge(now_ready, turns)
            nc.vector.tensor_reduce(odd4[0:1, 0:1], cntP[0][0:1, 0:4], mybir.AxisListType.X, ALU.add).then_inc(found, 1)
            dve.wait_ge(found, 5)
            nc.vector.tensor_scalar(w["odd"][:, :], odd4[0:1, 0:1], 1.0, None, ALU.min).then_inc(found, 1)
            dve.wait_ge(seam_in, 16)
            dve.wait_ge(carry_turned, 1)
            nc.vector.tensor_tensor(rows[:, 0, 1, :], wP[1][:, 0:P], rows[:, 0, 0, :], ALU.max).then_inc(seam_done, 1)


def mlp(nc, pl, w, sems, xT, x, h1_dram, run_dram, x1_dram, h2_dram, tag=""):
    T, last = pl.tiles, pl.last
    G = pl.groups
    with ExitStack() as ctx:
        def sb(name, shape, dt):
            return ctx.enter_context(nc.sbuf_tensor(tag + name, shape, dt))

        def sem(name):
            return kept_semaphore(nc, sems, name)

        def ps(name):
            return ctx.enter_context(nc.psum_tensor(tag + name, [P, 512], F32))

        h1 = sb("h1", [P, 3, 4, P], F32)
        agg = sb("agg_rows", [P, 3, 4, P], F32)
        xr = sb("xr", [P, 3, 4, P], F32)
        u_in = sb("u_in", [P, 2, 512], F32)
        v_b = sb("v_b", [P, 512], F32)
        act1 = sb("act1", [P, 2, 512], F32)
        h2 = sb("h2", [P, 3, 4, P], F32)
        stats = sb("stats2", [P, 4, 6], F32)
        mv = sb("mv2", [P, 4, 2], F32)
        rstd = sb("rstd2", [P, 4], F32)
        shift = sb("shift2", [P, 4], F32)
        hP = [ps(f"hP{i}") for i in range(2)]
        vP = [ps(f"vP{i}") for i in range(2)]
        oP = [ps(f"oP{i}") for i in range(2)]
        tP = [ps(f"tP{i}") for i in range(2)]

        h_in = [sem(f"h_in{i}") for i in range(3)]
        xr_in = [sem(f"xr_in{i}") for i in range(3)]
        agg_in = [ctx.enter_context(nc.semaphore(tag + f"agg_in{i}")) for i in range(3)]
        u_rows = sem("u_rows")
        h_turned = sem("h_turned")
        aggfix = sem("aggfix")
        u_ready = sem("u_ready")
        v_ready = sem("v_ready")
        vb_ready = sem("vb_ready")
        leaky = sem("leaky")
        o_ready = sem("o_ready")
        x1_ready = sem("x1_ready")
        ln = sem("ln")
        root = sem("root")
        h2_ready = sem("h2_ready")
        rows_out = [sem(f"rows_out{i}") for i in range(3)]
        h2_turned = sem("h2_turned")
        xT_ready = sem("xT_ready")

        def tiles(g):
            return [(t, P if t < T - 1 else last) for t in range(4 * g, min(4 * g + 4, T))]

        def cols(g):
            a = 512 * g
            return a, min(512, pl.N - a)

        def move(eng, sb_tile, dram, g, to_dram, s):
            ts = tiles(g)
            fullt = [t for t, n in ts if n == P]
            n_dma = 0
            if fullt:
                a = fullt[0]
                k = len(fullt)
                d = dram[P * a:P * (a + k), :].rearrange("(t p) f -> p t f", p=P)
                s_ = sb_tile[:, 0:k, :]
                (eng.dma_start(d, s_) if to_dram else eng.dma_start(s_, d)).then_inc(s, 16)
                n_dma += 1
            if len(fullt) < len(ts):
                t, n = ts[-1]
                d = dram[P * t:P * t + n, :]
                s_ = sb_tile[0:n, t - 4 * g, :]
                (eng.dma_start(d, s_) if to_dram else eng.dma_start(s_, d)).then_inc(s, 16)
                n_dma += 1
            return n_dma

        def n_dmas(g):
            ns = [n for _, n in tiles(g)]
            return int(P in ns) + int(any(n < P for n in ns))

        def total(g, ring):
            return 16 * sum(n_dmas(k) for k in range(g % ring, g + 1, ring))

        block = ctx.enter_context(nc.Block())

        @block.sync
        def _(sp):
            def load_h1(g):
                if g >= 3:
                    sp.wait_ge(u_rows, g - 2)
                move(sp, h1[:, g % 3, :, :], h1_dram, g, False, h_in[g % 3])

            def load_x(g):
                if g >= 3:
                    sp.wait_ge(rows_out[g % 3], 2 * total(g - 3, 3))
                move(sp, xr[:, g % 3, :, :], x, g, False, xr_in[g % 3])
            load_h1(0)
            load_h1(1)
            for g in range(G):
                if g + 2 < G:
                    load_h1(g + 2)
                load_x(g)

        @block.gpsimd
        def _(pool):
            for g in range(G):
                if g >= 3:
                    pool.wait_ge(h_turned, g - 2)
                for t, _ in tiles(g):
                    pool.indirect_dma_start(out=agg[:, g % 3, t - 4 * g, :], out_offset=None, in_=run_dram,
                                            in_offset=bass.IndirectOffsetOnAxis(ap=w["row_of"][:, t:t + 1], axis=0)
                                            ).then_inc(agg_in[g % 3], 16)

        def s1_pe(pe, g):
            pe.wait_ge(u_rows, g + 1)
            if g >= 2:
                pe.wait_ge(u_ready, g - 1)
            for t, n in tiles(g):
                j = t - 4 * g
                mm = nc.tensor.transpose(hP[g % 2][:, j * P:j * P + n], agg[0:n, g % 3, j, :], w["ident"][0:n, 0:n])
            mm.then_inc(h_turned, 1)

        def s2_pe(pe, g):
            a, n = cols(g)
            pe.wait_ge(u_ready, g + 1)
            if g >= 2:
                pe.wait_ge(vb_ready, g - 1)
            nc.tensor.matmul(vP[g % 2][:, 0:n], w["w1T"][:, :], u_in[:, g % 2, 0:n], start=True, stop=True
                             ).then_inc(v_ready, 1)

        def s3_pe(pe, g):
            pe.wait_ge(leaky, g + 1)
            if g >= 2:
                pe.wait_ge(x1_ready, g - 1)
            for t, n in tiles(g):
                j = t - 4 * g
                nc.tensor.matmul(oP[g % 2][0:n, j * P:(j + 1) * P], act1[:, g % 2, j * P:j * P + n], w["w2T"][:, :],
                                 start=True, stop=False)
                mm = nc.tensor.matmul(oP[g % 2][0:n, j * P:(j + 1) * P], w["ones_row"][0:1, 0:n], w["b2row"][0:1, :],
                                      start=False, stop=True)
            mm.then_inc(o_ready, 1)

        def s4_pe(pe, g):
            pe.wait_ge(h2_ready, g + 1)
            if g >= 2:
                pe.wait_ge(xT_ready, g - 1)
            for t, n in tiles(g):
                j = t - 4 * g
                mm = nc.tensor.transpose(tP[g % 2][:, j * P:j * P + n], h2[0:n, g % 3, j, :], w["ident"][0:n, 0:n])
            mm.then_inc(h2_turned, 1)

        def s1_dve(dve, g):
            ts = tiles(g)
            k = len(ts)
            dve.wait_ge(agg_in[g % 3], 16 * sum(len(tiles(i)) for i in range(g % 3, g + 1, 3)))
            nc.vector.scalar_tensor_tensor(out=agg[:, g % 3, 0:k, :], in0=agg[:, g % 3, 0:k, :], scalar=NEG_INIT,
                                           in1=agg[:, g % 3, 0:k, :], op0=ALU.is_gt, op1=ALU.mult).then_inc(aggfix, 1)
            dve.wait_ge(aggfix, g + 1)
            dve.wait_ge(h_in[g % 3], total(g, 3))
            m = min(n for _, n in ts)
            nc.vector.scalar_tensor_tensor(out=agg[0:m, g % 3, 0:k, :], in0=h1[0:m, g % 3, 0:k, :],
                                           scalar=w["eps1"][0:m, 0:1], in1=agg[0:m, g % 3, 0:k, :], op0=ALU.mult,
                                           op1=ALU.add).then_inc(u_rows, 1)

        def s1_act(act, g):
            a, n = cols(g)
            act.wait_ge(h_turned, g + 1)
            if g >= 2:
                act.wait_ge(v_ready, g - 1)
            nc.scalar.copy(u_in[:, g % 2, 0:n], hP[g % 2][:, 0:n]).then_inc(u_ready, 1)

        def s2_act(act, g):
            a, n = cols(g)
            act.wait_ge(v_ready, g + 1)
            if g >= 1:
                act.wait_ge(leaky, g)
            nc.scalar.activation(v_b[:, 0:n], vP[g % 2][:, 0:n], ACT.Identity, bias=w["b1c"][:, 0:1]
                                 ).then_inc(vb_ready, 1)

        def s2_dve(dve, g):
            a, n = cols(g)
            dve.wait_ge(vb_ready, g + 1)
            if g >= 2:
                dve.wait_ge(o_ready, g - 1)
            nc.vector.scalar_tensor_tensor(out=act1[:, g % 2, 0:n], in0=v_b[:, 0:n], scalar=LEAKY, in1=v_b[:, 0:n],
                                           op0=ALU.mult, op1=ALU.max).then_inc(leaky, 1)

        lncount = [0]

        def s3_dve(dve, g):
            dve.wait_ge(o_ready, g + 1)
            dve.wait_ge(xr_in[g % 3], total(g, 3))
            ts = tiles(g)
            k = len([1 for _, n in ts if n == P])
            if k:
                nc_last = nc.vector.tensor_tensor(xr[:, g % 3, 0:k, :], oP[g % 2][:, 0:k * P].rearrange("p (j f) -> p j f", f=P),
                                                  xr[:, g % 3, 0:k, :], ALU.add)
                rows_ = P
            if k < len(ts):
                n = ts[-1][1]
                nc_last = nc.vector.tensor_tensor(xr[0:n, g % 3, k, :], oP[g % 2][0:n, k * P:(k + 1) * P],
                                                  xr[0:n, g % 3, k, :], ALU.add)
            nc_last.then_inc(x1_ready, 1)
            dve.wait_ge(x1_ready, g + 1)
            if g >= 1:
                dve.wait_ge(h2_ready, g)
            for t, n in ts:
                j = t - 4 * g
                ins = nc.vector.bn_stats(stats[0:n, j, :], xr[0:n, g % 3, j, :])
            ins.then_inc(ln, 1)
            lncount[0] += 1
            dve.wait_ge(ln, lncount[0])
            for t, n in ts:
                j = t - 4 * g
                ins = nc.vector.bn_aggr(mv[0:n, j, :], stats[0:n, j, :])
            ins.then_inc(ln, 1)
            lncount[0] += 1
            dve.wait_ge(ln, lncount[0])
            m, k = min(n for _, n in ts), len(ts)
            nc.vector.tensor_scalar(mv[0:m, 0:k, 1], mv[0:m, 0:k, 1], LN_EPS, None, ALU.add).then_inc(ln, 1)
            lncount[0] += 1

        def s3_dve_late(dve, g):
            ts = tiles(g)
            m, k = min(n for _, n in ts), len(ts)
            dve.wait_ge(root, g + 1)
            nc.vector.reciprocal(rstd[0:m, 0:k], rstd[0:m, 0:k]).then_inc(ln, 1)
            lncount[0] += 1
            dve.wait_ge(ln, lncount[0])
            nc.vector.scalar_tensor_tensor(out=shift[0:m, 0:k], in0=mv[0:m, 0:k, 0], scalar=-1.0, in1=rstd[0:m, 0:k],
                                           op0=ALU.mult, op1=ALU.mult).then_inc(ln, 1)
            lncount[0] += 1

        def s3_act(act, g):
            ts = tiles(g)
            m, k = min(n for _, n in ts), len(ts)
            act.wait_ge(x1_ready, g + 1)
            move(act, xr[:, g % 3, :, :], x1_dram, g, True, rows_out[g % 3])
            act.wait_ge(ln, 5 * g + 3)
            nc.scalar.activation(rstd[0:m, 0:k], mv[0:m, 0:k, 1], ACT.Sqrt).then_inc(root, 1)
            act.wait_ge(ln, 5 * g + 5)
            if g >= 3:
                act.wait_ge(rows_out[g % 3], 2 * total(g - 3, 3))
                act.wait_ge(h2_turned, g - 2)
            for t, n in ts:
                j = t - 4 * g
                ins = nc.scalar.activation(h2[0:n, g % 3, j, :], xr[0:n, g % 3, j, :], ACT.Relu,
                                           bias=shift[0:n, j:j + 1], scale=rstd[0:n, j:j + 1])
            ins.then_inc(h2_ready, 1)
            act.wait_ge(h2_ready, g + 1)
            move(act, h2[:, g % 3, :, :], h2_dram, g, True, rows_out[g % 3])

        def s4_act(act, g):
            a, n = cols(g)
            act.wait_ge(h2_turned, g + 1)
            nc.scalar.copy(xT[:, a:a + n], tP[g % 2][:, 0:n]).then_inc(xT_ready, 1)

        def skewed(*stages):
            for turn in range(G + max(late for late, _ in stages)):
                for late, stage in stages:
                    if 0 <= turn - late < G:
                        stage(turn - late)

        @block.tensor
        def _(pe):
            skewed((3, lambda g: s3_pe(pe, g)), (2, lambda g: s2_pe(pe, g)), (1, lambda g: s1_pe(pe, g)),
                   (4, lambda g: s4_pe(pe, g)))

        @block.vector
        def _(dve):
            nc.vector.memset(xT[:, pl.N:pl.cols], 0.0)
            skewed((3, lambda g: s3_dve(dve, g)), (2, lambda g: s2_dve(dve, g)), (0, lambda g: s1_dve(dve, g)),
                   (3, lambda g: s3_dve_late(dve, g)))

        @block.scalar
        def _(act):
            skewed((2, lambda g: s2_act(act, g)), (1, lambda g: s1_act(act, g)), (4, lambda g: s4_act(act, g)),
                   (3, lambda g: s3_act(act, g)))
            for g in range(G - 3, G):
                act.wait_ge(rows_out[g % 3], 2 * total(g, 3))


def kept_semaphore(nc, sems, name):
    if name not in sems:
        sems[name] = nc.alloc_semaphore(name)
    return sems[name]


def clear_semaphores(nc, sems):
    todo = list(sems.values())

    def share(engine, k):
        for s in todo[k::5]:
            engine.sem_clear(s)

    with nc.Block() as block:
        @block.sync
        def _(sp):
            share(sp, 0)

        @block.gpsimd
        def _(pool):
            share(pool, 1)

        @block.scalar
        def _(act):
            share(act, 2)

        @block.vector
        def _(dve):
            share(dve, 3)

        @block.tensor
        def _(pe):
            share(pe, 4)


def as_columns(pl, counts, i):
    return counts.rearrange("p t c -> p (t c)")[:, 2 * pl.cols * i:2 * pl.cols * (i + 1)].bitcast(F32)


def edge_pages(pl):
    page = max(k for k in range(1, 1025) if pl.E % k == 0)
    return pl.E // page, page, max(k for k in range(1, 6) if page % k == 0)


def page_in(act, pl, tile, dram, at):
    n, page = tile.shape
    return act.dma_start(tile, dram[bass.ds(at, page)].rearrange("(a k) -> a k", a=1).broadcast_to([n, page]))


def general_maxima(nc, pl, w, counts, one_by_one, h1_dram, run_dram):
    src, dst, edge_weight = one_by_one
    T, last = pl.tiles, pl.last
    pages, page, U = edge_pages(pl)
    with ExitStack() as ctx:
        def sb(name, shape, dt):
            return ctx.enter_context(nc.sbuf_tensor(name, shape, dt))

        def sem(name):
            return ctx.enter_context(nc.semaphore(name))

        h1T, aggT = as_columns(pl, counts, 0), as_columns(pl, counts, 1)
        row = sb("row", [P, P], F32)
        tile_cols = sb("tile_cols", [P, P], F32)
        ends = sb("ends", [1, 2, page], I32)
        wpage = sb("wpage", [P, page], F32)
        colP = ctx.enter_context(nc.psum_tensor("colP", [P, 512], F32))
        row_in = sem("row_in")
        row_turned = sem("row_turned")
        row_used = sem("row_used")
        row_out = sem("row_out")
        page_here = sem("page_here")
        started = sem("started")
        cut = sem("cut")
        edge_done = sem("edge_done")
        named = sem("named")

        with nc.Block() as block:
            @block.sync
            def _(sp):
                def load(t, n, node):
                    sp.wait_ge(row_turned, t)
                    sp.dma_start(row[0:n, :], h1_dram[node, :]).then_inc(row_in, 16)

                def store(t, n, node):
                    sp.wait_ge(row_used, T + t + 1)
                    sp.dma_start(run_dram[node, :], row[0:n, :]).then_inc(row_out, 16)
                load(0, P, slice(0, P))
                with sp.Fori(1, T - 1) as t:
                    load(t, P, bass.ds(P * t, P))
                load(T - 1, last, slice(P * (T - 1), pl.N))
                with sp.Fori(0, T - 1) as t:
                    store(t, P, bass.ds(P * t, P))
                store(T - 1, last, slice(P * (T - 1), pl.N))
                sp.wait_ge(row_out, 16 * T)

            @block.scalar
            def _(act):
                with act.Fori(0, pages) as i:
                    act.wait_ge(edge_done, page * i)
                    page_in(act, pl, ends[:, 0, :], src, page * i).then_inc(page_here, 16)
                    page_in(act, pl, ends[:, 1, :], dst, page * i).then_inc(page_here, 16)
                    page_in(act, pl, wpage[:, :], edge_weight, page * i).then_inc(page_here, 16)

            @block.gpsimd
            def _(pool):
                nc.gpsimd.iota(w["row_of"][:, :], pattern=[[P, T]], base=0, channel_multiplier=1).then_inc(named, 1)

            @block.tensor
            def _(pe):
                def rows_to_columns(t, n):
                    pe.wait_ge(row_in, 16 * t + 16)
                    pe.wait_ge(row_used, t)
                    nc.tensor.transpose(colP[:, 0:n], row[0:n, :], w["ident"][0:n, 0:n]).then_inc(row_turned, 1)

                def columns_to_rows(t):
                    pe.wait_ge(cut, t + 1)
                    nc.tensor.transpose(colP[:, 0:P], tile_cols[:, :], w["ident"][:, :]).then_inc(row_turned, 1)
                with pe.Fori(0, T - 1) as t:
                    rows_to_columns(t, P)
                rows_to_columns(T - 1, last)
                with pe.Fori(0, T) as t:
                    columns_to_rows(t)

            @block.vector
            def _(dve):
                def out_of_psum(t, n):
                    dve.wait_ge(row_turned, t + 1)
                    nc.vector.tensor_copy(h1T[:, bass.ds(P * t, n)], colP[:, 0:n]).then_inc(row_used, 1)

                def rows_out(t):
                    dve.wait_ge(row_used, T + t)
                    nc.vector.tensor_copy(tile_cols[:, :], aggT[:, bass.ds(P * t, P)]).then_inc(cut, 1)
                    dve.wait_ge(row_turned, T + t + 1)
                    dve.wait_ge(row_out, 16 * t)
                    nc.vector.tensor_copy(row[:, :], colP[:, 0:P]).then_inc(row_used, 1)
                nc.vector.memset(aggT[:, :], NEG_INIT).then_inc(started, 1)
                with dve.Fori(0, T) as t:
                    out_of_psum(t, P)
                dve.wait_ge(started, 1)
                dve.wait_ge(row_used, T)
                with dve.Fori(0, pages) as i:
                    dve.wait_ge(page_here, 48 * i + 48)
                    nc.vector.tensor_copy(tile_cols[0:1, 0:1], w["ones_row"][0:1, 0:1])
                    with dve.Fori(0, page // U) as k:
                        s, d = ends_of(nc, pl, ends, U * k, U)
                        for u in range(U):
                            to = aggT[:, bass.ds(d[u], 1)]
                            dve.wait_ge(edge_done, page * i + U * k + u)
                            nc.vector.scalar_tensor_tensor(out=to, in0=h1T[:, bass.ds(s[u], 1)],
                                                           scalar=wpage[:, bass.ds(U * k + u, 1)], in1=to,
                                                           op0=ALU.mult, op1=ALU.max).then_inc(edge_done, 1)
                dve.wait_ge(edge_done, pl.E)
                with dve.Fori(0, T) as t:
                    rows_out(t)
                dve.wait_ge(named, 1)


def ends_of(nc, pl, ends, k, n):
    return [nc.values_load_multi_w_load_instructions(
        ends[0:1, e, bass.ds(k, n)], engines=[mybir.EngineType.DVE], min_val=0, max_val=pl.N - 1,
        skip_runtime_bounds_check_because="the reference takes nodes below N")[1] for e in range(2)]


def layers(nc, pl, w, sems, counts, xT, weight, x1_dram, h2_dram, out, tag="", one_by_one=None):
    T, last, S, W, G = pl.tiles, pl.last, pl.steps, pl.width, pl.groups
    with ExitStack() as ctx:
        def sb(name, shape, dt):
            return ctx.enter_context(nc.sbuf_tensor(tag + name, shape, dt))

        def sem(name):
            return kept_semaphore(nc, sems, name)

        def ps(name):
            return ctx.enter_context(nc.psum_tensor(tag + name, [P, 512], F32))

        parts = sb("parts", [P, T, 3, P], BF16)
        rest = sb("rest", [P, 4, P], F32)
        lw = sb("lw", [P, pl.L, P], F32)
        agg = sb("agg", [P, 2, W], F32)
        rg = sb("rg", [P, W], F32)
        zg = sb("zg", [P, W], F32)
        ng = sb("ng", [P, W], F32)
        hn = sb("hn", [P, W], F32)

        mP = [ps(f"mP{i}") for i in range(2)]
        aP = [ps(f"aP{i}") for i in range(2)]
        rP, zP, iP, nP = ps("rP"), ps("zP"), ps("iP"), ps("nP")

        lw_in = sem("lw_in")
        m_ready = sem("m_ready")
        m_hi = sem("m_hi")
        m_rest = sem("m_rest")
        m_mid = sem("m_mid")
        m_lo = sem("m_lo")
        a_ready = sem("a_ready")
        a_out = sem("a_out")
        g_ready = sem("g_ready")
        r_done = sem("r_done")
        z_done = sem("z_done")
        hn_r = sem("hn_r")
        hn_i = sem("hn_i")
        n_done = sem("n_done")
        diff = sem("diff")
        prod = sem("prod")
        x_new = sem("x_new")

        if one_by_one:
            src, dst, _ = one_by_one
            mT, sumT = as_columns(pl, counts, 0), as_columns(pl, counts, 1)
            pages, page, U = edge_pages(pl)
            ends = as_columns(pl, counts, 2)[0:1, 0:2 * page].bitcast(I32).rearrange("p (e k) -> p e k", e=2)
            page_here = sem("page_here")
            m_out = sem("m_out")
            lw_cut = sem("lw_cut")
            lw_now = as_columns(pl, counts, 3)[:, 0:P]
            spare = as_columns(pl, counts, 3)[0:1, P:P + 1]
            cleared = sem("cleared")
            edge_done = sem("edge_done")

        def tiles(g):
            return range(4 * g, min(4 * g + 4, T))

        def chunk_of(g):
            return min(S, -(-P * (tiles(g)[-1] + 1) // W))

        def m_group_pe(pe, l, g):
            if g == 0:
                pe.wait_ge(m_rest, G * l)
            elif g > 1:
                pe.wait_ge(m_rest, G * l + g - 1)
            if not (isinstance(l, int) and l == 0):
                pe.wait_ge(x_new, S * (l - 1) + chunk_of(g))
            for t in tiles(g):
                rhs = lw[:, l, :] if isinstance(l, int) else \
                    lw[:, bass.ds(l, 1), :].rearrange("p a f -> p (a f)")
                mm = nc.tensor.matmul(mP[g % 2][:, (t - 4 * g) * P:(t - 4 * g + 1) * P],
                                      xT[:, t * P:(t + 1) * P], rhs, start=True, stop=True)
            mm.then_inc(m_ready, 1)

        def m_group_act(act, l, g):
            n = len(tiles(g))
            src_ = mP[g % 2][:, 0:n * P].rearrange("p (t f) -> p t f", f=P)
            act.wait_ge(m_ready, G * l + g + 1)
            nc.scalar.copy(parts[:, 4 * g:4 * g + n, 0, :], src_).then_inc(m_hi, 1)
            act.wait_ge(m_rest, G * l + g + 1)
            nc.scalar.copy(parts[:, 4 * g:4 * g + n, 1, :], rest[:, 0:n, :]).then_inc(m_mid, 1)

        def m_group_dve(dve, l, g):
            n = len(tiles(g))
            src_ = mP[g % 2][:, 0:n * P].rearrange("p (t f) -> p t f", f=P)
            dve.wait_ge(m_hi, G * l + g + 1)
            dve.wait_ge(m_lo, G * l + g)
            nc.vector.tensor_tensor(rest[:, 0:n, :], src_, parts[:, 4 * g:4 * g + n, 0, :], ALU.subtract
                                    ).then_inc(m_rest, 1)
            dve.wait_ge(m_mid, G * l + g + 1)
            nc.vector.tensor_tensor(parts[:, 4 * g:4 * g + n, 2, :], rest[:, 0:n, :], parts[:, 4 * g:4 * g + n, 1, :],
                                    ALU.subtract).then_inc(m_lo, 1)

        def agg_pe(pe, l, c, tiles_=range(T)):
            if c == 0 and tiles_[0] == 0:
                pe.wait_ge(a_out, S * l)
            elif c > 1:
                pe.wait_ge(a_out, S * l + c - 1)
            for t in tiles_:
                if c == 0 and t % 4 == 0:
                    pe.wait_ge(m_lo, G * l + t // 4 + 1)
                for k in range(3):
                    mm = nc.tensor.matmul(aP[c % 2][:, 0:W], parts[:, t, k, :], counts[:, t, c * W:(c + 1) * W],
                                          start=(t == 0 and k == 0), stop=(t == T - 1 and k == 2))
            if tiles_[-1] == T - 1:
                mm.then_inc(a_ready, 1)

        def gate_pe(pe, l, c):
            a = agg[:, c % 2, :]
            h = xT[:, c * W:(c + 1) * W]
            pe.wait_ge(a_out, S * l + c + 1)
            pe.wait_ge(z_done, S * l + c)
            pe.wait_ge(hn_i, S * l + c)
            nc.tensor.matmul(rP[:, 0:W], w["wihT"][:, 0, :], a, start=True, stop=False)
            nc.tensor.matmul(rP[:, 0:W], w["whhT"][:, 0, :], h, start=False, stop=True)
            nc.tensor.matmul(nP[:, 0:W], w["whhT"][:, 2, :], h, start=True, stop=True)
            nc.tensor.matmul(iP[:, 0:W], w["wihT"][:, 2, :], a, start=True, stop=True)
            nc.tensor.matmul(zP[:, 0:W], w["wihT"][:, 1, :], a, start=True, stop=False)
            nc.tensor.matmul(zP[:, 0:W], w["whhT"][:, 1, :], h, start=False, stop=True).then_inc(g_ready, 1)

        def agg_act(act, l, c):
            if one_by_one:
                act.wait_ge(edge_done, pl.E * (l + 1))
                if c >= 2:
                    act.wait_ge(g_ready, S * l + c - 1)
                nc.scalar.copy(agg[:, c % 2, :], sumT[:, c * W:(c + 1) * W]).then_inc(a_out, 1)
                return
            act.wait_ge(a_ready, S * l + c + 1)
            nc.scalar.copy(agg[:, c % 2, :], aP[c % 2][:, 0:W]).then_inc(a_out, 1)

        def gate_act(act, l, c):
            act.wait_ge(g_ready, S * l + c + 1)
            act.wait_ge(x_new, S * l + c)
            nc.scalar.activation(rg[:, :], rP[:, 0:W], ACT.Sigmoid, bias=w["bsum"][:, 0:1]).then_inc(r_done, 1)
            nc.scalar.activation(zg[:, :], zP[:, 0:W], ACT.Sigmoid, bias=w["bsum"][:, 1:2]).then_inc(z_done, 1)
            act.wait_ge(hn_i, S * l + c + 1)
            nc.scalar.activation(ng[:, :], hn[:, :], ACT.Tanh, bias=w["bihc"][:, 2:3]).then_inc(n_done, 1)

        def gate_dve(dve, l, c):
            h = xT[:, c * W:(c + 1) * W]
            dve.wait_ge(r_done, S * l + c + 1)
            dve.wait_ge(n_done, S * l + c)
            dve.wait_ge(g_ready, S * l + c + 1)
            nc.vector.scalar_tensor_tensor(out=hn[:, :], in0=nP[:, 0:W], scalar=w["bhhc"][:, 2:3], in1=rg[:, :],
                                           op0=ALU.add, op1=ALU.mult).then_inc(hn_r, 1)
            dve.wait_ge(hn_r, S * l + c + 1)
            nc.vector.tensor_tensor(hn[:, :], iP[:, 0:W], hn[:, :], ALU.add).then_inc(hn_i, 1)
            dve.wait_ge(n_done, S * l + c + 1)
            nc.vector.tensor_tensor(rg[:, :], h, ng[:, :], ALU.subtract).then_inc(diff, 1)
            dve.wait_ge(diff, S * l + c + 1)
            nc.vector.tensor_tensor(rg[:, :], rg[:, :], zg[:, :], ALU.mult).then_inc(prod, 1)
            dve.wait_ge(prod, S * l + c + 1)
            nc.vector.tensor_tensor(h, rg[:, :], ng[:, :], ALU.add).then_inc(x_new, 1)

        def messages_pe(pe, l):
            pe.wait_ge(x_new, S * l)
            pe.wait_ge(lw_cut, l + 1)
            for c in range(S):
                pe.wait_ge(m_out, S * l + c)
                nc.tensor.matmul(mP[0][:, 0:W], lw_now[:, :],
                                 xT[:, c * W:(c + 1) * W], start=True, stop=True).then_inc(m_ready, 1)

        def messages_act(act, l):
            nc.scalar.copy(lw_now[:, :], lw[:, bass.ds(l, 1), :].rearrange("p a f -> p (a f)")).then_inc(lw_cut, 1)
            for c in range(S):
                act.wait_ge(m_ready, S * l + c + 1)
                nc.scalar.copy(mT[:, c * W:(c + 1) * W], mP[0][:, 0:W]).then_inc(m_out, 1)

        def pages_act(act, l):
            with act.Fori(0, pages) as i:
                act.wait_ge(edge_done, pl.E * l + page * i)
                page_in(act, pl, ends[:, 0, :], src, page * i).then_inc(page_here, 16)
                page_in(act, pl, ends[:, 1, :], dst, page * i).then_inc(page_here, 16)

        def sums_dve(dve, l):
            dve.wait_ge(m_out, S * l + S)
            nc.vector.memset(sumT[:, :], 0.0).then_inc(cleared, 1)
            with dve.Fori(0, pages) as i:
                dve.wait_ge(cleared, l + 1)
                dve.wait_ge(page_here, 32 * (pages * l + i) + 32)
                nc.vector.tensor_copy(spare, w["ones_row"][0:1, 0:1])
                with dve.Fori(0, page // U) as k:
                    s, d = ends_of(nc, pl, ends, U * k, U)
                    for u in range(U):
                        to = sumT[:, bass.ds(d[u], 1)]
                        dve.wait_ge(edge_done, pl.E * l + page * i + U * k + u)
                        nc.vector.tensor_tensor(to, to, mT[:, bass.ds(s[u], 1)], ALU.add).then_inc(edge_done, 1)

        def general_layers():
            with nc.Block() as block:
                @block.sync
                def _(sp):
                    sp.dma_start(lw[:, :, :], weight.rearrange("l p f -> p l f")).then_inc(lw_in, 16)

                @block.tensor
                def _(pe):
                    with pe.Fori(0, pl.L) as l:
                        messages_pe(pe, l)
                        for c in range(S):
                            gate_pe(pe, l, c)

                @block.scalar
                def _(act):
                    act.wait_ge(lw_in, 16)
                    with act.Fori(0, pl.L) as l:
                        messages_act(act, l)
                        pages_act(act, l)
                        agg_act(act, l, 0)
                        for c in range(1, S):
                            agg_act(act, l, c)
                            gate_act(act, l, c - 1)
                        gate_act(act, l, S - 1)

                @block.vector
                def _(dve):
                    with dve.Fori(0, pl.L) as l:
                        sums_dve(dve, l)
                        for c in range(S):
                            gate_dve(dve, l, c)

        early = G - 2
        assert chunk_of(early - 1) < S and chunk_of(early - 2) < S - 1
        half = 4 * (early - 1)

        def layer(engine, l, more, sums, cell, messages):
            if sums is agg_pe:
                agg_pe(engine, l, 0, range(half))
            for g in range(early, G):
                messages(engine, l, g)
            if sums is agg_pe:
                agg_pe(engine, l, 0, range(half, T))
            elif sums:
                sums(engine, l, 0)
            for c in range(1, S):
                if sums:
                    sums(engine, l, c)
                cell(engine, l, c - 1) if c < S - 1 else None
            if more:
                messages(engine, l + 1, 0)
                messages(engine, l + 1, 1)
            cell(engine, l, S - 2)
            if more:
                for g in range(2, early - 1):
                    messages(engine, l + 1, g)
            cell(engine, l, S - 1)
            if more:
                messages(engine, l + 1, early - 1)

        def fast_layers():
            with nc.Block() as block:
                @block.sync
                def _(sp):
                    sp.dma_start(lw[:, :, :], weight.rearrange("l p f -> p l f")).then_inc(lw_in, 16)

                @block.tensor
                def _(pe):
                    pe.wait_ge(lw_in, 16)
                    for g in range(early):
                        m_group_pe(pe, 0, g)
                    with pe.Fori(0, pl.L - 1) as l:
                        layer(pe, l, True, agg_pe, gate_pe, m_group_pe)
                    layer(pe, pl.L - 1, False, agg_pe, gate_pe, m_group_pe)

                @block.scalar
                def _(act):
                    for g in range(early):
                        m_group_act(act, 0, g)
                    with act.Fori(0, pl.L - 1) as l:
                        layer(act, l, True, agg_act, gate_act, m_group_act)
                    layer(act, pl.L - 1, False, agg_act, gate_act, m_group_act)

                @block.vector
                def _(dve):
                    for g in range(early):
                        m_group_dve(dve, 0, g)
                    with dve.Fori(0, pl.L - 1) as l:
                        layer(dve, l, True, None, gate_dve, m_group_dve)
                    layer(dve, pl.L - 1, False, None, gate_dve, m_group_dve)

        general_layers() if one_by_one else fast_layers()

    with ExitStack() as ctx:
        rx = ctx.enter_context(nc.sbuf_tensor(tag + "rx", [P, T, P], F32))
        r1 = ctx.enter_context(nc.sbuf_tensor(tag + "r1", [P, 3, 4, P], F32))
        tP = [ctx.enter_context(nc.psum_tensor(tag + f"tP2{i}", [P, 512], F32)) for i in range(2)]
        h2_in = kept_semaphore(nc, sems, "h2_in")
        x1_in = [kept_semaphore(nc, sems, f"x1_in{i}") for i in range(3)]
        turned = kept_semaphore(nc, sems, "x_turned")
        with_h2 = kept_semaphore(nc, sems, "with_h2")
        summed = kept_semaphore(nc, sems, "summed")
        stored = ctx.enter_context(nc.semaphore(tag + "stored"))
        full = pl.N // P

        def spans(g):
            a, b = 4 * g, min(4 * g + 4, T)
            k = min(b, full) - a
            found = [(P, 0, k, P * a)] if k > 0 else []
            if b > full:
                found.append((last, full - a, 1, P * full))
            return found

        def n_x1(g):
            return 16 * sum(len(spans(k)) for k in range(g % 3, g + 1, 3))

        with nc.Block() as block:
            @block.sync
            def _(sp):
                sp.dma_start(rx[:, 0:full, :], h2_dram[0:P * full, :].rearrange("(t p) f -> p t f", p=P)).then_inc(h2_in, 16)
                sp.dma_start(rx[0:last, full, :], h2_dram[P * full:pl.N, :]).then_inc(h2_in, 16)
                for g in range(G):
                    if g >= 3:
                        sp.wait_ge(summed, g - 2)
                    for n, s, k, node in spans(g):
                        d = x1_dram[node:node + n * k, :].rearrange("(t p) f -> p t f", p=n)
                        sp.dma_start(r1[0:n, g % 3, s:s + k, :], d).then_inc(x1_in[g % 3], 16)

            @block.gpsimd
            def _(pool):
                done = 0
                for g in range(G):
                    pool.wait_ge(summed, g + 1)
                    for n, s, k, node in spans(g):
                        d = out[node:node + n * k, :].rearrange("(t p) f -> p t f", p=n)
                        pool.dma_start(d, rx[0:n, 4 * g + s:4 * g + s + k, :]).then_inc(stored, 16)
                        done += 16
                pool.wait_ge(stored, done)

            @block.tensor
            def _(pe):
                for g in range(G):
                    if g >= 2:
                        pe.wait_ge(with_h2, g - 1)
                    for t in range(4 * g, min(4 * g + 4, T)):
                        mm = nc.tensor.transpose(tP[g % 2][:, (t - 4 * g) * P:(t - 4 * g + 1) * P],
                                                 xT[:, t * P:(t + 1) * P], w["ident"][:, :])
                    mm.then_inc(turned, 1)

            @block.vector
            def _(dve):
                dve.wait_ge(h2_in, 32)
                for g in range(G):
                    dve.wait_ge(turned, g + 1)
                    for n, s, k, node in spans(g):
                        r = rx[0:n, 4 * g + s:4 * g + s + k, :]
                        ins = nc.vector.tensor_tensor(r, tP[g % 2][0:n, s * P:(s + k) * P].rearrange("p (t f) -> p t f", f=P),
                                                      r, ALU.add)
                    ins.then_inc(with_h2, 1)
                    dve.wait_ge(with_h2, g + 1)
                    dve.wait_ge(x1_in[g % 3], n_x1(g))
                    for n, s, k, node in spans(g):
                        r = rx[0:n, 4 * g + s:4 * g + s + k, :]
                        ins = nc.vector.tensor_tensor(r, r, r1[0:n, g % 3, s:s + k, :], ALU.add)
                    ins.then_inc(summed, 1)


_INS = ['x', 'src', 'dst', 'edge_weight', 'L0_gnn_w1', 'L0_gnn_b1', 'L0_gnn_w2', 'L0_gnn_b2', 'L0_gnn_eps',
        'L1_gnn_weight', 'L1_gnn_w_ih', 'L1_gnn_w_hh', 'L1_gnn_b_ih', 'L1_gnn_b_hh']


def kernel(**inputs):
    import numpy as _np
    import concourse.bacc as _bacc
    from concourse import mybir as _mybir
    from concourse.bass_utils import run_bass_kernel_spmd as _run

    nc = _bacc.Bacc("TRN2", target_bir_lowering=False, num_devices=1)
    arrays, args = {}, []
    for name in _INS:
        a = _np.ascontiguousarray(inputs[name])
        arrays[f"in_{name}_dram"] = a
        args.append(nc.dram_tensor(f"in_{name}_dram", a.shape, _mybir.dt.from_np(a.dtype), kind="ExternalInput").ap())
    shape = tuple(inputs['x'].shape)
    args.append(nc.dram_tensor("out_0_dram", shape, _mybir.dt.float32, kind="ExternalOutput").ap())
    gnn_kernel(nc, *args)
    r = _run(nc, [arrays], core_ids=[0])
    return r.results[0]["out_0_dram"]
```

```python
from contextlib import ExitStack

import concourse.bass as bass
from concourse import mybir

P = 128
ALU = mybir.AluOpType
ACT = mybir.ActivationFunctionType
F32 = mybir.dt.float32
BF16 = mybir.dt.bfloat16
FP16 = mybir.dt.float16
I32 = mybir.dt.int32

NEG_INIT = -1.0e9
LEAKY = 0.01
LN_EPS = 1.0e-5
FAR = 8192.0
PAD_DST = 4095
RESET = -(2.0 ** 120)
WIN = 20
DEPTH = 4


class Plan:

    def __init__(self, nodes, feat, edges, layers):
        self.N, self.E, self.L = nodes, edges, layers
        assert feat == P
        self.tiles = -(-nodes // P)
        self.last = nodes - P * (self.tiles - 1)
        self.chunks = -(-edges // 512)
        self.chunks += -self.chunks % DEPTH
        assert self.chunks <= P and nodes <= PAD_DST
        self.run = 4 * self.chunks
        self.slots = P * self.run
        self.cols = P * self.tiles
        self.acols = nodes + WIN - 1
        self.groups = -(-self.tiles // 4)
        self.steps = 7
        self.width = self.cols // self.steps // 64 * 64
        while self.width * self.steps < nodes:
            self.width += 64
        assert self.width <= 512 and self.width * self.steps <= self.acols


def gnn_kernel(nc, x, src, dst, edge_weight, w1, b1, w2, b2, eps, weight, w_ih, w_hh, b_ih, b_hh, out):
    N, F = x.shape
    pl = Plan(N, F, src.shape[0], weight.shape[0])
    h1_dram = nc.dram_tensor("h1_rows", (N, P), F32, kind="Internal").ap()
    x1_dram = nc.dram_tensor("x1_rows", (N, P), F32, kind="Internal").ap()
    h2_dram = nc.dram_tensor("h2_rows", (N, P), F32, kind="Internal").ap()
    run_dram = nc.dram_tensor("run_rows", (pl.slots + 1, P), F32, kind="Internal").ap()

    with ExitStack() as ctx:
        def sb(name, shape, dt, stack=ctx):
            return stack.enter_context(nc.sbuf_tensor(name, shape, dt))

        counts = sb("counts", [P, pl.tiles, pl.acols], BF16)
        w = dict(
            ident=sb("ident", [P, P], F32),
            w1T=sb("w1T", [P, P], F32),
            w2T=sb("w2T", [P, P], F32),
            wihT=sb("wihT", [P, 3, P], F32),
            whhT=sb("whhT", [P, 3, P], F32),
            b1c=sb("b1c", [P, 1], F32),
            bihc=sb("bihc", [P, 3], F32),
            bhhc=sb("bhhc", [P, 3], F32),
            bsum=sb("bsum", [P, 2], F32),
            b2row=sb("b2row", [1, P], F32),
            ones_row=sb("ones_row", [1, P], F32),
            eps1=sb("eps1", [P, 1], F32),
            row_of=sb("row_of", [P, pl.tiles], I32),
            odd=sb("odd", [1, 1], I32),
        )
        sems = {}
        edges(nc, pl, w, counts, x, src, dst, edge_weight, w1, b1, w2, b2, eps, weight, w_ih, w_hh, b_ih, b_hh,
              h1_dram, run_dram)
        xT = sb("xT", [P, pl.cols], F32)
        w["lw"] = sb("lw", [P, pl.L, P], F32)
        mlp(nc, pl, w, sems, xT, weight, x, h1_dram, run_dram, x1_dram, h2_dram)
        layers(nc, pl, w, sems, counts, xT, weight, x1_dram, h2_dram, out)
        odd = nc.values_load(w["odd"][0:1, 0:1], min_val=0, max_val=1,
                             skip_runtime_bounds_check_because="it is clamped to one when it is made")
        with nc.If(odd > 0):
            one_by_one = (src, dst, edge_weight)
            clear_semaphores(nc, sems)
            general_maxima(nc, pl, w, counts, one_by_one, h1_dram, run_dram)
            mlp(nc, pl, w, sems, xT, weight, x, h1_dram, run_dram, x1_dram, h2_dram, "general_")
            layers(nc, pl, w, sems, counts, xT, weight, x1_dram, h2_dram, out, "general_", one_by_one)


def edges(nc, pl, w, counts, x, src, dst, edge_weight, w1, b1, w2, b2, eps, weight, w_ih, w_hh, b_ih, b_hh,
          h1_dram, run_dram):
    R, T, last, RUN = pl.chunks, pl.tiles, pl.last, pl.run
    TW = T * WIN
    turns = R // DEPTH
    assert turns - 1 >= T
    whole_p = pl.E // RUN
    rest_p = pl.E - whole_p * RUN
    whole_r = pl.E // 512
    rest_r = pl.E - whole_r * 512
    GX = pl.groups

    with ExitStack() as ctx:
        def sb(name, shape, dt):
            return ctx.enter_context(nc.sbuf_tensor(name, shape, dt))

        def sem(name):
            return ctx.enter_context(nc.semaphore(name))

        def ps(name):
            return ctx.enter_context(nc.psum_tensor(name, [P, 512], F32))

        src_walk = sb("src_walk", [P, RUN], I32)
        w_walk = sb("w_walk", [P, RUN], F32)
        dstI_walk = sb("dstI_walk", [P, RUN], I32)
        dst_walk = sb("dst_walk", [P, RUN + 1], F32)
        before = sb("before", [P, 1], I32)
        beforeF = sb("beforeF", [P, 1], F32)
        hot_cnt_mem = sb("hot_cnt", [P, 4 * 512], BF16)
        hot_cnt = hot_cnt_mem[:, 0:4 * TW].rearrange("p (j n) -> p j n", j=4)
        dst_rows = hot_cnt_mem[:, 0:1024].bitcast(I32)
        src_rows = hot_cnt_mem[:, 1024:2048].bitcast(I32)
        hot_src = sb("hot_src", [P, 2, 4, P], BF16)
        src_now = sb("src_now", [P, 4 * DEPTH], F32)
        dloc = sb("dloc", [P, 512], F32)
        far = sb("far", [P, 512], F32)
        chain, carry, seam_mask = [far[:, i * P:(i + 1) * P] for i in range(3)]
        baseF = sb("baseF", [P, 2], F32)
        base = sb("base", [1, R, 2], I32)
        terms = sb("terms", [P, turns, 3, 4 * DEPTH], F32)
        now = sb("now", [P, 3, 4 * DEPTH], F32)
        iota_count = sb("iota_count", [P, TW], FP16)
        iota_src = sb("iota_src", [P, P], BF16)
        node = sb("node", [P, T], F32)
        tile0 = sb("tile0", [P, T], F32)
        walk0 = sb("walk0", [P, 1], F32)
        shiftm = sb("shiftm", [P, 2 * P], F32)
        lastn = sb("lastn", [P, T], F32)
        prevn = sb("prevn", [P, T], F32)
        ge = sb("ge", [P, P], F32)
        at_part = sb("at_part", [P, P], F32)
        dumped_walk = dstI_walk[:, 0:RUN // 2].bitcast(BF16)
        w_tmp = hot_cnt_mem[:, 0:2 * RUN].bitcast(F32)
        within_walk = sb("within_walk", [P, 1], F32)
        upto = sb("upto", [P, T + 1], F32)
        first_n = sb("first_n", [P, 1], F32)
        seam_row = sb("seam_row", [P, 1], I32)
        seam = sb("seam", [P, 2], F32)
        seam_tmp = sb("seam_tmp", [P, 1], F32)
        zero_row = sb("zero_row", [1, P], F32)
        mv = sb("mv", [P, T, 2], F32)
        stats = sb("stats", [P, 4, 6], F32)
        rstd = sb("rstd", [P, T], F32)
        has = rstd
        shift = sb("shift", [P, T], F32)
        xs_run = sb("xs_run", [P, max(T, DEPTH * 4), P], F32)
        xs = xs_run
        runs_b = xs_run[:, 0:DEPTH * 4, :].rearrange("p (b j) f -> p b j f", b=DEPTH)
        rows = sb("rows", [P, DEPTH, 4, P], F32)
        idx = sb("idx", [P, DEPTH, 4], I32)
        w_now = sb("w_now", [P, 4 * DEPTH], F32)
        dumped_rows = terms.rearrange("p i s k -> p (i s k)")[:, 0:512]
        ones_col = sb("ones_col", [P, 1], F32)
        zero_col = sb("zero_col", [P, 1], BF16)
        odd_found = sb("odd_found", [P, 4], F32)

        wraw = counts[:, 0, 0:512].bitcast(F32)
        graw = counts[:, 1, 0:1536].bitcast(F32)

        countP = [ps(f"countP{i}") for i in range(2)]
        nodeP = ps("nodeP")
        termP = [ps(f"termP{i}") for i in range(2)]
        weightP = [ps(f"weightP{i}") for i in range(3)]

        x_in = [sem(f"x_in{i}") for i in range(GX)]
        padded = sem("padded")
        dstw_in = sem("dstw_in")
        rows_in = sem("rows_in")
        srcw_in = sem("srcw_in")
        w_in = sem("w_in")
        small_in = sem("small_in")
        zero_out = sem("zero_out")
        consts = sem("consts")
        ln_step = sem("ln_step")
        rooted = sem("rooted")
        var_ready = sem("var_ready")
        scale_ready = sem("scale_ready")
        normed = sem("normed")
        h1_out = sem("h1_out")
        edge_step = sem("edge_step")
        based = sem("based")
        terms_turned = sem("terms_turned")
        terms_out = sem("terms_out")
        w_turned = sem("w_turned")
        w_done = sem("w_done")
        zeroed = sem("zeroed")
        gathered = [sem(f"gathered{i}") for i in range(DEPTH)]
        idx_ready = sem("idx_ready")
        w_now_ready = sem("w_now_ready")
        chunk_begun = sem("chunk_begun")
        scaled = sem("scaled")
        maxed = sem("maxed")
        stored = [sem(f"stored{i}") for i in range(DEPTH)]
        hot_ready = sem("hot_ready")
        cnt_ready = sem("cnt_ready")
        cnt_added = sem("cnt_added")
        part_ready = sem("part_ready")
        node_ready = sem("node_ready")
        node_done = sem("node_done")
        small_set = sem("small_set")
        zero_set = sem("zero_set")
        first_zeroed = sem("first_zeroed")
        zeros_copied = sem("zeros_copied")
        src_now_ready = sem("src_now_ready")
        abs_done = sem("abs_done")
        src_ready = sem("src_ready")
        found = sem("found")
        odd_summed = sem("odd_summed")
        ge_done = sem("ge_done")
        counted = sem("counted")
        now_ready = sem("now_ready")
        seam_step = sem("seam_step")
        shifted = sem("shifted")
        seam_spread = sem("seam_spread")
        last_turned = sem("last_turned")
        carry_ready = sem("carry_ready")
        carry_turned = sem("carry_turned")
        seam_in = sem("seam_in")
        seam_done = sem("seam_done")
        seam_out = sem("seam_out")

        first_tiles, pool_tiles, dve_tiles = slice(2, 4), slice(4, 10), slice(22, T)
        copied_early, copied_late = range(10, 12), range(12, 17)
        act_early, act_late = range(17, 19), range(19, 22)

        block = ctx.enter_context(nc.Block())

        def x_spans(g):
            a, b = 4 * g, min(4 * g + 4, T)
            k = b - a - (1 if b == T and last < P else 0)
            return ([(P, a, k)] if k else []) + ([(last, T - 1, 1)] if b == T and last < P else [])

        @block.sync
        def _(sp):
            for g in range(GX):
                for n, a, k in x_spans(g):
                    sp.dma_start(xs[0:n, a:a + k, :],
                                 x[P * a:P * a + n * k, :].rearrange("(t p) f -> p t f", p=n)).then_inc(x_in[g], 16)
            sp.dma_start(wraw[:, 0:P], w1).then_inc(w_in, 16)
            sp.dma_start(wraw[:, P:2 * P], w2).then_inc(w_in, 16)
            sp.dma_start(graw[:, 0:3 * P].rearrange("p (g f) -> p g f", g=3),
                         w_ih.rearrange("(g p) f -> p g f", p=P)).then_inc(w_in, 16)
            sp.dma_start(graw[:, 3 * P:6 * P].rearrange("p (g f) -> p g f", g=3),
                         w_hh.rearrange("(g p) f -> p g f", p=P)).then_inc(w_in, 16)
            def copy_zeros(ts):
                for t in ts:
                    sp.dma_start(counts[:, t, :], counts[:, first_tiles.start, :]).then_inc(zeros_copied, 16)
            sp.wait_ge(first_zeroed, 1)
            copy_zeros(copied_early)
            for g in range(GX):
                sp.wait_ge(normed, min(4 * g + 4, T))
                for n, a, k in x_spans(g):
                    sp.dma_start(h1_dram[P * a:P * a + n * k, :].rearrange("(t p) f -> p t f", p=n),
                                 xs[0:n, a:a + k, :]).then_inc(h1_out, 16)
            copy_zeros(copied_late)
            sp.dma_start(w["eps1"][:, :], eps.rearrange("(a b) -> a b", a=1).broadcast_to([P, 1])).then_inc(small_in, 16)
            sp.dma_start(w["b1c"][:, :], b1.rearrange("(p a) -> p a", a=1)).then_inc(small_in, 16)
            sp.dma_start(w["b2row"][:, :], b2.rearrange("(a p) -> a p", a=1)).then_inc(small_in, 16)
            for g in range(3):
                sp.dma_start(w["bihc"][:, g:g + 1], b_ih[g * P:(g + 1) * P].rearrange("(p a) -> p a", a=1)
                             ).then_inc(small_in, 16)
                sp.dma_start(w["bhhc"][:, g:g + 1], b_hh[g * P:(g + 1) * P].rearrange("(p a) -> p a", a=1)
                             ).then_inc(small_in, 16)
            sp.wait_ge(small_set, 1)
            sp.dma_start(run_dram[pl.slots:pl.slots + 1, :], zero_row[:, :]).then_inc(zero_out, 16)

            by_walk = run_dram[0:pl.slots, :].rearrange("(p k) f -> p k f", p=P)

            def step(c, u):
                b = u % DEPTH
                sp.wait_ge(maxed, 4 * c + 4)
                to = by_walk[:, 4 * c:4 * c + 4, :] if isinstance(c, int) else by_walk[:, bass.ds(4 * c, 4), :]
                sp.dma_start(to, runs_b[:, b, :, :]).then_inc(stored[b], 16)
            for c in range(DEPTH):
                step(c, c)
            with sp.Fori(1, turns) as i:
                for u in range(DEPTH):
                    step(DEPTH * i + u, u)
            for b in range(DEPTH):
                sp.wait_ge(stored[b], 16 * turns)
            sp.wait_ge(zero_out, 16)
            sp.wait_ge(small_in, 16 * 9)

        @block.gpsimd
        def _(pool):
            def gpi(tile, step, base, cm):
                return nc.gpsimd.iota(tile, pattern=[[step, tile.shape[-1]]], base=base, channel_multiplier=cm,
                                      allow_small_or_imprecise_dtypes=True)
            nc.gpsimd.memset(w["ident"][:, :], 0.0).then_inc(consts, 1)
            nc.gpsimd.memset(shiftm[:, :], 0.0).then_inc(consts, 1)
            pool.wait_ge(consts, 2)
            nc.gpsimd.affine_select(out=w["ident"][:, :], in_=w["ident"][:, :], compare_op=ALU.not_equal, fill=1.0,
                                    base=0, pattern=[[-1, P]], channel_multiplier=1).then_inc(consts, 1)
            nc.gpsimd.affine_select(out=shiftm[:, :], in_=shiftm[:, :], compare_op=ALU.not_equal, fill=1.0,
                                    base=1, pattern=[[-1, 2 * P]], channel_multiplier=1).then_inc(consts, 1)
            gpi(iota_count[:, :], 1, 0, 0).then_inc(consts, 1)
            gpi(iota_src[:, :], 1, 0, 0).then_inc(consts, 1)
            gpi(node[:, :], P, 0, 1).then_inc(consts, 1)
            gpi(tile0[:, :], P, 0, 0).then_inc(consts, 1)
            gpi(walk0[:, :], 1, 0, RUN).then_inc(consts, 1)
            nc.gpsimd.memset(counts[:, first_tiles, :], 0.0).then_inc(first_zeroed, 1)
            nc.gpsimd.memset(counts[:, pool_tiles, :], 0.0).then_inc(zeroed, 1)

            n_out = sum(len(x_spans(g)) for g in range(GX))
            pool.wait_ge(h1_out, 16 * n_out)

            def step(c, u):
                b = u % DEPTH
                if u >= DEPTH:
                    pool.wait_ge(maxed, 4 * c + 4 - 4 * DEPTH)
                pool.wait_ge(idx_ready, c + 1)
                pool.sem_inc(chunk_begun, 1)
                for j in range(4):
                    pool.indirect_dma_start(out=rows[:, b, j, :], out_offset=None, in_=h1_dram,
                                            in_offset=bass.IndirectOffsetOnAxis(ap=idx[:, b, j:j + 1], axis=0)
                                            ).then_inc(gathered[b], 16)
            pool.wait_ge(consts, 9)
            for c in range(DEPTH):
                step(c, c)
            with pool.Fori(1, turns) as i:
                for u in range(DEPTH):
                    step(DEPTH * i + u, u + DEPTH)

            for b in range(DEPTH):
                pool.wait_ge(stored[b], 16 * turns)
            pool.indirect_dma_start(out=rows[:, 0, 0, :], out_offset=None, in_=run_dram,
                                    in_offset=bass.IndirectOffsetOnAxis(ap=seam_row[:, 0:1], axis=0)
                                    ).then_inc(seam_in, 16)
            pool.wait_ge(seam_done, 1)
            pool.indirect_dma_start(out=run_dram, out_offset=bass.IndirectOffsetOnAxis(ap=seam_row[:, 0:1], axis=0),
                                    in_=rows[:, 0, 1, :], in_offset=None).then_inc(seam_out, 16)
            pool.wait_ge(seam_out, 16)

        @block.scalar
        def _(act):
            def load_rows(tile, dram):
                act.wait_ge(padded, 6)
                act.dma_start(tile[0:whole_r, :], dram[0:512 * whole_r].rearrange("(r i) -> r i", i=512)
                              ).then_inc(rows_in, 16)
                act.dma_start(tile[whole_r:whole_r + 1, 0:rest_r], dram[512 * whole_r:pl.E].rearrange("(r i) -> r i", r=1)
                              ).then_inc(rows_in, 16)

            def load_walk(tile, dram, s, n_set):
                act.wait_ge(padded, n_set)
                act.dma_start(tile[0:whole_p, :], dram[0:whole_p * RUN].rearrange("(p k) -> p k", k=RUN)
                              ).then_inc(s, 16)
                act.dma_start(tile[whole_p:whole_p + 1, 0:rest_p],
                              dram[whole_p * RUN:pl.E].rearrange("(p k) -> p k", p=1)).then_inc(s, 16)

            def load_before():
                act.wait_ge(padded, 2)
                act.dma_start(before[1:P, :], dst[0:(P - 1) * RUN].rearrange("(p k) -> p k", k=RUN)[:, RUN - 1:RUN],
                              allow_slow_non_contiguous=True).then_inc(dstw_in, 16)

            def clear(tiles_):
                act.wait_ge(zero_set, 1)
                for t in tiles_:
                    nc.scalar.copy(counts[:, t, :], zero_col[:, 0:1].broadcast_to([P, pl.acols])).then_inc(zeroed, 1)

            def roots(g):
                a, b = 4 * g, min(4 * g + 4, T)
                act.wait_ge(var_ready, g + 1)
                nc.scalar.activation(rstd[:, a:b], mv[:, a:b, 1], ACT.Sqrt).then_inc(rooted, 1)

            def normalise(g):
                act.wait_ge(scale_ready, g + 1)
                for t in range(4 * g, min(4 * g + 4, T)):
                    n = P if t < T - 1 else last
                    nc.scalar.activation(xs[0:n, t, :], xs[0:n, t, :], ACT.Relu, bias=shift[0:n, t:t + 1],
                                         scale=rstd[0:n, t:t + 1]).then_inc(normed, 1)

            for g in range(GX):
                roots(g)
                if g:
                    normalise(g - 1)
                if g == 0:
                    load_rows(dst_rows, dst)
                if g == 1:
                    load_rows(src_rows, src)
                if g == 2:
                    load_walk(dstI_walk, dst, dstw_in, 1)
                if g == 3:
                    load_before()
                if g == 4:
                    load_walk(src_walk, src, srcw_in, 3)
                if g == 5:
                    load_walk(w_walk, edge_weight, srcw_in, 4)
            normalise(GX - 1)
            act.wait_ge(srcw_in, 64)
            for c in range(DEPTH):
                nc.scalar.copy(idx[:, c, :], src_walk[:, 4 * c:4 * c + 4]).then_inc(idx_ready, 1)
            clear(act_early)
            act.wait_ge(w_turned, 3)
            nc.scalar.copy(w["w1T"][:, :], weightP[0][:, 0:P]).then_inc(w_done, 1)
            nc.scalar.copy(w["w2T"][:, :], weightP[0][:, P:2 * P]).then_inc(w_done, 1)
            nc.scalar.copy(w["wihT"][:, :, :], weightP[1][:, 0:3 * P].rearrange("p (g f) -> p g f", g=3)).then_inc(w_done, 1)
            nc.scalar.copy(w["whhT"][:, :, :], weightP[2][:, 0:3 * P].rearrange("p (g f) -> p g f", g=3)).then_inc(w_done, 1)

            def weights(i):
                if not (isinstance(i, int) and i == 0):
                    act.wait_ge(scaled, DEPTH * i)
                nc.scalar.copy(w_now[:, :], w_walk[:, 4 * DEPTH * i:4 * DEPTH * (i + 1)] if isinstance(i, int) else
                               w_walk[:, bass.ds(4 * DEPTH * i, 4 * DEPTH)]).then_inc(w_now_ready, 1)
                act.wait_ge(w_now_ready, i + 1)

            def sources(i):
                if not (isinstance(i, int) and i == 0):
                    act.wait_ge(src_ready, DEPTH * i)
                nc.scalar.copy(src_now[:, :], terms[:, i, 0, :] if isinstance(i, int) else
                               terms[:, bass.ds(i, 1), 0, :].rearrange("p a k -> p (a k)")).then_inc(src_now_ready, 1)
                act.wait_ge(src_now_ready, i + 1)

            def hot_sources(c, u):
                if u >= 2:
                    act.wait_ge(cnt_ready, 2 * c - 2)
                for j in range(4):
                    ins = nc.scalar.activation(hot_src[:, u % 2, j, :], iota_src[:, :], ACT.Abs,
                                               bias=src_now[:, 4 * (u % DEPTH) + j:4 * (u % DEPTH) + j + 1])
                ins.then_inc(abs_done, 1)
                act.wait_ge(abs_done, c + 1)
                nc.scalar.activation(hot_src[:, u % 2, :, :], hot_src[:, u % 2, :, :], ACT.Relu,
                                     bias=ones_col[:, 0:1], scale=-1.0).then_inc(src_ready, 1)

            def step(c, u, more):
                b = u % DEPTH
                hot_sources(c, u)
                act.wait_ge(gathered[b], 16 * (c - b) + 64)
                if more:
                    k = 4 * (c + DEPTH)
                    nc.scalar.copy(idx[:, b, :], src_walk[:, k:k + 4] if isinstance(c, int) else
                                   src_walk[:, bass.ds(k, 4)]).then_inc(idx_ready, 1)
                for j in range(4):
                    ins = nc.scalar.activation(rows[:, b, j, :], rows[:, b, j, :], ACT.Copy,
                                               scale=w_now[:, 4 * b + j:4 * b + j + 1])
                ins.then_inc(scaled, 1)

            clear(act_late)
            act.wait_ge(terms_out, 3)
            act.wait_ge(consts, 9)
            act.wait_ge(small_set, 3)
            weights(0)
            sources(0)
            for c in range(DEPTH):
                step(c, c, True)
            with act.Fori(1, turns - 1) as i:
                weights(i)
                sources(i)
                for u in range(DEPTH):
                    step(DEPTH * i + u, u + DEPTH, True)
            weights(turns - 1)
            sources(turns - 1)
            for u in range(DEPTH):
                step(R - DEPTH + u, u + DEPTH, False)

        @block.tensor
        def _(pe):
            pe.wait_ge(consts, 9)
            pe.wait_ge(edge_step, 1)
            for j in range(2):
                mm = nc.tensor.matmul(nodeP[0:1, j * R:(j + 1) * R], baseF[0:R, j:j + 1],
                                      w["ident"][0:R, 0:R], start=True, stop=True)
            mm.then_inc(based, 1)
            pe.wait_ge(edge_step, 9)
            for i, frm in enumerate((far, dloc)):
                for j in range(4):
                    mm = nc.tensor.transpose(termP[i][:, j * R:(j + 1) * R], frm[0:R, j * P:(j + 1) * P],
                                             w["ident"][0:R, 0:R])
                mm.then_inc(terms_turned, 1)
            pe.wait_ge(w_in, 16 * 4)
            for i in range(2):
                mm = nc.tensor.transpose(weightP[0][:, i * P:(i + 1) * P], wraw[:, i * P:(i + 1) * P], w["ident"][:, :])
            mm.then_inc(w_turned, 1)
            for b in range(2):
                for i in range(3):
                    mm = nc.tensor.transpose(weightP[1 + b][:, i * P:(i + 1) * P],
                                             graw[:, (3 * b + i) * P:(3 * b + i + 1) * P], w["ident"][:, :])
                mm.then_inc(w_turned, 1)

            def step(c, u):
                for v in range(2):
                    pe.wait_ge(src_ready, c + 1)
                    pe.wait_ge(hot_ready, 2 * c + v + 1)
                    if u >= 1:
                        pe.wait_ge(cnt_added, 2 * c + v - 1)
                    for j in range(2):
                        mm = nc.tensor.matmul(countP[v][:, 0:TW], hot_src[:, u % 2, 2 * v + j, :],
                                              hot_cnt[:, 2 * v + j, :], start=(j == 0), stop=(j == 1))
                    mm.then_inc(cnt_ready, 1)

            def nodes_of_tile(t):
                pe.wait_ge(part_ready, t + 1)
                pe.wait_ge(node_done, t + 1)
                nc.tensor.matmul(nodeP[:, 0:RUN + 1], at_part[:, :], dst_walk[:, :], start=True, stop=True
                                 ).then_inc(node_ready, 1)

            for c in range(DEPTH):
                step(c, c)
            with pe.Fori(1, turns) as i:
                for u in range(DEPTH):
                    step(DEPTH * i + u, u + DEPTH)
                    if u == 0:
                        nodes_of_tile(i - 1)

            pe.wait_ge(found, 4)
            nc.tensor.matmul(countP[0][0:1, 0:4], ones_col[:, 0:1], odd_found[:, :], start=True, stop=True
                             ).then_inc(odd_summed, 1)
            pe.wait_ge(node_done, turns)
            nc.tensor.matmul(termP[0][:, 0:T], shiftm[:, 0:P], upto[:, 1:T + 1], start=True, stop=False)
            nc.tensor.matmul(termP[0][:, 0:T], shiftm[:, P:2 * P], upto[:, 0:T], start=False, stop=True
                             ).then_inc(shifted, 1)
            for i in range(2):
                mm = nc.tensor.matmul(termP[1][:, i * P:(i + 1) * P], seam[:, i:i + 1].broadcast_to([P, P]),
                                      w["ident"][:, :], start=True, stop=True)
            mm.then_inc(seam_spread, 1)
            pe.wait_ge(maxed, RUN)
            nc.tensor.transpose(weightP[0][:, 0:P], runs_b[:, DEPTH - 1, 3, :], w["ident"][:, :]).then_inc(last_turned, 1)
            pe.wait_ge(carry_ready, 2)
            nc.tensor.transpose(weightP[1][:, 0:P], carry[:, :], w["ident"][:, :]).then_inc(carry_turned, 1)

        @block.vector
        def _(dve):
            nc.vector.memset(zero_col[:, :], 0.0).then_inc(zero_set, 1)
            nc.vector.memset(dstI_walk[:, :], PAD_DST).then_inc(padded, 1)
            nc.vector.memset(before[:, :], -1).then_inc(padded, 1)
            nc.vector.memset(src_walk[:, :], 0).then_inc(padded, 1)
            nc.vector.memset(w_walk[:, :], 0.0).then_inc(padded, 1)
            nc.vector.memset(dst_rows[:, :], PAD_DST).then_inc(padded, 1)
            nc.vector.memset(src_rows[:, :], 0).then_inc(padded, 1)
            nc.vector.memset(zero_row[:, :], 0.0).then_inc(small_set, 1)
            nc.vector.memset(w["ones_row"][:, :], 1.0).then_inc(small_set, 1)
            nc.vector.memset(ones_col[:, :], 1.0).then_inc(small_set, 1)
            nc.vector.memset(upto[:, 0:1], 0.0).then_inc(node_done, 1)
            nc.vector.memset(mv[:, :, :], 1.0).then_inc(ln_step, 1)
            dve.wait_ge(ln_step, 1)
            done = [1]

            def ln_op(ins):
                ins.then_inc(ln_step, 1)
                done[0] += 1

            def statistics(g):
                ts = [(t, P if t < T - 1 else last) for t in range(4 * g, min(4 * g + 4, T))]
                dve.wait_ge(x_in[g], 16 * len(x_spans(g)))
                for t, n in ts:
                    ln_op(nc.vector.bn_stats(stats[0:n, t % 4, :], xs[0:n, t, :]))
                dve.wait_ge(ln_step, done[0])
                for t, n in ts:
                    ln_op(nc.vector.bn_aggr(mv[0:n, t, :], stats[0:n, t % 4, :]))
                dve.wait_ge(ln_step, done[0])
                a, b = 4 * g, min(4 * g + 4, T)
                nc.vector.tensor_scalar(mv[:, a:b, 1], mv[:, a:b, 1], LN_EPS, None, ALU.add).then_inc(var_ready, 1)

            def scales(g):
                a, b = 4 * g, min(4 * g + 4, T)
                dve.wait_ge(rooted, g + 1)
                ln_op(nc.vector.reciprocal(rstd[:, a:b], rstd[:, a:b]))
                dve.wait_ge(ln_step, done[0])
                nc.vector.scalar_tensor_tensor(out=shift[:, a:b], in0=mv[:, a:b, 0], scalar=-1.0, in1=rstd[:, a:b],
                                               op0=ALU.mult, op1=ALU.mult).then_inc(scale_ready, 1)

            for g in range(GX):
                statistics(g)
                if g:
                    scales(g - 1)
            scales(GX - 1)

            k = [0]

            def step_of(s, ins):
                k[0] += 1
                ins.then_inc(s, 1)
                dve.wait_ge(s, k[0])

            dve.wait_ge(rows_in, 64)
            step_of(edge_step, nc.vector.tensor_copy(baseF[:, :], dst_rows[:, 0:512:256]))
            for j in range(2):
                step_of(edge_step, nc.vector.tensor_scalar(dloc[:, 256 * j:256 * j + 256], dst_rows[:, 256 * j:256 * j + 256],
                                                      baseF[:, j:j + 1], None, ALU.subtract))
            step_of(edge_step, nc.vector.tensor_scalar(far[:, :], dloc[:, :], float(WIN), FAR, ALU.is_ge, ALU.mult))
            nc.vector.scalar_tensor_tensor(out=dumped_rows[:, :], in0=dst_rows[:, :], scalar=float(PAD_DST), in1=far[:, :],
                                           op0=ALU.is_lt, op1=ALU.mult, accum_out=odd_found[:, 0:1]).then_inc(found, 1)
            step_of(edge_step, nc.vector.tensor_tensor(dloc[:, :], dloc[:, :], far[:, :], ALU.add))
            dve.wait_ge(found, 1)
            step_of(edge_step, nc.vector.tensor_scalar(dst_rows[:, :], src_rows[:, :], P - 1, None, ALU.bitwise_and))
            step_of(edge_step, nc.vector.tensor_copy(far[:, :], dst_rows[:, :]))
            step_of(edge_step, nc.vector.tensor_scalar(src_rows[:, :], src_rows[:, :], 7, None, ALU.logical_shift_right))
            step_of(edge_step, nc.vector.scalar_tensor_tensor(out=dloc[:, :], in0=src_rows[:, :], scalar=float(WIN),
                                                         in1=dloc[:, :], op0=ALU.mult, op1=ALU.add))
            n_rows = k[0]
            dve.wait_ge(dstw_in, 48)
            dve.wait_ge(consts, 9)
            step_of(edge_step, nc.vector.tensor_copy(dst_walk[:, 0:RUN], dstI_walk[:, :]))
            nc.vector.tensor_copy(dst_walk[:, RUN:RUN + 1], walk0[:, :])
            nc.vector.memset(w_tmp[:, 0:1], 1.0)
            step_of(edge_step, nc.vector.tensor_tensor(w_tmp[:, 1:RUN], dst_walk[:, 1:RUN], dst_walk[:, 0:RUN - 1],
                                                  ALU.not_equal))
            step_of(edge_step, nc.vector.tensor_scalar(terms[:, :, 2, :], w_tmp.rearrange("p (i k) -> p i k", i=turns),
                                                  RESET, None, ALU.mult))
            step_of(edge_step, nc.vector.tensor_copy(beforeF[:, :], before[:, :]))
            nc.vector.tensor_scalar(lastn[:, :], tile0[:, :], -1.0, dst_walk[:, RUN - 1:RUN], ALU.mult, ALU.add)
            nc.vector.tensor_scalar(prevn[:, :], tile0[:, :], -1.0, beforeF[:, 0:1], ALU.mult, ALU.add)
            step_of(edge_step, nc.vector.tensor_scalar(dumped_walk[:, :], dst_walk[:, 0:RUN], dst_walk[:, 0:1], 0.0, ALU.is_equal,
                                                  ALU.add, accum_out=first_n[:, 0:1]))
            step_of(edge_step, nc.vector.tensor_tensor(seam_tmp[:, :], first_n[:, :], walk0[:, :], ALU.add))
            step_of(edge_step, nc.vector.tensor_scalar(seam_row[:, :], seam_tmp[:, :], -1.0, None, ALU.add))
            step_of(edge_step, nc.vector.tensor_tensor(seam[:, 1:2], beforeF[:, :], dst_walk[:, 0:1], ALU.not_equal))
            step_of(edge_step, nc.vector.tensor_tensor(seam_tmp[:, :], dst_walk[:, RUN - 1:RUN], dst_walk[:, 0:1], ALU.not_equal))
            step_of(edge_step, nc.vector.tensor_tensor(seam_tmp[:, :], seam_tmp[:, :], seam[:, 1:2], ALU.max))
            step_of(edge_step, nc.vector.tensor_scalar(seam[:, 0:1], seam_tmp[:, :], RESET, None, ALU.mult))
            step_of(edge_step, nc.vector.tensor_scalar(seam[:, 1:2], seam[:, 1:2], RESET, None, ALU.mult))

            dve.wait_ge(based, 1)
            nc.vector.tensor_scalar(base[:, :, :], nodeP[0:1, 0:2 * R].rearrange("p (j c) -> p c j", j=2),
                                    0.0, float(pl.N - 1), ALU.max, ALU.min).then_inc(terms_out, 1)
            for i in range(2):
                dve.wait_ge(terms_turned, 1 + i)
                nc.vector.tensor_scalar(terms[:, :, i, :].rearrange("p i (d j) -> p i d j", j=4),
                                        termP[i][:, 0:4 * R].rearrange("p (j i d) -> p i d j", j=4, d=DEPTH),
                                        (-1.0, 1.0)[i], None, ALU.mult).then_inc(terms_out, 1)
            dve.wait_ge(w_turned, 3)
            nc.vector.memset(counts[:, 0:2, :], 0.0).then_inc(zeroed, 1)
            nc.vector.memset(counts[:, dve_tiles, :], 0.0).then_inc(zeroed, 1)
            dve.wait_ge(small_in, 16 * 9)
            nc.vector.tensor_tensor(w["bsum"][:, :], w["bihc"][:, 0:2], w["bhhc"][:, 0:2], ALU.add).then_inc(small_set, 1)
            nc.vector.tensor_scalar(w["eps1"][:, :], w["eps1"][:, :], 1.0, None, ALU.add).then_inc(small_set, 1)
            dve.wait_ge(terms_out, 3)
            dve.wait_ge(zeroed, 3 + len(act_early) + len(act_late))
            dve.wait_ge(first_zeroed, 1)
            dve.wait_ge(zeros_copied, 16 * (len(copied_early) + len(copied_late)))

            def bases(c):
                row = base[0:1, c, :] if isinstance(c, int) else \
                    base[0:1, bass.ds(c, 1), :].rearrange("p c v -> p (c v)")
                _, vals = nc.values_load_multi_w_load_instructions(
                    row, engines=[mybir.EngineType.DVE], min_val=0, max_val=pl.N - 1,
                    skip_runtime_bounds_check_because="the bases are clamped to the nodes when they are made")
                return vals

            def not_before(t):
                dve.wait_ge(node_done, t + 1)
                nc.vector.tensor_scalar(ge[:, :], iota_src[:, :], prevn[:, bass.ds(t, 1)], None, ALU.is_ge
                                        ).then_inc(ge_done, 1)

            def part_of_tile(t):
                dve.wait_ge(ge_done, t + 1)
                nc.vector.scalar_tensor_tensor(out=at_part[:, :], in0=iota_src[:, :], scalar=lastn[:, bass.ds(t, 1)],
                                               in1=ge[:, :], op0=ALU.is_lt, op1=ALU.mult).then_inc(part_ready, 1)

            def count_of_tile(t):
                dve.wait_ge(node_ready, t + 1)
                nc.vector.tensor_scalar(dumped_walk[:, :], nodeP[:, 0:RUN], node[:, bass.ds(t, 1)], 0.0, ALU.is_le, ALU.add,
                                        accum_out=within_walk[:, 0:1]).then_inc(counted, 1)

            def edges_up_to(t):
                dve.wait_ge(counted, t + 1)
                nc.vector.tensor_tensor(upto[:, bass.ds(t + 1, 1)], nodeP[:, RUN:RUN + 1], within_walk[:, 0:1], ALU.add
                                        ).then_inc(node_done, 1)

            def turn(i, first):
                src_i = terms[:, i, :, :] if isinstance(i, int) else \
                    terms[:, bass.ds(i, 1), :, :].rearrange("p a s k -> p (a s) k")
                if not first:
                    dve.wait_ge(maxed, 4 * DEPTH * i)
                    dve.wait_ge(hot_ready, 2 * DEPTH * i)
                nc.vector.tensor_copy(now[:, :, :], src_i).then_inc(now_ready, 1)
                if not first:
                    not_before(i - 1)
                dve.wait_ge(now_ready, i + 1)
                for u in range(DEPTH):
                    c = DEPTH * i + u

                    def hot(j):
                        k = 4 * u + j
                        ins = nc.vector.tensor_scalar(hot_cnt[:, j, :], iota_count[:, :], now[:, 1, k:k + 1], None,
                                                      ALU.is_equal)
                        if j % 2:
                            ins.then_inc(hot_ready, 1)

                    def maximum(j):
                        if first and u == 0 and j == 0:
                            nc.vector.tensor_copy(runs_b[:, 0, 0, :], rows[:, 0, 0, :]).then_inc(maxed, 1)
                            return
                        pu, pj = (u, j - 1) if j else ((u - 1) % DEPTH, 3)
                        dve.wait_ge(maxed, 4 * c + j)
                        nc.vector.scalar_tensor_tensor(out=runs_b[:, u, j, :], in0=runs_b[:, pu, pj, :],
                                                       scalar=now[:, 2, 4 * u + j:4 * u + j + 1],
                                                       in1=rows[:, u, j, :], op0=ALU.add, op1=ALU.max
                                                       ).then_inc(maxed, 1)

                    def add_counts(v):
                        dve.wait_ge(cnt_ready, 2 * c + v + 1)
                        if not (first and u + v == 0):
                            dve.wait_ge(cnt_added, 2 * c + v)
                        win = counts[:, :, bass.ds(at[v], WIN)]
                        nc.vector.tensor_tensor(win, countP[v][:, 0:TW].rearrange("p (t d) -> p t d", d=WIN), win,
                                                ALU.add).then_inc(cnt_added, 1)

                    hot(0)
                    hot(1)
                    if not first and u == 0:
                        part_of_tile(i - 1)
                    at = bases(c)
                    dve.wait_ge(scaled, c + 1)
                    if first:
                        dve.wait_ge(h1_out, 16 * sum(len(x_spans(g)) for g in range(GX)))
                    else:
                        dve.wait_ge(stored[u], 16 * i)
                    maximum(0)
                    hot(2)
                    maximum(1)
                    hot(3)
                    maximum(2)
                    add_counts(0)
                    maximum(3)
                    if not first and u == 2:
                        edges_up_to(i - 1)
                    add_counts(1)
                    if not first and u == 1:
                        count_of_tile(i - 1)

            turn(0, True)
            with dve.Fori(1, turns) as i:
                turn(i, False)
            assert pl.slots - pl.E <= P
            nc.vector.scalar_tensor_tensor(out=dumped_walk[:, 1:RUN], in0=dst_walk[:, 0:RUN - 1], scalar=0.0,
                                           in1=dst_walk[:, 1:RUN], op0=ALU.add, op1=ALU.is_gt,
                                           accum_out=odd_found[:, 1:2]).then_inc(found, 1)
            dve.wait_ge(found, 2)
            nc.vector.scalar_tensor_tensor(out=dumped_walk[:, P:RUN], in0=dst_walk[:, 0:RUN - P], scalar=0.0,
                                           in1=dst_walk[:, P:RUN], op0=ALU.add, op1=ALU.is_equal,
                                           accum_out=odd_found[:, 2:3]).then_inc(found, 1)
            nc.vector.tensor_tensor(odd_found[:, 3:4], beforeF[:, :], dst_walk[:, 0:1], ALU.is_gt).then_inc(found, 1)

            dve.wait_ge(seam_spread, 1)
            nc.vector.tensor_copy(seam_mask[:, :], termP[1][:, 0:P]).then_inc(seam_step, 1)
            dve.wait_ge(last_turned, 1)
            dve.wait_ge(seam_step, 1)
            nc.vector.tensor_tensor_scan(chain[:, :], seam_mask[:, :], weightP[0][:, 0:P], 0.0, ALU.add, ALU.max
                                         ).then_inc(seam_step, 1)
            dve.wait_ge(seam_step, 2)
            nc.vector.memset(carry[:, 0:1], RESET).then_inc(carry_ready, 1)
            nc.vector.tensor_tensor(carry[:, 1:P], chain[:, 0:P - 1], termP[1][:, P + 1:2 * P], ALU.add
                                    ).then_inc(carry_ready, 1)
            dve.wait_ge(shifted, 1)
            dve.wait_ge(node_done, turns)
            nc.vector.tensor_tensor(has[:, :], upto[:, 1:T + 1], termP[0][:, 0:T], ALU.is_gt).then_inc(seam_step, 1)
            dve.wait_ge(seam_step, 3)
            nc.vector.scalar_tensor_tensor(out=has[:, :], in0=upto[:, 1:T + 1], scalar=float(-1 - pl.slots),
                                           in1=has[:, :], op0=ALU.add, op1=ALU.mult).then_inc(seam_step, 1)
            dve.wait_ge(seam_step, 4)
            nc.vector.tensor_scalar(w["row_of"][:, :], has[:, :], float(pl.slots), float(pl.slots), ALU.add, ALU.min
                                    ).then_inc(seam_step, 1)
            dve.wait_ge(odd_summed, 1)
            dve.wait_ge(now_ready, turns)
            nc.vector.tensor_reduce(odd_found[0:1, 0:1], countP[0][0:1, 0:4], mybir.AxisListType.X, ALU.add
                                    ).then_inc(found, 1)
            dve.wait_ge(found, 5)
            nc.vector.tensor_scalar(w["odd"][:, :], odd_found[0:1, 0:1], 1.0, None, ALU.min).then_inc(found, 1)
            dve.wait_ge(seam_in, 16)
            dve.wait_ge(carry_turned, 1)
            nc.vector.tensor_tensor(rows[:, 0, 1, :], weightP[1][:, 0:P], rows[:, 0, 0, :], ALU.max).then_inc(seam_done, 1)


def mlp(nc, pl, w, sems, xT, weight, x, h1_dram, run_dram, x1_dram, h2_dram, tag=""):
    T, last = pl.tiles, pl.last
    G = pl.groups
    with ExitStack() as ctx:
        def sb(name, shape, dt):
            return ctx.enter_context(nc.sbuf_tensor(tag + name, shape, dt))

        def sem(name):
            return kept_semaphore(nc, sems, name)

        def ps(name):
            return ctx.enter_context(nc.psum_tensor(tag + name, [P, 512], F32))

        h1 = sb("h1", [P, 3, 4, P], F32)
        agg = sb("agg_rows", [P, 3, 4, P], F32)
        xr = sb("xr", [P, 3, 4, P], F32)
        u_in = sb("u_in", [P, 2, 512], F32)
        act1 = sb("act1", [P, 2, 512], F32)
        h2 = sb("h2", [P, 3, 4, P], F32)
        stats = sb("stats2", [P, 4, 6], F32)
        mv = sb("mv2", [P, 4, 2], F32)
        rstd = sb("rstd2", [P, 4], F32)
        shift = sb("shift2", [P, 4], F32)
        hP = [ps(f"hP{i}") for i in range(2)]
        vP = [ps(f"vP{i}") for i in range(2)]
        oP = [ps(f"oP{i}") for i in range(2)]
        tP = [ps(f"tP{i}") for i in range(2)]

        h_in = [sem(f"h_in{i}") for i in range(3)]
        xr_in = [sem(f"xr_in{i}") for i in range(3)]
        agg_in = [ctx.enter_context(nc.semaphore(tag + f"agg_in{i}")) for i in range(3)]
        lw_in = sem("lw_in")
        u_rows = sem("u_rows")
        h_turned = sem("h_turned")
        aggfix = sem("aggfix")
        u_ready = sem("u_ready")
        v_ready = sem("v_ready")
        vb_ready = sem("vb_ready")
        leaky = sem("leaky")
        o_ready = sem("o_ready")
        x1_ready = sem("x1_ready")
        ln = sem("ln")
        root = sem("root")
        h2_ready = sem("h2_ready")
        rows_out = [sem(f"rows_out{i}") for i in range(3)]
        h2_turned = sem("h2_turned")
        xT_ready = sem("xT_ready")

        def tiles(g):
            return [(t, P if t < T - 1 else last) for t in range(4 * g, min(4 * g + 4, T))]

        def cols(g):
            a = 512 * g
            return a, min(512, pl.N - a)

        def move(eng, sb_tile, dram, g, to_dram, s):
            ts = tiles(g)
            fullt = [t for t, n in ts if n == P]
            n_dma = 0
            if fullt:
                a = fullt[0]
                k = len(fullt)
                d = dram[P * a:P * (a + k), :].rearrange("(t p) f -> p t f", p=P)
                s_ = sb_tile[:, 0:k, :]
                (eng.dma_start(d, s_) if to_dram else eng.dma_start(s_, d)).then_inc(s, 16)
                n_dma += 1
            if len(fullt) < len(ts):
                t, n = ts[-1]
                d = dram[P * t:P * t + n, :]
                s_ = sb_tile[0:n, t - 4 * g, :]
                (eng.dma_start(d, s_) if to_dram else eng.dma_start(s_, d)).then_inc(s, 16)
                n_dma += 1
            return n_dma

        def n_dmas(g):
            ns = [n for _, n in tiles(g)]
            return int(P in ns) + int(any(n < P for n in ns))

        def total(g, ring):
            return 16 * sum(n_dmas(k) for k in range(g % ring, g + 1, ring))

        block = ctx.enter_context(nc.Block())

        @block.sync
        def _(sp):
            def load_h1(g):
                if g >= 3:
                    sp.wait_ge(u_rows, g - 2)
                move(sp, h1[:, g % 3, :, :], h1_dram, g, False, h_in[g % 3])

            def load_x(g):
                if g >= 3:
                    sp.wait_ge(rows_out[g % 3], 2 * total(g - 3, 3))
                move(sp, xr[:, g % 3, :, :], x, g, False, xr_in[g % 3])
            load_h1(0)
            load_h1(1)
            sp.dma_start(w["lw"][:, :, :], weight.rearrange("l p f -> p l f")).then_inc(lw_in, 16)
            for g in range(G):
                if g + 2 < G:
                    load_h1(g + 2)
                load_x(g)

        @block.gpsimd
        def _(pool):
            for g in range(G):
                if g >= 3:
                    pool.wait_ge(h_turned, g - 2)
                for t, _ in tiles(g):
                    pool.indirect_dma_start(out=agg[:, g % 3, t - 4 * g, :], out_offset=None, in_=run_dram,
                                            in_offset=bass.IndirectOffsetOnAxis(ap=w["row_of"][:, t:t + 1], axis=0)
                                            ).then_inc(agg_in[g % 3], 16)

        def s1_pe(pe, g):
            pe.wait_ge(u_rows, g + 1)
            if g >= 2:
                pe.wait_ge(u_ready, g - 1)
            for t, n in tiles(g):
                j = t - 4 * g
                mm = nc.tensor.transpose(hP[g % 2][:, j * P:j * P + n], agg[0:n, g % 3, j, :], w["ident"][0:n, 0:n])
            mm.then_inc(h_turned, 1)

        def s2_pe(pe, g):
            a, n = cols(g)
            pe.wait_ge(u_ready, g + 1)
            if g >= 2:
                pe.wait_ge(vb_ready, g - 1)
            nc.tensor.matmul(vP[g % 2][:, 0:n], w["w1T"][:, :], u_in[:, g % 2, 0:n], start=True, stop=True
                             ).then_inc(v_ready, 1)

        def s3_pe(pe, g):
            pe.wait_ge(leaky, g + 1)
            if g >= 2:
                pe.wait_ge(x1_ready, g - 1)
            for t, n in tiles(g):
                j = t - 4 * g
                nc.tensor.matmul(oP[g % 2][0:n, j * P:(j + 1) * P], act1[:, g % 2, j * P:j * P + n], w["w2T"][:, :],
                                 start=True, stop=False)
                mm = nc.tensor.matmul(oP[g % 2][0:n, j * P:(j + 1) * P], w["ones_row"][0:1, 0:n], w["b2row"][0:1, :],
                                      start=False, stop=True)
            mm.then_inc(o_ready, 1)

        def s4_pe(pe, g):
            pe.wait_ge(h2_ready, g + 1)
            if g >= 2:
                pe.wait_ge(xT_ready, g - 1)
            for t, n in tiles(g):
                j = t - 4 * g
                mm = nc.tensor.transpose(tP[g % 2][:, j * P:j * P + n], h2[0:n, g % 3, j, :], w["ident"][0:n, 0:n])
            mm.then_inc(h2_turned, 1)

        def s1_dve(dve, g):
            ts = tiles(g)
            k = len(ts)
            dve.wait_ge(agg_in[g % 3], 16 * sum(len(tiles(i)) for i in range(g % 3, g + 1, 3)))
            nc.vector.scalar_tensor_tensor(out=agg[:, g % 3, 0:k, :], in0=agg[:, g % 3, 0:k, :], scalar=NEG_INIT,
                                           in1=agg[:, g % 3, 0:k, :], op0=ALU.is_gt, op1=ALU.mult).then_inc(aggfix, 1)
            dve.wait_ge(aggfix, g + 1)
            dve.wait_ge(h_in[g % 3], total(g, 3))
            m = min(n for _, n in ts)
            nc.vector.scalar_tensor_tensor(out=agg[0:m, g % 3, 0:k, :], in0=h1[0:m, g % 3, 0:k, :],
                                           scalar=w["eps1"][0:m, 0:1], in1=agg[0:m, g % 3, 0:k, :], op0=ALU.mult,
                                           op1=ALU.add).then_inc(u_rows, 1)

        def s1_act(act, g):
            a, n = cols(g)
            act.wait_ge(h_turned, g + 1)
            if g >= 2:
                act.wait_ge(v_ready, g - 1)
            nc.scalar.copy(u_in[:, g % 2, 0:n], hP[g % 2][:, 0:n]).then_inc(u_ready, 1)

        def s2_act(act, g):
            a, n = cols(g)
            act.wait_ge(v_ready, g + 1)
            if g >= 2:
                act.wait_ge(o_ready, g - 1)
            nc.scalar.activation(act1[:, g % 2, 0:n], vP[g % 2][:, 0:n], ACT.Identity, bias=w["b1c"][:, 0:1]
                                 ).then_inc(vb_ready, 1)

        def s2_dve(dve, g):
            a, n = cols(g)
            dve.wait_ge(vb_ready, g + 1)
            v = act1[:, g % 2, 0:n]
            nc.vector.scalar_tensor_tensor(out=v, in0=v, scalar=LEAKY, in1=v,
                                           op0=ALU.mult, op1=ALU.max).then_inc(leaky, 1)

        lncount = [0]

        def s3_dve(dve, g):
            dve.wait_ge(o_ready, g + 1)
            dve.wait_ge(xr_in[g % 3], total(g, 3))
            ts = tiles(g)
            k = len([1 for _, n in ts if n == P])
            if k:
                nc_last = nc.vector.tensor_tensor(xr[:, g % 3, 0:k, :], oP[g % 2][:, 0:k * P].rearrange("p (j f) -> p j f", f=P),
                                                  xr[:, g % 3, 0:k, :], ALU.add)
                rows_ = P
            if k < len(ts):
                n = ts[-1][1]
                nc_last = nc.vector.tensor_tensor(xr[0:n, g % 3, k, :], oP[g % 2][0:n, k * P:(k + 1) * P],
                                                  xr[0:n, g % 3, k, :], ALU.add)
            nc_last.then_inc(x1_ready, 1)
            dve.wait_ge(x1_ready, g + 1)
            if g >= 1:
                dve.wait_ge(h2_ready, g)
            for t, n in ts:
                j = t - 4 * g
                ins = nc.vector.bn_stats(stats[0:n, j, :], xr[0:n, g % 3, j, :])
            ins.then_inc(ln, 1)
            lncount[0] += 1
            dve.wait_ge(ln, lncount[0])
            for t, n in ts:
                j = t - 4 * g
                ins = nc.vector.bn_aggr(mv[0:n, j, :], stats[0:n, j, :])
            ins.then_inc(ln, 1)
            lncount[0] += 1
            dve.wait_ge(ln, lncount[0])
            m, k = min(n for _, n in ts), len(ts)
            nc.vector.tensor_scalar(mv[0:m, 0:k, 1], mv[0:m, 0:k, 1], LN_EPS, None, ALU.add).then_inc(ln, 1)
            lncount[0] += 1

        def s3_dve_late(dve, g):
            ts = tiles(g)
            m, k = min(n for _, n in ts), len(ts)
            dve.wait_ge(root, g + 1)
            nc.vector.reciprocal(rstd[0:m, 0:k], rstd[0:m, 0:k]).then_inc(ln, 1)
            lncount[0] += 1
            dve.wait_ge(ln, lncount[0])
            nc.vector.scalar_tensor_tensor(out=shift[0:m, 0:k], in0=mv[0:m, 0:k, 0], scalar=-1.0, in1=rstd[0:m, 0:k],
                                           op0=ALU.mult, op1=ALU.mult).then_inc(ln, 1)
            lncount[0] += 1

        def s3_act(act, g):
            ts = tiles(g)
            m, k = min(n for _, n in ts), len(ts)
            act.wait_ge(x1_ready, g + 1)
            move(act, xr[:, g % 3, :, :], x1_dram, g, True, rows_out[g % 3])
            act.wait_ge(ln, 5 * g + 3)
            nc.scalar.activation(rstd[0:m, 0:k], mv[0:m, 0:k, 1], ACT.Sqrt).then_inc(root, 1)
            act.wait_ge(ln, 5 * g + 5)
            if g >= 3:
                act.wait_ge(rows_out[g % 3], 2 * total(g - 3, 3))
                act.wait_ge(h2_turned, g - 2)
            for t, n in ts:
                j = t - 4 * g
                ins = nc.scalar.activation(h2[0:n, g % 3, j, :], xr[0:n, g % 3, j, :], ACT.Relu,
                                           bias=shift[0:n, j:j + 1], scale=rstd[0:n, j:j + 1])
            ins.then_inc(h2_ready, 1)
            act.wait_ge(h2_ready, g + 1)
            move(act, h2[:, g % 3, :, :], h2_dram, g, True, rows_out[g % 3])

        def s4_act(act, g):
            a, n = cols(g)
            act.wait_ge(h2_turned, g + 1)
            nc.scalar.copy(xT[:, a:a + n], tP[g % 2][:, 0:n]).then_inc(xT_ready, 1)

        turns = G + 4

        @block.tensor
        def _(pe):
            for turn in range(turns):
                if turn - 3 in range(G):
                    s3_pe(pe, turn - 3)
                if turn - 2 in range(G):
                    s2_pe(pe, turn - 2)
                if turn - 1 in range(G):
                    s1_pe(pe, turn - 1)
                if turn - 4 in range(G):
                    s4_pe(pe, turn - 4)

        @block.vector
        def _(dve):
            nc.vector.memset(xT[:, pl.N:pl.cols], 0.0)
            for turn in range(turns):
                if turn - 3 in range(G):
                    s3_dve(dve, turn - 3)
                if turn - 2 in range(G):
                    s2_dve(dve, turn - 2)
                if turn - 3 in range(G):
                    s3_dve_late(dve, turn - 3)
                if turn in range(G):
                    s1_dve(dve, turn)

        @block.scalar
        def _(act):
            for turn in range(turns):
                if turn - 2 in range(G):
                    s2_act(act, turn - 2)
                if turn - 1 in range(G):
                    s1_act(act, turn - 1)
                if turn - 3 in range(G):
                    s3_act(act, turn - 3)
                if turn - 4 in range(G):
                    s4_act(act, turn - 4)
            for g in range(G - 3, G):
                act.wait_ge(rows_out[g % 3], 2 * total(g, 3))


def kept_semaphore(nc, sems, name):
    if name not in sems:
        sems[name] = nc.alloc_semaphore(name)
    return sems[name]


def clear_semaphores(nc, sems):
    todo = list(sems.values())

    def share(engine, k):
        for s in todo[k::5]:
            engine.sem_clear(s)

    with nc.Block() as block:
        @block.sync
        def _(sp):
            share(sp, 0)

        @block.gpsimd
        def _(pool):
            share(pool, 1)

        @block.scalar
        def _(act):
            share(act, 2)

        @block.vector
        def _(dve):
            share(dve, 3)

        @block.tensor
        def _(pe):
            share(pe, 4)


def as_columns(pl, counts, i):
    return counts.rearrange("p t c -> p (t c)")[:, 2 * pl.cols * i:2 * pl.cols * (i + 1)].bitcast(F32)


def edge_pages(pl):
    page = max(k for k in range(1, 1025) if pl.E % k == 0)
    return pl.E // page, page, max(k for k in range(1, 6) if page % k == 0)


def page_in(act, pl, tile, dram, at):
    n, page = tile.shape
    return act.dma_start(tile, dram[bass.ds(at, page)].rearrange("(a k) -> a k", a=1).broadcast_to([n, page]))


def general_maxima(nc, pl, w, counts, one_by_one, h1_dram, run_dram):
    src, dst, edge_weight = one_by_one
    T, last = pl.tiles, pl.last
    pages, page, U = edge_pages(pl)
    with ExitStack() as ctx:
        def sb(name, shape, dt):
            return ctx.enter_context(nc.sbuf_tensor(name, shape, dt))

        def sem(name):
            return ctx.enter_context(nc.semaphore(name))

        h1T, aggT = as_columns(pl, counts, 0), as_columns(pl, counts, 1)
        row = sb("row", [P, P], F32)
        tile_cols = sb("tile_cols", [P, P], F32)
        ends = sb("ends", [1, 2, page], I32)
        wpage = sb("wpage", [P, page], F32)
        colP = ctx.enter_context(nc.psum_tensor("colP", [P, 512], F32))
        row_in = sem("row_in")
        row_turned = sem("row_turned")
        row_used = sem("row_used")
        row_out = sem("row_out")
        page_here = sem("page_here")
        cut = sem("cut")
        edge_done = sem("edge_done")
        named = sem("named")

        with nc.Block() as block:
            @block.sync
            def _(sp):
                def load(t, n, node):
                    if not (isinstance(t, int) and t == 0):
                        sp.wait_ge(row_turned, t)
                    sp.dma_start(row[0:n, :], h1_dram[node, :]).then_inc(row_in, 16)

                def store(t, n, node):
                    sp.wait_ge(row_used, T + t + 1)
                    sp.dma_start(run_dram[node, :], row[0:n, :]).then_inc(row_out, 16)
                load(0, P, slice(0, P))
                with sp.Fori(1, T - 1) as t:
                    load(t, P, bass.ds(P * t, P))
                load(T - 1, last, slice(P * (T - 1), pl.N))
                with sp.Fori(0, T - 1) as t:
                    store(t, P, bass.ds(P * t, P))
                store(T - 1, last, slice(P * (T - 1), pl.N))
                sp.wait_ge(row_out, 16 * T)

            @block.scalar
            def _(act):
                with act.Fori(0, pages) as i:
                    act.wait_ge(edge_done, page * i + 1)
                    page_in(act, pl, ends[:, 0, :], src, page * i).then_inc(page_here, 16)
                    page_in(act, pl, ends[:, 1, :], dst, page * i).then_inc(page_here, 16)
                    page_in(act, pl, wpage[:, :], edge_weight, page * i).then_inc(page_here, 16)

            @block.gpsimd
            def _(pool):
                nc.gpsimd.iota(w["row_of"][:, :], pattern=[[P, T]], base=0, channel_multiplier=1).then_inc(named, 1)

            @block.tensor
            def _(pe):
                def rows_to_columns(t, n):
                    pe.wait_ge(row_in, 16 * t + 16)
                    if not (isinstance(t, int) and t == 0):
                        pe.wait_ge(row_used, t)
                    nc.tensor.transpose(colP[:, 0:n], row[0:n, :], w["ident"][0:n, 0:n]).then_inc(row_turned, 1)

                def columns_to_rows(t):
                    pe.wait_ge(cut, t + 1)
                    nc.tensor.transpose(colP[:, 0:P], tile_cols[:, :], w["ident"][:, :]).then_inc(row_turned, 1)
                rows_to_columns(0, P)
                with pe.Fori(1, T - 1) as t:
                    rows_to_columns(t, P)
                rows_to_columns(T - 1, last)
                with pe.Fori(0, T) as t:
                    columns_to_rows(t)

            @block.vector
            def _(dve):
                def out_of_psum(t, n):
                    dve.wait_ge(row_turned, t + 1)
                    nc.vector.tensor_copy(h1T[:, bass.ds(P * t, n)], colP[:, 0:n]).then_inc(row_used, 1)

                def rows_out(t):
                    dve.wait_ge(row_used, T + t)
                    nc.vector.tensor_copy(tile_cols[:, :], aggT[:, bass.ds(P * t, P)]).then_inc(cut, 1)
                    dve.wait_ge(row_turned, T + t + 1)
                    if not (isinstance(t, int) and t == 0):
                        dve.wait_ge(row_out, 16 * t)
                    nc.vector.tensor_copy(row[:, :], colP[:, 0:P]).then_inc(row_used, 1)
                nc.vector.memset(aggT[:, :], NEG_INIT).then_inc(edge_done, 1)
                with dve.Fori(0, T) as t:
                    out_of_psum(t, P)
                dve.wait_ge(row_used, T)
                with dve.Fori(0, pages) as i:
                    dve.wait_ge(page_here, 48 * i + 48)
                    nc.vector.tensor_copy(tile_cols[0:1, 0:1], w["ones_row"][0:1, 0:1])
                    with dve.Fori(0, page // U) as k:
                        s, d = ends_of(nc, pl, ends, U * k, U)
                        for u in range(U):
                            to = aggT[:, bass.ds(d[u], 1)]
                            dve.wait_ge(edge_done, page * i + U * k + u + 1)
                            nc.vector.scalar_tensor_tensor(out=to, in0=h1T[:, bass.ds(s[u], 1)],
                                                           scalar=wpage[:, bass.ds(U * k + u, 1)], in1=to,
                                                           op0=ALU.mult, op1=ALU.max).then_inc(edge_done, 1)
                dve.wait_ge(edge_done, pl.E + 1)
                rows_out(0)
                with dve.Fori(1, T) as t:
                    rows_out(t)
                dve.wait_ge(named, 1)


def ends_of(nc, pl, ends, k, n):
    return [nc.values_load_multi_w_load_instructions(
        ends[0:1, e, bass.ds(k, n)], engines=[mybir.EngineType.DVE], min_val=0, max_val=pl.N - 1,
        skip_runtime_bounds_check_because="the reference takes nodes below N")[1] for e in range(2)]


def layers(nc, pl, w, sems, counts, xT, weight, x1_dram, h2_dram, out, tag="", one_by_one=None):
    T, last, S, W, G = pl.tiles, pl.last, pl.steps, pl.width, pl.groups
    with ExitStack() as ctx:
        def sb(name, shape, dt):
            return ctx.enter_context(nc.sbuf_tensor(tag + name, shape, dt))

        def sem(name):
            return kept_semaphore(nc, sems, name)

        def ps(name):
            return ctx.enter_context(nc.psum_tensor(tag + name, [P, 512], F32))

        parts = sb("parts", [P, T, 3, P], BF16)
        rest = sb("rest", [P, 2, 4, P], F32)
        lw = w["lw"]
        agg = sb("agg", [P, 2, W], F32)
        rg = sb("rg", [P, W], F32)
        zg = sb("zg", [P, W], F32)
        ng = sb("ng", [P, W], F32)
        hn = sb("hn", [P, W], F32)

        mP = [ps(f"mP{i}") for i in range(2)]
        aP = [ps(f"aP{i}") for i in range(2)]
        rP, zP, iP, nP = ps("rP"), ps("zP"), ps("iP"), ps("nP")

        lw_in = sem("lw_in")
        m_ready = sem("m_ready")
        m_hi = sem("m_hi")
        m_rest = sem("m_rest")
        m_mid = sem("m_mid")
        m_lo = sem("m_lo")
        a_ready = sem("a_ready")
        a_out = sem("a_out")
        g_ready = sem("g_ready")
        r_done = sem("r_done")
        z_done = sem("z_done")
        hn_r = sem("hn_r")
        hn_i = sem("hn_i")
        n_done = sem("n_done")
        diff = sem("diff")
        prod = sem("prod")
        x_new = sem("x_new")

        if one_by_one:
            src, dst, _ = one_by_one
            mT, sumT = as_columns(pl, counts, 0), as_columns(pl, counts, 1)
            pages, page, U = edge_pages(pl)
            ends = as_columns(pl, counts, 2)[0:1, 0:2 * page].bitcast(I32).rearrange("p (e k) -> p e k", e=2)
            page_here = sem("page_here")
            m_out = sem("m_out")
            lw_cut = sem("lw_cut")
            lw_now = as_columns(pl, counts, 3)[:, 0:P]
            spare = as_columns(pl, counts, 3)[0:1, P:P + 1]
            edge_done = sem("sum_edge_done")

        def tiles(g):
            return range(4 * g, min(4 * g + 4, T))

        def chunk_of(g):
            return min(S, -(-P * (tiles(g)[-1] + 1) // W))

        def m_group_pe(pe, l, g):
            if g > 1:
                pe.wait_ge(m_rest, G * l + g - 1)
            elif g == 0 and not (isinstance(l, int) and l == 0):
                pe.wait_ge(m_rest, G * l)
            pe.wait_ge(x_new, S * l + chunk_of(g))
            for t in tiles(g):
                rhs = lw[:, l, :] if isinstance(l, int) else \
                    lw[:, bass.ds(l, 1), :].rearrange("p a f -> p (a f)")
                mm = nc.tensor.matmul(mP[g % 2][:, (t - 4 * g) * P:(t - 4 * g + 1) * P],
                                      xT[:, t * P:(t + 1) * P], rhs, start=True, stop=True)
            mm.then_inc(m_ready, 1)

        def m_psum(g):
            return mP[g % 2][:, 0:len(tiles(g)) * P].rearrange("p (t f) -> p t f", f=P)

        def part(g, k):
            return parts[:, 4 * g:4 * g + len(tiles(g)), k, :]

        def high_act(act, l, g):
            act.wait_ge(m_ready, G * l + g + 1)
            nc.scalar.copy(part(g, 0), m_psum(g)).then_inc(m_hi, 1)

        def rest_dve(dve, l, g):
            dve.wait_ge(m_hi, G * l + g + 1)
            if not (isinstance(l, int) and l == 0 and g < 2):
                dve.wait_ge(m_lo, G * l + max(g - 1, 0))
            nc.vector.tensor_tensor(rest[:, g % 2, 0:len(tiles(g)), :], m_psum(g), part(g, 0), ALU.subtract
                                    ).then_inc(m_rest, 1)

        def middle_act(act, l, g):
            act.wait_ge(m_rest, G * l + g + 1)
            nc.scalar.copy(part(g, 1), rest[:, g % 2, 0:len(tiles(g)), :]).then_inc(m_mid, 1)

        def low_dve(dve, l, g):
            dve.wait_ge(m_mid, G * l + g + 1)
            nc.vector.tensor_tensor(part(g, 2), rest[:, g % 2, 0:len(tiles(g)), :], part(g, 1), ALU.subtract
                                    ).then_inc(m_lo, 1)

        def m_groups_act(act, l, groups):
            for g in groups:
                high_act(act, l, g)
                if g > groups[0]:
                    middle_act(act, l, g - 1)
            middle_act(act, l, groups[-1])

        def m_groups_dve(dve, l, groups):
            for g in groups:
                rest_dve(dve, l, g)
                if g > groups[0]:
                    low_dve(dve, l, g - 1)
            low_dve(dve, l, groups[-1])

        def m_groups_pe(pe, l, groups):
            for g in groups:
                m_group_pe(pe, l, g)

        def agg_pe(pe, l, c, tiles_=range(T)):
            if c > 1:
                pe.wait_ge(a_out, S * l + c - 1)
            for t in tiles_:
                if c == 0 and t % 4 == 0:
                    pe.wait_ge(m_lo, G * l + t // 4 + 1)
                for k in range(3):
                    mm = nc.tensor.matmul(aP[c % 2][:, 0:W], parts[:, t, k, :], counts[:, t, c * W:(c + 1) * W],
                                          start=(t == 0 and k == 0), stop=(t == T - 1 and k == 2))
            if tiles_[-1] == T - 1:
                mm.then_inc(a_ready, 1)

        def gate_pe(pe, l, c):
            a = agg[:, c % 2, :]
            h = xT[:, c * W:(c + 1) * W]
            pe.wait_ge(a_out, S * l + c + 1)
            if c:
                pe.wait_ge(z_done, S * l + c)
                pe.wait_ge(hn_i, S * l + c)
            nc.tensor.matmul(rP[:, 0:W], w["wihT"][:, 0, :], a, start=True, stop=False)
            nc.tensor.matmul(rP[:, 0:W], w["whhT"][:, 0, :], h, start=False, stop=True)
            nc.tensor.matmul(nP[:, 0:W], w["whhT"][:, 2, :], h, start=True, stop=True)
            nc.tensor.matmul(iP[:, 0:W], w["wihT"][:, 2, :], a, start=True, stop=True)
            nc.tensor.matmul(zP[:, 0:W], w["wihT"][:, 1, :], a, start=True, stop=False)
            nc.tensor.matmul(zP[:, 0:W], w["whhT"][:, 1, :], h, start=False, stop=True).then_inc(g_ready, 1)

        def agg_act(act, l, c):
            if one_by_one:
                act.wait_ge(edge_done, (pl.E + 1) * (l + 1))
                if c >= 2:
                    act.wait_ge(g_ready, S * l + c - 1)
                nc.scalar.copy(agg[:, c % 2, :], sumT[:, c * W:(c + 1) * W]).then_inc(a_out, 1)
                return
            act.wait_ge(a_ready, S * l + c + 1)
            nc.scalar.copy(agg[:, c % 2, :], aP[c % 2][:, 0:W]).then_inc(a_out, 1)

        def gate_act(act, l, c):
            act.wait_ge(g_ready, S * l + c + 1)
            act.wait_ge(x_new, S * (l + 1) + c)
            nc.scalar.activation(rg[:, :], rP[:, 0:W], ACT.Sigmoid, bias=w["bsum"][:, 0:1]).then_inc(r_done, 1)
            nc.scalar.activation(zg[:, :], zP[:, 0:W], ACT.Sigmoid, bias=w["bsum"][:, 1:2]).then_inc(z_done, 1)
            act.wait_ge(hn_i, S * l + c + 1)
            nc.scalar.activation(ng[:, :], hn[:, :], ACT.Tanh, bias=w["bihc"][:, 2:3]).then_inc(n_done, 1)

        def gate_dve(dve, l, c):
            h = xT[:, c * W:(c + 1) * W]
            dve.wait_ge(r_done, S * l + c + 1)
            dve.wait_ge(g_ready, S * l + c + 1)
            nc.vector.scalar_tensor_tensor(out=hn[:, :], in0=nP[:, 0:W], scalar=w["bhhc"][:, 2:3], in1=rg[:, :],
                                           op0=ALU.add, op1=ALU.mult).then_inc(hn_r, 1)
            dve.wait_ge(hn_r, S * l + c + 1)
            nc.vector.tensor_tensor(hn[:, :], iP[:, 0:W], hn[:, :], ALU.add).then_inc(hn_i, 1)
            dve.wait_ge(n_done, S * l + c + 1)
            nc.vector.tensor_tensor(rg[:, :], h, ng[:, :], ALU.subtract).then_inc(diff, 1)
            dve.wait_ge(diff, S * l + c + 1)
            nc.vector.tensor_tensor(rg[:, :], rg[:, :], zg[:, :], ALU.mult).then_inc(prod, 1)
            dve.wait_ge(prod, S * l + c + 1)
            nc.vector.tensor_tensor(h, rg[:, :], ng[:, :], ALU.add).then_inc(x_new, 1)

        def messages_pe(pe, l):
            pe.wait_ge(x_new, S * l + S)
            pe.wait_ge(lw_cut, l + 1)
            for c in range(S):
                if c:
                    pe.wait_ge(m_out, S * l + c)
                nc.tensor.matmul(mP[0][:, 0:W], lw_now[:, :],
                                 xT[:, c * W:(c + 1) * W], start=True, stop=True).then_inc(m_ready, 1)

        def messages_act(act, l):
            nc.scalar.copy(lw_now[:, :], lw[:, bass.ds(l, 1), :].rearrange("p a f -> p (a f)")).then_inc(lw_cut, 1)
            for c in range(S):
                act.wait_ge(m_ready, S * l + c + 1)
                nc.scalar.copy(mT[:, c * W:(c + 1) * W], mP[0][:, 0:W]).then_inc(m_out, 1)

        def pages_act(act, l):
            with act.Fori(0, pages) as i:
                act.wait_ge(edge_done, (pl.E + 1) * l + page * i + 1)
                page_in(act, pl, ends[:, 0, :], src, page * i).then_inc(page_here, 16)
                page_in(act, pl, ends[:, 1, :], dst, page * i).then_inc(page_here, 16)

        def sums_dve(dve, l):
            dve.wait_ge(m_out, S * l + S)
            nc.vector.memset(sumT[:, :], 0.0).then_inc(edge_done, 1)
            with dve.Fori(0, pages) as i:
                dve.wait_ge(page_here, 32 * (pages * l + i) + 32)
                nc.vector.tensor_copy(spare, w["ones_row"][0:1, 0:1])
                with dve.Fori(0, page // U) as k:
                    s, d = ends_of(nc, pl, ends, U * k, U)
                    for u in range(U):
                        to = sumT[:, bass.ds(d[u], 1)]
                        dve.wait_ge(edge_done, (pl.E + 1) * l + page * i + U * k + u + 1)
                        nc.vector.tensor_tensor(to, to, mT[:, bass.ds(s[u], 1)], ALU.add).then_inc(edge_done, 1)

        def general_pe(pe):
            with pe.Fori(0, pl.L) as l:
                messages_pe(pe, l)
                for c in range(S):
                    gate_pe(pe, l, c)
            output_pe(pe, range(G))

        def general_act(act):
            act.wait_ge(lw_in, 16)
            with act.Fori(0, pl.L) as l:
                messages_act(act, l)
                pages_act(act, l)
                agg_act(act, l, 0)
                for c in range(1, S):
                    agg_act(act, l, c)
                    gate_act(act, l, c - 1)
                gate_act(act, l, S - 1)

        def general_dve(dve):
            with dve.Fori(0, pl.L) as l:
                sums_dve(dve, l)
                for c in range(S):
                    gate_dve(dve, l, c)
            output_dve(dve, range(G))

        early = G - 2
        assert chunk_of(early - 1) < S and chunk_of(early - 2) < S - 1
        half = 4 * (early - 1)

        def layer(engine, l, more, sums, cell, messages, output=None):
            if sums is agg_pe:
                agg_pe(engine, l, 0, range(half))
            messages(engine, l, range(early, G))
            if sums is agg_pe:
                agg_pe(engine, l, 0, range(half, T))
            elif sums:
                sums(engine, l, 0)
            for c in range(1, S):
                if sums:
                    sums(engine, l, c)
                if c < S - 1:
                    cell(engine, l, c - 1)
            if more:
                messages(engine, l + 1, range(0, 2))
            cell(engine, l, S - 2)
            if more:
                messages(engine, l + 1, range(2, early - 1))
            elif output:
                output(engine, range(0, 2))
            cell(engine, l, S - 1)
            if more:
                messages(engine, l + 1, range(early - 1, early))
            elif output:
                output(engine, range(2, G))

        def layers_of(engine, sums, cell, messages, output):
            messages(engine, 0, range(early))
            with engine.Fori(0, pl.L - 1) as l:
                layer(engine, l, True, sums, cell, messages)
            layer(engine, pl.L - 1, False, sums, cell, messages, output)

        full = pl.N // P
        rx = as_columns(pl, counts, 4).rearrange("p (t f) -> p t f", f=P)
        r1 = as_columns(pl, counts, 5).rearrange("p (t f) -> p t f", f=P)
        h2_in = sem("h2_in")
        x1_in = sem("x1_in")
        turned = sem("x_turned")
        with_h2 = sem("with_h2")
        summed = sem("summed")
        summed_late = sem("summed_late")
        pooled = G - 2
        stored = sem("stored")

        def spans(g):
            a, b = 4 * g, min(4 * g + 4, T)
            found = [(P, a, min(b, full) - a)] if min(b, full) > a else []
            return found + ([(last, full, 1)] if b > full else [])

        def output_sp(sp):
            if not one_by_one:
                sp.wait_ge(a_ready, S * pl.L)
            for rows_, dram, s in ((rx, h2_dram, h2_in), (r1, x1_dram, x1_in)):
                sp.dma_start(rows_[:, 0:full, :], dram[0:P * full, :].rearrange("(t p) f -> p t f", p=P)).then_inc(s, 16)
                sp.dma_start(rows_[0:last, full, :], dram[P * full:pl.N, :]).then_inc(s, 16)
            n_out = 0
            for g in range(G):
                sp.wait_ge(*((summed, g + 1) if g < pooled else (summed_late, g + 1 - pooled)))
                for n, a, k in spans(g):
                    d = out[P * a:P * a + n * k, :].rearrange("(t p) f -> p t f", p=n)
                    sp.dma_start(d, rx[0:n, a:a + k, :]).then_inc(stored, 16)
                    n_out += 16
            sp.wait_ge(stored, n_out)

        def output_pe(pe, groups):
            for g in groups:
                pe.wait_ge(x_new, S * pl.L + chunk_of(g))
                if g >= 2:
                    pe.wait_ge(with_h2, g - 1)
                for t in tiles(g):
                    mm = nc.tensor.transpose(mP[g % 2][:, (t - 4 * g) * P:(t - 4 * g + 1) * P],
                                             xT[:, t * P:(t + 1) * P], w["ident"][:, :])
                mm.then_inc(turned, 1)

        def output_dve(dve, groups):
            dve.wait_ge(h2_in, 32)
            for g in groups:
                dve.wait_ge(turned, g + 1)
                for n, a, k in spans(g):
                    j = (a - 4 * g) * P
                    ins = nc.vector.tensor_tensor(rx[0:n, a:a + k, :], mP[g % 2][0:n, j:j + k * P].rearrange(
                        "p (t f) -> p t f", f=P), rx[0:n, a:a + k, :], ALU.add)
                ins.then_inc(with_h2, 1)
                if g >= pooled:
                    dve.wait_ge(x1_in, 32)
                    dve.wait_ge(with_h2, g + 1)
                    add_x1(nc.vector, g).then_inc(summed_late, 1)

        def add_x1(engine, g):
            for n, a, k in spans(g):
                ins = engine.tensor_tensor(rx[0:n, a:a + k, :], rx[0:n, a:a + k, :], r1[0:n, a:a + k, :], ALU.add)
            return ins

        def output_pool(pool):
            pool.wait_ge(x1_in, 32)
            for g in range(pooled):
                pool.wait_ge(with_h2, g + 1)
                add_x1(nc.gpsimd, g).then_inc(summed, 1)

        with nc.Block() as block:
            @block.sync
            def _(sp):
                output_sp(sp)

            @block.gpsimd
            def _(pool):
                output_pool(pool)

            @block.tensor
            def _(pe):
                if one_by_one:
                    general_pe(pe)
                else:
                    pe.wait_ge(lw_in, 16)
                    layers_of(pe, agg_pe, gate_pe, m_groups_pe, output_pe)

            @block.scalar
            def _(act):
                if one_by_one:
                    general_act(act)
                else:
                    layers_of(act, agg_act, gate_act, m_groups_act, None)

            @block.vector
            def _(dve):
                dve.sem_inc(x_new, S)
                if one_by_one:
                    general_dve(dve)
                else:
                    layers_of(dve, None, gate_dve, m_groups_dve, output_dve)


_INS = ['x', 'src', 'dst', 'edge_weight', 'L0_gnn_w1', 'L0_gnn_b1', 'L0_gnn_w2', 'L0_gnn_b2', 'L0_gnn_eps',
        'L1_gnn_weight', 'L1_gnn_w_ih', 'L1_gnn_w_hh', 'L1_gnn_b_ih', 'L1_gnn_b_hh']


def kernel(**inputs):
    import numpy as _np
    import concourse.bacc as _bacc
    from concourse import mybir as _mybir
    from concourse.bass_utils import run_bass_kernel_spmd as _run

    nc = _bacc.Bacc("TRN2", target_bir_lowering=False, num_devices=1)
    arrays, args = {}, []
    for name in _INS:
        a = _np.ascontiguousarray(inputs[name])
        arrays[f"in_{name}_dram"] = a
        args.append(nc.dram_tensor(f"in_{name}_dram", a.shape, _mybir.dt.from_np(a.dtype), kind="ExternalInput").ap())
    shape = tuple(inputs['x'].shape)
    args.append(nc.dram_tensor("out_0_dram", shape, _mybir.dt.float32, kind="ExternalOutput").ap())
    gnn_kernel(nc, *args)
    r = _run(nc, [arrays], core_ids=[0])
    return r.results[0]["out_0_dram"]
```
